# Optimizing a Trainium2 kernel written in Bass

```python
import numpy as np
import jax
import jax.numpy as jnp

def _softmax(x, axis=-1):
    return jax.nn.softmax(x, axis=axis)

def _gelu(x):
    return jax.nn.gelu(x, approximate=True)

def _silu(x):
    return jax.nn.silu(x)

def _sigmoid(x):
    return jax.nn.sigmoid(x)

def _layernorm(x, axis=-1, eps=1e-05):
    m = jnp.mean(x, axis=axis, keepdims=True)
    v = jnp.var(x, axis=axis, keepdims=True)
    return (x - m) / jnp.sqrt(v + eps)

def _scatter_add(tgt, idx, src, axis=0):
    return tgt.at[idx].add(src)

def _segment_sum(src, seg, n):
    return jax.ops.segment_sum(src, seg, n)
kernel_name = 'mk_gps_d1_gnn_r8_e2eb9b'

def setup_inputs(seed: int=0):
    np.random.seed(seed)
    _w = jnp.asarray

    def _rec_inputs():
        import jax
        import jax.numpy as jnp
        _gk = jax.random.key(seed)
        x = -0.0003713 + 1 * jax.random.normal(jax.random.fold_in(_gk, 1), (6250, 256), jnp.float32)
        _s = jax.random.randint(jax.random.fold_in(_gk, 2), (50000,), 0, 6250, jnp.int32)
        _d = jax.random.randint(jax.random.fold_in(_gk, 3), (50000,), 0, 6250, jnp.int32)
        _loop = jnp.arange(6250, dtype=jnp.int32)
        src = jnp.concatenate([_s, _d, _loop])
        dst = jnp.concatenate([_d, _s, _loop])
        _o = jnp.argsort(dst, stable=True)
        src = src[_o]
        dst = dst[_o]
        edge_attr_64 = 0.000189758 + 1.00013 * jax.random.normal(jax.random.fold_in(_gk, 12), (106250, 64), jnp.float32)
        return (x, src, dst, edge_attr_64)
    x, src, dst, edge_attr_64 = _rec_inputs()

    def _L0_gnn_setup():
        import jax, jax.numpy as jnp
        import numpy as np
        N_NODES = 6250
        N_EDGES = 100000
        NODE_IN = 256
        EDGE_OUT = 64
        GLOBAL_IN = 128
        NODE_OUT = 256
        HIDDEN = 512
        N_GRAPHS = 64
        key = jax.random.key(seed)
        ks = jax.random.split(key, 8)
        x = jax.random.normal(ks[0], (N_NODES, NODE_IN), dtype=jnp.float32)
        edge_index = jax.random.randint(ks[1], (2, N_EDGES), 0, N_NODES, dtype=jnp.int64)
        edge_attr = jax.random.normal(ks[2], (N_EDGES, EDGE_OUT), dtype=jnp.float32)
        u = jax.random.normal(ks[3], (N_GRAPHS, GLOBAL_IN), dtype=jnp.float32)
        batch = jnp.sort(jax.random.randint(ks[4], (N_NODES,), 0, N_GRAPHS, dtype=jnp.int64))
        in_dim = NODE_IN + EDGE_OUT + GLOBAL_IN
        b1s = 1.0 / np.sqrt(in_dim)
        b2s = 1.0 / np.sqrt(HIDDEN)
        W1 = jax.random.uniform(ks[5], (in_dim, HIDDEN), dtype=jnp.float32, minval=-b1s, maxval=b1s)
        b1 = jnp.zeros((HIDDEN,), dtype=jnp.float32)
        W2 = jax.random.uniform(ks[6], (HIDDEN, NODE_OUT), dtype=jnp.float32, minval=-b2s, maxval=b2s)
        b2 = jnp.zeros((NODE_OUT,), dtype=jnp.float32)
        return {'x': x, 'edge_index': edge_index, 'edge_attr': edge_attr, 'u': u, 'batch': batch, 'W1': W1, 'b1': b1, 'W2': W2, 'b2': b2}
    _L0_gnn_all = _L0_gnn_setup()
    _L0_gnn_in = {k: v for k, v in _L0_gnn_all.items() if k in ('u', 'W1', 'b1', 'W2', 'b2')}
    del _L0_gnn_all

    def _L0_mix_setup():
        import jax, jax.numpy as jnp
        import numpy as np
        EMB, HEADS, DEPTH, SEQ, BATCH = (256, 8, 4, 1024, 4)
        DH = EMB // HEADS
        FF = 4 * EMB
        EPS = 1e-05

        def _layernorm(x, g, b):
            mu = x.mean(-1, keepdims=True)
            var = ((x - mu) ** 2).mean(-1, keepdims=True)
            return (x - mu) * jax.lax.rsqrt(var + EPS) * g + b

        def _linear_attn(x, Wq, Wk, Wv, Wo, bo):
            b, n, dm = x.shape
            split = lambda t: t.reshape(b, n, HEADS, DH).transpose(0, 2, 1, 3)
            scale = DH ** (-0.25)
            q = jax.nn.softmax(split(x @ Wq) * scale, axis=-1)
            k = jax.nn.softmax(split(x @ Wk) * scale, axis=-2)
            v = split(x @ Wv)
            context = jnp.einsum('bhnd,bhne->bhde', k, v)
            out = jnp.einsum('bhnd,bhde->bhne', q, context)
            out = out.transpose(0, 2, 1, 3).reshape(b, n, dm)
            return out @ Wo + bo

        def _forward(x, Wq, Wk, Wv, Wo, bo, ln1_g, ln1_b, W1, b1, W2, b2, ln2_g, ln2_b):
            for i in range(DEPTH):
                h = _layernorm(x, ln1_g[i], ln1_b[i])
                x = x + _linear_attn(h, Wq[i], Wk[i], Wv[i], Wo[i], bo[i])
                h = _layernorm(x, ln2_g[i], ln2_b[i])
                x = x + (jax.nn.gelu(h @ W1[i] + b1[i], approximate=False) @ W2[i] + b2[i])
            return x
        key = jax.random.key(seed)
        ks = jax.random.split(key, 8)
        w = lambda k, shape: jax.random.normal(k, shape, dtype=jnp.float32) * 0.02
        D = DEPTH
        return {'x': jax.random.normal(ks[0], (BATCH, SEQ, EMB), dtype=jnp.float32), 'Wq': w(ks[1], (D, EMB, EMB)), 'Wk': w(ks[2], (D, EMB, EMB)), 'Wv': w(ks[3], (D, EMB, EMB)), 'Wo': w(ks[4], (D, EMB, EMB)), 'bo': jnp.zeros((D, EMB), jnp.float32), 'ln1_g': jnp.ones((D, EMB), jnp.float32), 'ln1_b': jnp.zeros((D, EMB), jnp.float32), 'W1': w(ks[5], (D, EMB, FF)), 'b1': jnp.zeros((D, FF), jnp.float32), 'W2': w(ks[6], (D, FF, EMB)), 'b2': jnp.zeros((D, EMB), jnp.float32), 'ln2_g': jnp.ones((D, EMB), jnp.float32), 'ln2_b': jnp.zeros((D, EMB), jnp.float32)}
    _L0_mix_all = _L0_mix_setup()
    _L0_mix_in = {k: v for k, v in _L0_mix_all.items() if k in ('Wq', 'Wk', 'Wv', 'Wo', 'bo', 'ln1_g', 'ln1_b', 'W1', 'b1', 'W2', 'b2', 'ln2_g', 'ln2_b')}
    del _L0_mix_all

    def _L0_ffn_setup():
        import jax, jax.numpy as jnp
        import numpy as np
        B, K, D = (512, 16, 256)
        E = 32
        H = int(D * 0.25)
        key = jax.random.key(seed)
        ks = jax.random.split(key, 7)
        d_rs = D ** (-0.5)
        h_rs = H ** (-0.5)
        x = jax.random.normal(ks[0], (B, K, D), dtype=jnp.float32)
        router_w = jax.random.uniform(ks[1], (E, D), jnp.float32, -d_rs, d_rs)
        router_b = jax.random.uniform(ks[2], (E,), jnp.float32, -d_rs, d_rs)
        W1 = jax.random.uniform(ks[3], (E, D, H), jnp.float32, -h_rs, h_rs)
        b1 = jax.random.uniform(ks[4], (E, H), jnp.float32, -h_rs, h_rs)
        W2 = jax.random.uniform(ks[5], (E, H, D), jnp.float32, -d_rs, d_rs)
        b2 = jax.random.uniform(ks[6], (E, D), jnp.float32, -d_rs, d_rs)
        return {'x': x, 'router_w': router_w, 'router_b': router_b, 'W1': W1, 'b1': b1, 'W2': W2, 'b2': b2}
    _L0_ffn_all = _L0_ffn_setup()
    _L0_ffn_in = {k: v for k, v in _L0_ffn_all.items() if k in ('router_w', 'router_b', 'W1', 'b1', 'W2', 'b2')}
    del _L0_ffn_all
    return {'x': x, 'src': src, 'dst': dst, 'edge_attr_64': edge_attr_64, 'L0_gnn_u': _L0_gnn_in['u'], 'L0_gnn_W1': _L0_gnn_in['W1'], 'L0_gnn_b1': _L0_gnn_in['b1'], 'L0_gnn_W2': _L0_gnn_in['W2'], 'L0_gnn_b2': _L0_gnn_in['b2'], 'L0_mix_Wq': _L0_mix_in['Wq'], 'L0_mix_Wk': _L0_mix_in['Wk'], 'L0_mix_Wv': _L0_mix_in['Wv'], 'L0_mix_Wo': _L0_mix_in['Wo'], 'L0_mix_bo': _L0_mix_in['bo'], 'L0_mix_ln1_g': _L0_mix_in['ln1_g'], 'L0_mix_ln1_b': _L0_mix_in['ln1_b'], 'L0_mix_W1': _L0_mix_in['W1'], 'L0_mix_b1': _L0_mix_in['b1'], 'L0_mix_W2': _L0_mix_in['W2'], 'L0_mix_b2': _L0_mix_in['b2'], 'L0_mix_ln2_g': _L0_mix_in['ln2_g'], 'L0_mix_ln2_b': _L0_mix_in['ln2_b'], 'L0_ffn_router_w': _L0_ffn_in['router_w'], 'L0_ffn_router_b': _L0_ffn_in['router_b'], 'L0_ffn_W1': _L0_ffn_in['W1'], 'L0_ffn_b1': _L0_ffn_in['b1'], 'L0_ffn_W2': _L0_ffn_in['W2'], 'L0_ffn_b2': _L0_ffn_in['b2']}

def reference(x, src, dst, edge_attr_64, L0_gnn_u, L0_gnn_W1, L0_gnn_b1, L0_gnn_W2, L0_gnn_b2, L0_mix_Wq, L0_mix_Wk, L0_mix_Wv, L0_mix_Wo, L0_mix_bo, L0_mix_ln1_g, L0_mix_ln1_b, L0_mix_W1, L0_mix_b1, L0_mix_W2, L0_mix_b2, L0_mix_ln2_g, L0_mix_ln2_b, L0_ffn_router_w, L0_ffn_router_b, L0_ffn_W1, L0_ffn_b1, L0_ffn_W2, L0_ffn_b2):
    import jax
    import jax.numpy as jnp

    def _L0_gnn_ref(x, edge_index, edge_attr, u, batch, W1, b1, W2, b2):
        import jax, jax.numpy as jnp
        import numpy as np
        N_NODES = 6250
        N_EDGES = 100000
        NODE_IN = 256
        EDGE_OUT = 64
        GLOBAL_IN = 128
        NODE_OUT = 256
        HIDDEN = 512
        N_GRAPHS = 64
        n = x.shape[0]
        src = edge_index[0]
        sums = jax.ops.segment_sum(edge_attr, src, num_segments=n)
        counts = jax.ops.segment_sum(jnp.ones((edge_attr.shape[0],), edge_attr.dtype), src, num_segments=n)
        edge_attr_agg = sums / jnp.maximum(counts, 1.0)[:, None]
        u_expanded = u[batch]
        combined = jnp.concatenate([x, edge_attr_agg, u_expanded], axis=1)
        h = jax.nn.relu(combined @ W1 + b1)
        return h @ W2 + b2

    def _L0_mix_ref(x, Wq, Wk, Wv, Wo, bo, ln1_g, ln1_b, W1, b1, W2, b2, ln2_g, ln2_b):
        import jax, jax.numpy as jnp
        import numpy as np
        EMB, HEADS, DEPTH, SEQ, BATCH = (256, 8, 4, 1024, 4)
        DH = EMB // HEADS
        FF = 4 * EMB
        EPS = 1e-05

        def _layernorm(x, g, b):
            mu = x.mean(-1, keepdims=True)
            var = ((x - mu) ** 2).mean(-1, keepdims=True)
            return (x - mu) * jax.lax.rsqrt(var + EPS) * g + b

        def _linear_attn(x, Wq, Wk, Wv, Wo, bo):
            b, n, dm = x.shape
            split = lambda t: t.reshape(b, n, HEADS, DH).transpose(0, 2, 1, 3)
            scale = DH ** (-0.25)
            q = jax.nn.softmax(split(x @ Wq) * scale, axis=-1)
            k = jax.nn.softmax(split(x @ Wk) * scale, axis=-2)
            v = split(x @ Wv)
            context = jnp.einsum('bhnd,bhne->bhde', k, v)
            out = jnp.einsum('bhnd,bhde->bhne', q, context)
            out = out.transpose(0, 2, 1, 3).reshape(b, n, dm)
            return out @ Wo + bo

        def _forward(x, Wq, Wk, Wv, Wo, bo, ln1_g, ln1_b, W1, b1, W2, b2, ln2_g, ln2_b):
            for i in range(DEPTH):
                h = _layernorm(x, ln1_g[i], ln1_b[i])
                x = x + _linear_attn(h, Wq[i], Wk[i], Wv[i], Wo[i], bo[i])
                h = _layernorm(x, ln2_g[i], ln2_b[i])
                x = x + (jax.nn.gelu(h @ W1[i] + b1[i], approximate=False) @ W2[i] + b2[i])
            return x
        return _forward(x, Wq, Wk, Wv, Wo, bo, ln1_g, ln1_b, W1, b1, W2, b2, ln2_g, ln2_b)

    def _L0_ffn_ref(x, router_w, router_b, W1, b1, W2, b2):
        import jax, jax.numpy as jnp
        import numpy as np
        B, K, D = (512, 16, 256)
        E = 32
        H = int(D * 0.25)
        xf = x.reshape(-1, D)
        logits = xf @ router_w.T + router_b
        idx = jnp.argmax(logits, axis=-1)
        w1t = jnp.take(W1, idx, axis=0)
        h = jnp.einsum('nd,ndh->nh', xf, w1t) + jnp.take(b1, idx, axis=0)
        h = jax.nn.relu(h)
        w2t = jnp.take(W2, idx, axis=0)
        out = jnp.einsum('nh,nhd->nd', h, w2t) + jnp.take(b2, idx, axis=0)
        out = jax.nn.relu(out)
        return out.reshape(x.shape)
    edge_index = jnp.stack([src, dst])
    batch0 = jnp.zeros((6250,), jnp.int32)
    xn = _layernorm(x, axis=-1)
    x = x + _L0_gnn_ref(xn, edge_index, edge_attr_64, L0_gnn_u, batch0, L0_gnn_W1, L0_gnn_b1, L0_gnn_W2, L0_gnn_b2) + _L0_mix_ref(xn[None], L0_mix_Wq, L0_mix_Wk, L0_mix_Wv, L0_mix_Wo, L0_mix_bo, L0_mix_ln1_g, L0_mix_ln1_b, L0_mix_W1, L0_mix_b1, L0_mix_W2, L0_mix_b2, L0_mix_ln2_g, L0_mix_ln2_b)[0]
    x = x + _L0_ffn_ref(_layernorm(x, axis=-1)[None], L0_ffn_router_w, L0_ffn_router_b, L0_ffn_W1, L0_ffn_b1, L0_ffn_W2, L0_ffn_b2)[0]
    return x

_drawn_inputs = setup_inputs


def setup_inputs(seed=0):
    import zlib

    import numpy as np

    out = dict(_drawn_inputs(seed))
    spreads = {'L0_gnn_b1': (0.0, 0.309),
     'L0_gnn_b2': (0.0, 0.1),
     'L0_mix_bo': (0.0, 0.1),
     'L0_mix_ln1_g': (1.0, 0.6),
     'L0_mix_ln1_b': (0.0, 0.529),
     'L0_mix_b1': (0.0, 0.1),
     'L0_mix_b2': (0.0, 0.1),
     'L0_mix_ln2_g': (1.0, 0.582),
     'L0_mix_ln2_b': (0.0, 0.457)}
    factors = {'edge_attr_64': 3.968,
     'L0_mix_Wq': 31.351,
     'L0_mix_Wk': 31.097,
     'L0_ffn_b1': 8.0,
     'L0_ffn_b2': 4.688}
    for name, (base, spread) in spreads.items():
        noise = np.random.default_rng([zlib.crc32(name.encode()), seed]).standard_normal(out[name].shape)
        drawn = base * np.exp(spread * noise) if base else spread * noise
        out[name] = jnp.asarray(drawn.astype(out[name].dtype))
    for name, factor in factors.items():
        out[name] = (out[name] * factor).astype(out[name].dtype)
    return out
```

```python
from contextlib import ExitStack

import concourse.bass as bass
from concourse import mybir

F32 = mybir.dt.float32
F32R = mybir.dt.float32r
I32 = mybir.dt.int32
U32 = mybir.dt.uint32
ALU = mybir.AluOpType
ACT = mybir.ActivationFunctionType
AX = mybir.AxisListType.X

P = 125
TILES = 50
D = 256
KC = D // 128
PAIR = 2
GROUPS = TILES // PAIR
GT = PAIR * P
N = P * TILES
LAYERS = 4
HEADS = 8
DH = D // HEADS
FF = 4 * D
FC = FF // 128
EA = 64
EDGES = 106250
ECOL = EDGES // P
ROW = EA + 1
SEG = 512
SEGR = SEG // 128
ETILES = -(-EDGES // SEG)
ESEGS = ETILES + TILES - 1
CH = 17
CHUNKS = ECOL // CH
GH = 512
GHC = GH // 128
GLOB = 128
EXP = 32
EH = 64
YROW = D + 4
FSEGS = TILES + EXP - 1
EPS = 1e-5
RND = 8388608.0
ROWS_LN = LAYERS * KC
NROW = 4 * ROWS_LN + LAYERS * FC + GHC + 1
NCONST = 10 + 128 // DH
SCALE = DH ** -0.25
SORT_DVE = 13
SPARE = ETILES * SEG - EDGES
SPARE_P = SPARE // 2


def build(nc, x, src, edge_attr, u, gW1, gb1, gW2, gb2, Wq, Wk, Wv, Wo, bo, ln1_g, ln1_b, mW1, mb1, mW2, mb2,
          ln2_g, ln2_b, rw, rb, fW1, fb1, fW2, fb2, out):
    edges_sorted = nc.dram_tensor("edges_sorted", (ETILES * SEG, ROW), F32, kind="Internal").ap()
    tokens_sorted = nc.dram_tensor("tokens_sorted", (N, YROW), F32, kind="Internal").ap()
    x_rows = x.rearrange("(p t) d -> p t d", t=TILES)
    edge_rows = edge_attr.rearrange("(p c) a -> p c a", c=ECOL)

    ctx = ExitStack()
    with ctx:
        def sb(name, shape, dt=F32, where=None):
            return (where or ctx).enter_context(nc.sbuf_tensor(name, shape, dt))

        def both(name, shape, where=None):
            return [sb(f"{name}_{n}", shape, F32R, where) for n in ("hi", "lo")]

        bank = [ctx.enter_context(nc.psum_tensor(f"bank{i}", [128, 512], F32)) for i in range(8)]
        PT, PQ, PQT, PM, PH0, PH1, PY, PS = bank
        PH = [PH0, PH1]

        res = sb("res", [P, TILES, YROW])
        ident = sb("ident", [128, 128])
        ones = sb("ones", [128, 128])
        tri = sb("tri", [128, 128])
        cols = sb("cols", [128, NROW])
        iota_node = sb("iota_node", [128, P])
        iota_seg = sb("iota_seg", [128, ESEGS])
        iota_part = sb("iota_part", [128, 1])
        eps = sb("eps", [128, 1])
        ekind = sb("ekind", [128, ESEGS])
        ekind_i = sb("ekind_i", [1, ESEGS], I32)
        efirst_i = sb("efirst_i", [1, ESEGS], I32)
        segtmp = sb("segtmp", [1, ESEGS])
        bn = sb("bn", [P, PAIR, 6])
        mv = sb("mv", [P, PAIR, 2])
        lnt = sb("lnt", [P, 4, PAIR])
        src_f = sb("src_f", [P, ECOL])
        pos_i = sb("pos_i", [P, ECOL], I32)
        cnt = sb("cnt", [P, TILES])
        tot = sb("tot", [P, TILES])
        totinc = sb("totinc", [P, TILES])
        base = sb("base", [P, TILES])
        kcol = sb("kcol", [TILES, 4])
        cmp = sb("cmp", [TILES, ESEGS])
        stage = sb("stage", [P, 2, CH, ROW])
        idx = sb("idx", [P, 2, CH], I32)

        layers = ExitStack()
        wqk = both("wqk", [128, KC, 2 * D], layers)
        w1 = both("w1", [128, KC, FF], layers)
        w2 = both("w2", [128, FC, D], layers)
        raw_vo = sb("raw_vo", [128, 2, KC, D], F32, layers)
        raw = sb("raw", [128, KC * FF], F32, layers)
        bo_b = sb("bo_b", [P, D], F32, layers)
        b2_b = sb("b2_b", [P, D], F32, layers)
        lcol = sb("lcol", [128, 4 * KC + FC], F32, layers)
        lnst = sb("lnst", [P, TILES, 2], F32, layers)
        xh = [sb(f"xh{i}", [P, PAIR, D], F32, layers) for i in range(2)]
        affine = sb("affine", [128, KC, GT], F32, layers)
        hT = both("hT", [128, KC, GT], layers)
        ek = sb("ek", [P, 2, PAIR, D], F32, layers)
        kmax = sb("kmax", [P, PAIR, D], F32, layers)
        km = sb("km", [P, D], F32, layers)
        mbc = sb("mbc", [P, D], F32, layers)
        esum = sb("esum", [P, PAIR, D], F32, layers)
        mcol = sb("mcol", [128, KC], F32, layers)
        blockmask = sb("blockmask", [128, 128], F32, layers)
        dg = sb("dg", [128, KC, 128], F32, layers)
        k_place = ExitStack()
        ksb = sb("ksb", [P, TILES, D], F32, k_place)
        k_place.close()
        k_place = ExitStack()
        scr = [sb(f"scr{i}", [P, ECOL], F32, k_place) for i in range(3)]
        pos_f = sb("pos_f", [P, ECOL], F32, k_place)
        tile_of = sb("tile_of", [P, ECOL], F32, k_place)
        src_i = sb("src_i", [P, ECOL], I32, k_place)
        ones_e = sb("ones_e", [P, ECOL], F32, k_place)
        colrows = sb("colrows", [NROW, 128], F32, k_place)
        k_place.close()
        k_place = ExitStack()
        gn = sb("gn", [128, KC, D], F32, k_place)
        ct = sb("ct", [128, KC, 128], F32, k_place)
        mmat = both("mmat", [128, KC, D], k_place)
        h2T = both("h2T", [128, KC, GT], k_place)
        qd = sb("qd", [P, PAIR, D], F32, k_place)
        qn = sb("qn", [P, PAIR, D], F32, k_place)
        qstat = sb("qstat", [P, 3, PAIR * HEADS], F32, k_place)
        qT = both("qT", [128, KC, GT], k_place)
        hid = [sb(f"hid{i}", [128, 2, GT], F32, k_place) for i in range(2)]
        hidh = [both(f"hidh{i}", [128, 2, GT], k_place) for i in range(2)]
        k_place.close()
        layers.close()

        gnn = ExitStack()
        agg = sb("agg", [P, TILES, ROW], F32, gnn)
        g1 = both("g1", [128, 3, GH], gnn)
        g2 = both("g2", [128, GHC, D], gnn)
        raw_g1 = sb("raw_g1", [128, 3, GH], F32, gnn)
        raw_g2 = sb("raw_g2", [128, GHC, D], F32, gnn)
        raw_gu = sb("raw_gu", [128, GH], F32, gnn)
        g1col = sb("g1col", [128, GHC], F32, gnn)
        gb2_b = sb("gb2_b", [P, D], F32, gnn)
        rows_in = [sb(f"rows_in{i}", [128, SEGR, ROW], F32, gnn) for i in range(4)]
        kb = sb("kb", [128, 2, SEGR], F32, gnn)
        oh = [sb(f"oh{i}", [128, SEGR, P], F32R, gnn) for i in range(2)]
        ehl = [sb(f"ehl{i}", [128, SEGR, 2 * EA + 2], F32R, gnn) for i in range(2)]
        x_in = sb("x_in", [P, 2, PAIR, D], F32, gnn)
        xn = sb("xn", [P, PAIR, D], F32, gnn)
        an = sb("an", [P, PAIR, EA], F32, gnn)
        crec = sb("crec", [P, 2, PAIR, 1], F32, gnn)
        cT = both("cT", [128, 3, GT], gnn)
        ghid = [sb(f"ghid{i}", [128, 2, GT], F32, gnn) for i in range(2)]
        ghh = [both(f"ghh{i}", [128, 2, GT], gnn) for i in range(2)]
        gst = sb("gst", [P, PAIR, 2], F32, gnn)
        zt = sb("zt", [P, PAIR, D], F32, gnn)
        zT = sb("zT", [128, KC, GT], F32, gnn)
        rwT = sb("rwT", [128, KC, EXP], F32, gnn)
        rw_in = sb("rw_in", [EXP, D], F32, gnn)
        rb_b = sb("rb_b", [P, EXP], F32, gnn)
        logit = sb("logit", [P, PAIR, EXP], F32, gnn)
        best = sb("best", [P, PAIR, 8], F32, gnn)
        besti = sb("besti", [P, PAIR, 8], U32, gnn)
        gnn.close()
        fw1 = sb("fw1", [128, KC, EXP * EH])
        fw2 = sb("fw2", [EH + 1, EXP * D])
        fb1_r = sb("fb1_r", [1, EXP * EH])
        fscr = [sb(f"fscr{i}", [P, TILES]) for i in range(3)]
        fpos = sb("fpos", [P, TILES])
        fpos_i = sb("fpos_i", [P, TILES], I32)
        fexp = sb("fexp", [P, TILES])
        fkind = sb("fkind", [128, FSEGS])
        fkind_i = sb("fkind_i", [1, FSEGS], I32)
        ffirst_i = sb("ffirst_i", [1, FSEGS], I32)
        yin = [sb(f"yin{i}", [P, YROW]) for i in range(3)]
        zs = sb("zs", [P, D])
        zsT = sb("zsT", [128, KC, P])
        hs = sb("hs", [P, EH])
        hsT = sb("hsT", [EH + 1, P])
        orow = [sb(f"orow{i}", [P, D]) for i in range(3)]
        omiss = sb("omiss", [P, 1])
        oidx = [sb(f"oidx{i}", [P, 1], I32) for i in range(3)]

        def sems(names):
            return [ctx.enter_context(nc.semaphore(n)) for n in names.split()]

        src_loaded, x_loaded, rows_loaded, w_qk, w_vo, w_1, w_2 = sems("src_loaded x_loaded rows_loaded w_qk w_vo w_1 w_2")
        w_bias, gw_raw, rw_raw, f_w, attr0, attr1 = sems("w_bias gw_raw rw_raw f_w attr0 attr1")
        consts, cols_T, cols_ready, lcol_ready, e_conv = sems("consts cols_T cols_ready lcol_ready e_conv")
        r_zero, r_cnt, r_m, r_scan, r_mul, r_acc, sort_pe = sems("r_zero r_cnt r_m r_scan r_mul r_acc sort_pe")
        sort_dve, r_table, pos_ready, f_posi = sems("sort_dve r_table pos_ready f_posi")
        key_staged, scattered0, scattered1, spare_rows, spare_written = sems("key_staged scattered0 scattered1 spare_rows spare_written")
        ln_st, ln_mv, ln_log, ln_exp, ln_step, ln_stats = sems("ln_st ln_mv ln_log ln_exp ln_step ln_stats")
        qk_hi, qk_lo, w1_hi, w1_lo, w2_hi, w2_lo, gw_hi = sems("qk_hi qk_lo w1_hi w1_lo w2_hi w2_lo gw_hi")
        gw_lo, = sems("gw_lo")
        xs_norm, h_xh, h_T, h_aff, h_hi, h_lo = sems("xs_norm h_xh h_T h_aff h_hi h_lo")
        a_K, a_ks, a_max, c_mbc = sems("a_K a_ks a_max c_mbc")
        g_dk, g_ek, g_xh, g_esum, g_pe = sems("g_dk g_ek g_xh g_esum g_pe")
        ctx_pe, ctx_dve, d_hi, d_lo = sems("ctx_pe ctx_dve d_hi d_lo")
        b_Q, b_soft, b_qe, b_qT, b_qhi, b_qlo, b_M = sems("b_Q b_soft b_qe b_qT b_qhi b_qlo b_M")
        b_x1, = sems("b_x1")
        b_xh2, b_T2, b_aff2, b_hi2, b_lo2 = sems("b_xh2 b_T2 b_aff2 b_hi2 b_lo2")
        b_H, b_gelu, b_hhi, b_hlo, b_Y, b_x2 = sems("b_H b_gelu b_hhi b_hlo b_Y b_x2")
        s_in0, s_in1, s_in2, s_in3, s_kb, s_oh, s_hi = sems("s_in0 s_in1 s_in2 s_in3 s_kb s_oh s_hi")
        s_lo, s_pe, s_add, s_add2, s_ones = sems("s_lo s_pe s_add s_add2 s_ones")
        gcol_pe, gcol_ready, n_in0, n_in1, n_st, n_mv, n_ln = sems("gcol_pe gcol_ready n_in0 n_in1 n_st n_mv n_ln")
        n_r0, n_nw, n_stats, n_xn, n_an, n_T, n_hi = sems("n_r0 n_nw n_stats n_xn n_an n_T n_hi")
        n_lo, n_H, n_relu, n_hhi, n_hlo, n_Y, n_y = sems("n_lo n_H n_relu n_hhi n_hlo n_Y n_y")
        o_st, o_mv, o_ln, o_r0, o_nw, o_stats, n_z = sems("o_st o_mv o_ln o_r0 o_nw o_stats n_z")
        n_zT, n_zTs, n_log, n_top, rw_T, rw_ready = sems("n_zT n_zTs n_log n_top rw_T rw_ready")
        f_bias, f_ones, f_scat, f_in0, f_in1, f_in2, f_z = sems("f_bias f_ones f_scat f_in0 f_in1 f_in2 f_z")
        f_T, f_zT, f_h, f_hs, f_hT, f_hTs, f_o = sems("f_T f_zT f_h f_hs f_hT f_hTs f_o")
        f_row, f_idx, f_out0, f_out1, f_out2 = sems("f_row f_idx f_out0 f_out1 f_out2")
        ATTR, SCATTERED, S_IN = [attr0, attr1], [scattered0, scattered1], [s_in0, s_in1, s_in2, s_in3]
        N_IN, F_IN, F_OUT = [n_in0, n_in1], [f_in0, f_in1, f_in2], [f_out0, f_out1, f_out2]

        def mm(o, left, right, start, stop):
            return nc.tensor.matmul(o, left, right, start=start, stop=stop, skip_group_check=True)

        def mm3(o, left, right, start, stop):
            (lh, ll), (rh, rl) = left, right
            mm(o, lh, rh, start, False)
            mm(o, lh, rl, False, False)
            return mm(o, ll, rh, False, stop)

        def counted(eng, value):
            if isinstance(value, int):
                return value
            register = eng.alloc_register()
            eng.reg_mov(register, value)
            return register

        def at(halves, *where):
            return [h[where] for h in halves]

        def pipeline(eng, depth, body):
            for i in range(depth):
                body(i, lambda d, i=i: d <= i)
            with eng.Fori(depth, GROUPS) as i:
                body(i, lambda d: True)
            for i in range(GROUPS, GROUPS + depth):
                body(i, lambda d, i=i: i - d < GROUPS)

        def ln_a(l, g):
            return l * (2 * GROUPS) + (g + GROUPS)

        def ln_b(l, g):
            return l * (2 * GROUPS) + (g + 2 * GROUPS)

        def h_a(l, g):
            return l * (2 * GROUPS) + g

        def h_b(l, g):
            return l * (2 * GROUPS) + (g + GROUPS)

        def chunks(b, k=KC, n=GT):
            return b[:, 0:k * n].rearrange("p (k n) -> p k n", k=k)

        def pair(t, g, n=D):
            return t[:, bass.ds(g * PAIR, PAIR), 0:n]

        def f32(ap):
            return ap.bitcast(F32)

        block = ctx.enter_context(nc.Block())

        @block.sync
        def _(sp):
            sp.dma_start(src_i[:, :], src.rearrange("(p c) -> p c", c=ECOL)).then_inc(src_loaded, 16)
            r = 0
            for a, n in ((ln1_g, ROWS_LN), (ln1_b, ROWS_LN), (ln2_g, ROWS_LN), (ln2_b, ROWS_LN), (mb1, LAYERS * FC)):
                sp.dma_start(colrows[r:r + n, :], a.rearrange("l (c f) -> (l c) f", f=128)).then_inc(rows_loaded, 16)
                r += n
            sp.dma_start(colrows[r:r + GHC, :], gb1.rearrange("(c f) -> c f", f=128)).then_inc(rows_loaded, 16)
            sp.dma_start(colrows[r + GHC:r + GHC + 1, :], u[0:1, :]).then_inc(rows_loaded, 16)
            sp.dma_start(res[:, :, 0:D], x_rows).then_inc(x_loaded, 16)

            def weights(w, l, n):
                return w[bass.ds(l, 1), :, :].rearrange("l (k p) n -> p (l k) n", p=128)

            with sp.Fori(0, LAYERS) as l:
                sp.wait_ge(w2_hi, l)
                sp.wait_ge(w2_lo, l)
                raw_qk = raw[:, 0:KC * 2 * D].rearrange("p (k n) -> p k n", k=KC)
                sp.dma_start(raw_qk[:, :, 0:D], weights(Wq, l, D)).then_inc(w_qk, 16)
                sp.dma_start(raw_qk[:, :, D:2 * D], weights(Wk, l, D)).then_inc(w_qk, 16)
                sp.wait_ge(ctx_pe, 5 * l)
                sp.dma_start(raw_vo[:, 0, :, :], weights(Wv, l, D)).then_inc(w_vo, 16)
                sp.dma_start(raw_vo[:, 1, :, :], weights(Wo, l, D)).then_inc(w_vo, 16)
                sp.wait_ge(qk_hi, l + 1)
                sp.wait_ge(qk_lo, l + 1)
                sp.dma_start(raw[:, :].rearrange("p (k n) -> p k n", k=KC), weights(mW1, l, FF)).then_inc(w_1, 16)
                sp.wait_ge(b_x2, l * (2 * GROUPS))
                sp.dma_start(bo_b[:, :], bo[bass.ds(l, 1), :].to_broadcast((P, D))).then_inc(w_bias, 16)
                sp.dma_start(b2_b[:, :], mb2[bass.ds(l, 1), :].to_broadcast((P, D))).then_inc(w_bias, 16)
                sp.wait_ge(w1_hi, l + 1)
                sp.wait_ge(w1_lo, l + 1)
                sp.dma_start(raw[:, :].rearrange("p (k n) -> p k n", k=FC), weights(mW2, l, D)).then_inc(w_2, 16)

            sp.wait_ge(b_x2, 2 * LAYERS * GROUPS)
            sp.dma_start(raw_g1[:, 0:2, :], gW1[0:D, :].rearrange("(k p) n -> p k n", p=128)).then_inc(gw_raw, 16)
            sp.dma_start(raw_g1[0:EA, 2, :], gW1[D:D + EA, :]).then_inc(gw_raw, 16)
            sp.dma_start(raw_gu[:, :], gW1[D + EA:D + EA + GLOB, :]).then_inc(gw_raw, 16)
            sp.dma_start(raw_g2[:, :, :], gW2.rearrange("(k p) n -> p k n", p=128)).then_inc(gw_raw, 16)
            sp.dma_start(gb2_b[:, :], gb2.rearrange("(a n) -> a n", a=1).to_broadcast((P, D))).then_inc(gw_raw, 16)
            sp.dma_start(rw_in[:, :], rw).then_inc(rw_raw, 16)
            sp.dma_start(rb_b[:, :], rb.rearrange("(a n) -> a n", a=1).to_broadcast((P, EXP))).then_inc(rw_raw, 16)

            sp.wait_ge(r_table, 1)
            for slot in range(2):
                sp.wait_ge(SCATTERED[slot], 16 * CH * (CHUNKS // 2))
            sp.wait_ge(spare_written, 16)

            def load_segment(n, slot):
                first = sp.value_load(efirst_i[0:1, bass.ds(n, 1)], min_val=0, max_val=(ETILES - 1) * SEG)
                if not (isinstance(n, int) and n < 4):
                    sp.wait_ge(s_lo, n - 3)
                    sp.wait_ge(s_kb, n - 3)
                sp.dma_start(rows_in[slot][:, :, :],
                             edges_sorted[bass.ds(first, SEG), :].rearrange("(p r) c -> p r c", r=SEGR)).then_inc(S_IN[slot], 16)

            for n in range(4):
                load_segment(n, n)
            with sp.Fori(1, ESEGS // 4) as q:
                for slot in range(4):
                    load_segment(4 * q + slot, slot)
            load_segment(ESEGS - 1, 0)

            def load_x(g, slot):
                sp.dma_start(x_in[:, slot, :, :], x_rows[:, bass.ds(g * PAIR, PAIR), :]).then_inc(N_IN[slot], 16)
            load_x(0, 0)
            load_x(1, 1)
            with sp.Fori(1, GROUPS // 2) as q:
                for slot in range(2):
                    sp.wait_ge(n_y, 3 * (2 * q + (slot - 1)))
                    load_x(2 * q + slot, slot)
            sp.wait_ge(n_y, 3 * (GROUPS - 2))
            load_x(GROUPS - 1, 0)

            sp.wait_ge(n_top, 6 * GROUPS)
            for k in range(KC):
                sp.dma_start(fw1[:, k, :].rearrange("p (e h) -> p e h", h=EH),
                             fW1[:, k * 128:(k + 1) * 128, :].rearrange("e p h -> p e h")).then_inc(f_w, 16)
            sp.dma_start(fw2[0:EH, :].rearrange("p (e h) -> p e h", h=D), fW2.rearrange("e p h -> p e h")).then_inc(f_w, 16)
            sp.dma_start(fb1_r[:, :], fb1.rearrange("(a e) h -> a (e h)", a=1)).then_inc(f_w, 16)
            sp.dma_start(fw2[EH:EH + 1, :], fb2.rearrange("(a e) h -> a (e h)", a=1)).then_inc(f_w, 16)

            sp.wait_ge(f_scat, 16 * TILES)
            sp.wait_ge(r_table, 2)

            def load_tokens(n, slot):
                first = sp.value_load(ffirst_i[0:1, bass.ds(n, 1)], min_val=0, max_val=N - P)
                rows = tokens_sorted[bass.ds(first, P), :]
                if not isinstance(n, int):
                    used, placed = counted(sp, n - 2), counted(sp, 2 * (n - 2))
                    sp.wait_ge(f_row, used)
                    sp.wait_ge(f_idx, placed)
                sp.dma_start(yin[slot][:, :], rows).then_inc(F_IN[slot], 16)
            for n in range(3):
                load_tokens(n, n)
            with sp.Fori(1, FSEGS // 3) as q:
                for slot in range(3):
                    load_tokens(3 * q + slot, slot)

        @block.gpsimd
        def _(pool):
            nc.gpsimd.memset(ones[:, :], 1.0).then_inc(consts, 1)
            nc.gpsimd.memset(ones_e[:, :], 1.0).then_inc(consts, 1)
            nc.gpsimd.memset(eps[:, :], EPS).then_inc(consts, 1)
            nc.gpsimd.memset(blockmask[:, :], 0.0).then_inc(consts, 1)
            nc.gpsimd.memset(stage[:, 0, :, :], 0.0).then_inc(consts, 1)
            pool.wait_ge(consts, 5)
            nc.gpsimd.affine_select(out=ident[:, :], in_=ones[:, :], compare_op=ALU.is_equal, fill=0.0,
                                    base=0, pattern=[[-1, 128]], channel_multiplier=1).then_inc(consts, 1)
            nc.gpsimd.affine_select(out=tri[:, :], in_=ones[:, :], compare_op=ALU.is_gt, fill=0.0,
                                    base=0, pattern=[[1, 128]], channel_multiplier=-1).then_inc(consts, 1)
            pool.wait_ge(consts, 7)
            for h in range(128 // DH):
                nc.gpsimd.memset(blockmask[h * DH:(h + 1) * DH, h * DH:(h + 1) * DH], 1.0).then_inc(consts, 1)
            pool.wait_ge(consts, 7 + 128 // DH)
            for tile, pattern, mult in ((iota_node, [[TILES, P]], 0), (iota_seg, [[1, ESEGS]], 0), (iota_part, [[1, 1]], 1)):
                nc.gpsimd.iota(tile[:, :], pattern=pattern, base=0, channel_multiplier=mult,
                               allow_small_or_imprecise_dtypes=True).then_inc(consts, 1)
            nc.gpsimd.memset(stage[:, 0, :, EA:ROW], -1.0).then_inc(spare_rows, 1)
            pool.wait_ge(spare_rows, 1)
            pool.dma_start(edges_sorted[EDGES:ETILES * SEG, :].rearrange("(p r) c -> p r c", r=SPARE // SPARE_P),
                           stage[0:SPARE_P, 0, 0:SPARE // SPARE_P, :]).then_inc(spare_written, 16)
            pool.wait_ge(spare_written, 16)

            def load_attr(c, slot):
                pool.dma_start(stage[:, slot, :, 0:EA], edge_rows[:, bass.ds(c * CH, CH), :]).then_inc(ATTR[slot], 16)

            def scatter(q, slot):
                c = 2 * q + slot
                nc.gpsimd.tensor_copy(idx[:, slot, :], pos_i[:, bass.ds(c * CH, CH)]).then_inc(key_staged, 1)
                nc.gpsimd.tensor_copy(stage[:, slot, :, EA], src_f[:, bass.ds(c * CH, CH)]).then_inc(key_staged, 1)
                staged, loaded = counted(pool, 2 * c + 2), counted(pool, 16 * q + 16)
                pool.wait_ge(pos_ready, 1)
                pool.wait_ge(key_staged, staged)
                pool.wait_ge(ATTR[slot], loaded)
                for j in range(CH):
                    nc.gpsimd.indirect_dma_start(
                        out=edges_sorted, out_offset=bass.IndirectOffsetOnAxis(ap=idx[:, slot, j:j + 1], axis=0),
                        in_=stage[:, slot, j, :], in_offset=None).then_inc(SCATTERED[slot], 16)

            load_attr(0, 0)
            load_attr(1, 1)
            pool.wait_ge(pos_ready, 1)
            scatter(0, 0)
            scatter(0, 1)
            with pool.Fori(1, CHUNKS // 2) as q:
                for slot in range(2):
                    pool.wait_ge(SCATTERED[slot], 16 * CH * q)
                    load_attr(2 * q + slot, slot)
                for slot in range(2):
                    scatter(q, slot)

            nc.gpsimd.iota(res[:, :, D + 2], pattern=[[1, TILES]], base=0, channel_multiplier=TILES,
                           allow_small_or_imprecise_dtypes=True).then_inc(f_ones, 1)
            pool.wait_ge(f_ones, 1)
            pool.wait_ge(f_posi, 1)
            for t in range(TILES):
                nc.gpsimd.indirect_dma_start(
                    out=tokens_sorted, out_offset=bass.IndirectOffsetOnAxis(ap=fpos_i[:, t:t + 1], axis=0),
                    in_=res[:, t, :], in_offset=None).then_inc(f_scat, 16)

            def put(n, slot):
                rows, places = counted(pool, n + 1), counted(pool, 2 * n + 2)
                pool.wait_ge(f_scat, 16 * TILES)
                pool.wait_ge(f_row, rows)
                pool.wait_ge(f_idx, places)
                nc.gpsimd.indirect_dma_start(
                    out=out, out_offset=bass.IndirectOffsetOnAxis(ap=oidx[slot][:, :], axis=0),
                    in_=orow[slot][:, :], in_offset=None, bounds_check=N - 1, oob_is_err=False).then_inc(F_OUT[slot], 16)
            with pool.Fori(0, FSEGS // 3) as q:
                for slot in range(3):
                    put(3 * q + slot, slot)
            for slot in range(3):
                pool.wait_ge(F_OUT[slot], 16 * (FSEGS // 3))

        @block.scalar
        def _(act):
            def ident_act(o, i, **kw):
                return nc.scalar.activation(o, i, ACT.Identity, **kw)

            def ln_rstd(ln, r0, mvd, n):
                act.wait_ge(mvd, PAIR * (n + 1))
                nc.scalar.activation(lnt[:, 0, :], mv[:, :, 1], ACT.Ln, bias=eps[0:P, :]).then_inc(ln, 1)
                act.wait_ge(ln, n + 1)
                nc.scalar.activation(lnt[:, 1, :], lnt[:, 0, :], ACT.Exp, scale=-0.5).then_inc(r0, 1)

            def normalise(o, st, g, done):
                for j in range(PAIR):
                    t = g * PAIR + j
                    a = ident_act(o[:, j, :], res[:, bass.ds(t, 1), 0:D].rearrange("p a d -> p (a d)"),
                                  scale=st[:, bass.ds(t, 1), 0:1].rearrange("p a d -> p (a d)"),
                                  bias=st[:, bass.ds(t, 1), 1:2].rearrange("p a d -> p (a d)"))
                a.then_inc(done, 1)

            def split_hi(o, i, loaded, count, done):
                act.wait_ge(loaded, count)
                nc.scalar.copy(o, i).then_inc(done, 1)

            act.wait_ge(consts, NCONST)
            act.wait_ge(cols_T, 1)
            nc.scalar.copy(cols[:, :], PS[:, 0:NROW]).then_inc(cols_ready, 1)

            with act.Fori(0, GROUPS) as g:
                ln_rstd(ln_log, ln_exp, ln_mv, g)
                act.wait_ge(ln_stats, g + 1)
                for j in range(PAIR):
                    t = g * PAIR + j
                    row = res[:, bass.ds(t, 1), 0:D].rearrange("p a d -> p (a d)")
                    a = ident_act(row, row, scale=lnst[:, bass.ds(t, 1), 0:1].rearrange("p a d -> p (a d)"),
                                  bias=lnst[:, bass.ds(t, 1), 1:2].rearrange("p a d -> p (a d)"))
                a.then_inc(xs_norm, 1)

            with act.Fori(0, LAYERS) as l:
                act.wait_ge(b_x2, l * (2 * GROUPS))
                split_hi(wqk[0][:, :, :], raw[:, 0:KC * 2 * D].rearrange("p (k n) -> p k n", k=KC), w_qk, 32 * l + 32, qk_hi)

                def keys(i, live):
                    if live(1):
                        n = l * GROUPS + (i - 1)
                        act.wait_ge(h_aff, h_a(l, i - 1) + 1)
                        act.wait_ge(a_K, n)
                        nc.scalar.copy(hT[0][:, :, :], affine[:, :, :]).then_inc(h_hi, 1)
                    if live(2):
                        n = l * GROUPS + (i - 2)
                        act.wait_ge(a_K, n + 1)
                        nc.scalar.copy(pair(ksb, i - 2), PQ[0:P, :].rearrange("p (j d) -> p j d", j=PAIR)).then_inc(a_ks, 1)
                    if live(0):
                        ln_rstd(ln_log, ln_exp, ln_mv, ln_a(l, i))
                        act.wait_ge(ln_stats, ln_a(l, i) + 1)
                        act.wait_ge(h_T, h_a(l, i))
                        normalise(xh[0], lnst, i, h_xh)
                pipeline(act, 2, keys)

                split_hi(w1[0][:, :, :], raw[:, :].rearrange("p (k n) -> p k n", k=KC), w_1, 16 * l + 16, w1_hi)
                act.wait_ge(ctx_pe, 5 * l + 2)
                nc.scalar.copy(mbc[:, :], PS[0:P, 0:D]).then_inc(c_mbc, 1)

                def key_exp(g, slot):
                    n = l * GROUPS + g
                    if not isinstance(g, int):
                        act.wait_ge(g_pe, n - 1)
                    normalise(xh[slot], lnst, g, g_xh)
                    act.wait_ge(g_dk, n + 1)
                    nc.scalar.activation(ek[:, slot, :, :], ek[:, slot, :, :], ACT.Exp, scale=SCALE).then_inc(g_ek, 1)
                key_exp(0, 0)
                with act.Fori(0, GROUPS // 2) as q:
                    key_exp(2 * q + 1, 1)
                    key_exp(2 * q + 2, 0)

                split_hi(w2[0][:, :, :], raw[:, :].rearrange("p (k n) -> p k n", k=FC), w_2, 16 * l + 16, w2_hi)
                act.wait_ge(ctx_pe, 5 * l + 5)
                nc.scalar.copy(mmat[0][:, :, :], chunks(PS, KC, D)).then_inc(d_hi, 1)

                def rest(i, live):
                    n0, n1, n2 = (l * GROUPS + (i - d) for d in range(3))
                    if live(1):
                        act.wait_ge(b_qT, n1 + 1)
                        act.wait_ge(b_M, n1)
                        nc.scalar.copy(qT[0][:, :, :], chunks(PQT)).then_inc(b_qhi, 1)
                    if live(0):
                        act.wait_ge(h_T, h_b(l, i))
                        normalise(xh[0], lnst, i, h_xh)

                    def gelu(c):
                        act.wait_ge(b_H, 4 * n2 + c + 1)
                        for j in range(2):
                            a = nc.scalar.activation(hid[c % 2][:, j, :], chunks(PH[c % 2])[:, j, :], ACT.Gelu,
                                                     bias=lcol[:, 4 * KC + 2 * c + j:4 * KC + 2 * c + j + 1])
                        a.then_inc(b_gelu, 1)
                        act.wait_ge(b_gelu, 4 * n2 + c + 1)
                        nc.scalar.copy(hidh[c % 2][0][:, :, :], hid[c % 2][:, :, :]).then_inc(b_hhi, 1)
                    if live(2):
                        gelu(0)
                    if live(0):
                        act.wait_ge(h_aff, h_b(l, i) + 1)
                        nc.scalar.copy(hT[0][:, :, :], affine[:, :, :]).then_inc(h_hi, 1)
                    if live(2):
                        gelu(1)
                    if live(1):
                        ln_rstd(ln_log, ln_exp, ln_mv, ln_b(l, i - 1))
                    if live(0):
                        act.wait_ge(b_soft, 5 * n0 + 2)
                        nc.scalar.activation(qd[:, :, :], qd[:, :, :], ACT.Exp, scale=SCALE).then_inc(b_qe, 1)
                    if live(2):
                        gelu(2)
                    if live(1):
                        act.wait_ge(ln_stats, ln_b(l, i - 1) + 1)
                        act.wait_ge(b_T2, n1)
                        normalise(xh[1], lnst, i - 1, b_xh2)
                    if live(2):
                        gelu(3)
                    if live(1):
                        act.wait_ge(b_aff2, n1 + 1)
                        nc.scalar.copy(h2T[0][:, :, :], affine[:, :, :]).then_inc(b_hi2, 1)
                pipeline(act, 2, rest)

            act.wait_ge(gw_raw, 80)
            nc.scalar.copy(g1[0][:, 0:2, :], raw_g1[:, 0:2, :]).then_inc(gw_hi, 1)
            nc.scalar.copy(g1[0][0:EA, 2, :], raw_g1[0:EA, 2, :]).then_inc(gw_hi, 1)
            nc.scalar.copy(g2[0][:, :, :], raw_g2[:, :, :]).then_inc(gw_hi, 1)
            act.wait_ge(rw_T, 1)
            nc.scalar.copy(rwT[:, :, :], chunks(PT, KC, EXP)).then_inc(rw_ready, 1)

            def seg_hi(n, slot, turn):
                act.wait_ge(S_IN[slot], 16 * turn + 16)
                if not (isinstance(n, int) and n < 2):
                    act.wait_ge(s_pe, n - 1)
                nc.scalar.copy(ehl[slot % 2][:, :, 0:EA], rows_in[slot][:, :, 0:EA]).then_inc(s_hi, 1)
            for n in range(4):
                seg_hi(n, n, 0)
            with act.Fori(1, ESEGS // 4) as q:
                for slot in range(4):
                    seg_hi(4 * q + slot, slot, q)
            seg_hi(ESEGS - 1, 0, ESEGS // 4)

            def graph(i, live):
                if live(0):
                    ln_rstd(n_ln, n_r0, n_mv, i)
                    act.wait_ge(n_stats, i + 1)
                    act.wait_ge(n_T, i)
                    for j in range(PAIR):
                        xin = x_in[:, bass.ds(i % 2, 1), j, :].rearrange("p a d -> p (a d)")
                        a = ident_act(xn[:, j, :], xin, scale=gst[:, j, 0:1], bias=gst[:, j, 1:2])
                    a.then_inc(n_xn, 1)
                if live(1):
                    for c in range(2):
                        act.wait_ge(n_H, 2 * (i - 1) + c + 1)
                        for j in range(2):
                            a = nc.scalar.activation(ghid[c][:, j, :], chunks(PH[c])[:, j, :], ACT.Relu,
                                                     bias=g1col[:, 2 * c + j:2 * c + j + 1])
                        a.then_inc(n_relu, 1)
                        act.wait_ge(n_relu, 2 * (i - 1) + c + 1)
                        nc.scalar.copy(ghh[c][0][:, :, :], ghid[c][:, :, :]).then_inc(n_hhi, 1)
                if live(0):
                    act.wait_ge(n_T, i + 1)
                    act.wait_ge(n_H, 2 * i)
                    nc.scalar.copy(cT[0][:, 0:2, :], chunks(PT)).then_inc(n_hi, 1)
                    nc.scalar.copy(cT[0][0:EA, 2, :], PS[0:EA, 0:GT]).then_inc(n_hi, 1)
                if live(2):
                    act.wait_ge(n_zT, i - 1)
                    nc.scalar.copy(zT[:, :, :], chunks(PQ)).then_inc(n_zTs, 1)
                if live(1):
                    ln_rstd(o_ln, o_r0, o_mv, i - 1)
                    act.wait_ge(o_stats, i)
                    act.wait_ge(n_zT, i - 1)
                    for j in range(PAIR):
                        row = res[:, bass.ds((i - 1) * PAIR + j, 1), :].rearrange("p a d -> p (a d)")
                        a = ident_act(zt[:, j, :], row[:, 0:D], scale=row[:, D:D + 1], bias=row[:, D + 1:D + 2])
                    a.then_inc(n_z, 1)
            pipeline(act, 2, graph)

            def expert(n, slot, turn):
                act.wait_ge(F_IN[slot], 16 * turn + 16)
                act.wait_ge(f_T, n)
                y = yin[slot]
                ident_act(zs[:, :], y[:, 0:D], scale=y[:, D:D + 1], bias=y[:, D + 1:D + 2]).then_inc(f_z, 1)
                act.wait_ge(f_h, n + 1)
                act.wait_ge(f_hT, n)
                nc.scalar.activation(hs[:, :], PM[0:P, 0:EH], ACT.Relu).then_inc(f_hs, 1)
                act.wait_ge(f_hT, n + 1)
                act.wait_ge(f_o, n)
                nc.scalar.copy(hsT[0:EH, :], PQT[0:EH, 0:P]).then_inc(f_hTs, 1)
            with act.Fori(0, FSEGS // 3) as q:
                for slot in range(3):
                    expert(3 * q + slot, slot, q)

        @block.vector
        def _(dve):
            def ln_moments(tiles, st, mvd, n):
                for j in range(PAIR):
                    nc.vector.bn_stats(bn[:, j, :], tiles[j]).then_inc(st, 1)
                stats = counted(dve, PAIR * (n + 1))
                dve.wait_ge(consts, NCONST)
                dve.wait_ge(st, stats)
                for j in range(PAIR):
                    nc.vector.bn_aggr(mv[:, j, :], bn[:, j, :]).then_inc(mvd, 1)

            def ln_finish(o, r0, step, done, n):
                dve.wait_ge(r0, n + 1)
                nc.vector.scalar_tensor_tensor(out=lnt[:, 2, :], in0=mv[:, :, 1], scalar=EPS, in1=lnt[:, 1, :],
                                               op0=ALU.add, op1=ALU.mult).then_inc(step, 1)
                dve.wait_ge(step, 3 * n + 1)
                nc.vector.scalar_tensor_tensor(out=lnt[:, 3, :], in0=lnt[:, 2, :], scalar=-0.5, in1=lnt[:, 1, :],
                                               op0=ALU.mult, op1=ALU.mult).then_inc(step, 1)
                dve.wait_ge(step, 3 * n + 2)
                nc.vector.scalar_tensor_tensor(out=o[:, :, 0], in0=lnt[:, 3, :], scalar=1.5, in1=lnt[:, 1, :],
                                               op0=ALU.add, op1=ALU.mult).then_inc(step, 1)
                dve.wait_ge(step, 3 * n + 3)
                nc.vector.scalar_tensor_tensor(out=o[:, :, 1], in0=mv[:, :, 0], scalar=-1.0, in1=o[:, :, 0],
                                               op0=ALU.mult, op1=ALU.mult).then_inc(done, 1)

            def tile_rows(t, g):
                return [t[:, bass.ds(g * PAIR + j, 1), 0:D].rearrange("p a d -> p (a d)") for j in range(PAIR)]

            def split_lo(o, i, hi, count, done):
                dve.wait_ge(done[0], count)
                nc.vector.tensor_tensor(o, i, f32(hi), ALU.subtract).then_inc(done[1], 1)

            def count_sort(kinds, ncol, nk, width, scr, pos, pos_int, segs, kind, kind_int, first_int, turn):
                nb = TILES * turn
                nc.vector.memset(pos, 0.0).then_inc(r_zero, 1)
                with dve.Fori(0, nk) as b:
                    dve.wait_ge(r_cnt, nb + b)
                    nc.vector.tensor_scalar(scr[0], kinds, iota_seg[0:P, bass.ds(b, 1)], 0.0, ALU.is_equal, ALU.add,
                                            accum_out=cnt[:, bass.ds(b, 1)]).then_inc(r_cnt, 1)
                dve.wait_ge(sort_pe, 3 * turn + 1)
                nc.vector.tensor_copy(tot[:, 0:nk], PS[0:P, 64:64 + nk]).then_inc(sort_dve, 1)
                dve.wait_ge(sort_dve, SORT_DVE * turn + 1)
                nc.vector.tensor_tensor_scan(totinc[:, 0:nk], ones[0:P, 0:nk], tot[:, 0:nk], 0.0, ALU.mult, ALU.add).then_inc(sort_dve, 1)
                dve.wait_ge(sort_dve, SORT_DVE * turn + 2)
                nc.vector.tensor_tensor(base[:, 0:nk], totinc[:, 0:nk], tot[:, 0:nk], ALU.subtract).then_inc(sort_dve, 1)
                dve.wait_ge(sort_dve, SORT_DVE * turn + 3)
                nc.vector.tensor_tensor(base[:, 0:nk], base[:, 0:nk], PS[0:P, 0:nk], ALU.add).then_inc(sort_dve, 1)
                nc.vector.tensor_copy(kcol[0:nk, 0:1], PS[0:nk, 128:129]).then_inc(sort_dve, 1)
                dve.wait_ge(sort_dve, SORT_DVE * turn + 4)
                dve.wait_ge(r_zero, turn + 1)
                with dve.Fori(0, nk) as b:
                    dve.wait_ge(r_mul, nb + b)
                    nc.vector.tensor_scalar(scr[0], kinds, iota_seg[0:P, bass.ds(b, 1)], None, ALU.is_equal).then_inc(r_m, 1)
                    dve.wait_ge(r_m, nb + b + 1)
                    nc.vector.tensor_tensor_scan(scr[1], ones_e[:, 0:ncol] if turn == 0 else ones[0:P, 0:ncol], scr[0],
                                                 base[:, bass.ds(b, 1)], ALU.mult, ALU.add).then_inc(r_scan, 1)
                    dve.wait_ge(r_scan, nb + b + 1)
                    nc.vector.tensor_tensor(scr[2], scr[1], scr[0], ALU.mult).then_inc(r_mul, 1)
                    dve.wait_ge(r_mul, nb + b + 1)
                    nc.vector.tensor_tensor(pos, pos, scr[2], ALU.add).then_inc(r_acc, 1)
                    dve.wait_ge(r_acc, nb + b + 1)
                nc.vector.tensor_scalar(pos_int, pos, -1.0, None, ALU.add).then_inc(pos_ready if turn == 0 else f_posi, 1)
                dve.wait_ge(sort_pe, 3 * turn + 2)
                nc.vector.tensor_scalar(kcol[0:nk, 1:2], PS[0:nk, 130:131], 1.0 / width, 0.5 / width - 0.5, ALU.mult, ALU.add).then_inc(sort_dve, 1)
                dve.wait_ge(sort_dve, SORT_DVE * turn + 6)
                nc.vector.tensor_scalar(kcol[0:nk, 2:3], kcol[0:nk, 1:2], RND, None, ALU.add).then_inc(sort_dve, 1)
                dve.wait_ge(sort_dve, SORT_DVE * turn + 7)
                nc.vector.tensor_scalar(kcol[0:nk, 3:4], kcol[0:nk, 2:3], -RND, None, ALU.add).then_inc(sort_dve, 1)
                dve.wait_ge(sort_dve, SORT_DVE * turn + 8)
                nc.vector.tensor_tensor(kcol[0:nk, 1:2], kcol[0:nk, 3:4], iota_part[0:nk, :], ALU.add).then_inc(sort_dve, 1)
                dve.wait_ge(sort_dve, SORT_DVE * turn + 9)
                nc.vector.tensor_scalar(cmp[0:nk, 0:segs], iota_seg[0:nk, 0:segs], kcol[0:nk, 1:2], None, ALU.is_ge).then_inc(sort_dve, 1)
                dve.wait_ge(sort_pe, 3 * turn + 3)
                nc.vector.tensor_scalar(kind[:, 0:segs], PS[:, 0:segs], -1.0, None, ALU.add).then_inc(sort_dve, 1)
                dve.wait_ge(sort_dve, SORT_DVE * turn + 11)
                nc.vector.tensor_copy(kind_int[:, 0:segs], kind[0:1, 0:segs]).then_inc(sort_dve, 1)
                nc.vector.tensor_tensor(segtmp[:, 0:segs], iota_seg[0:1, 0:segs], kind[0:1, 0:segs], ALU.subtract).then_inc(sort_dve, 1)
                dve.wait_ge(sort_dve, SORT_DVE * turn + 12)
                dve.wait_ge(sort_dve, SORT_DVE * turn + 13)
                nc.vector.tensor_scalar(first_int[:, 0:segs], segtmp[:, 0:segs], float(width), None, ALU.mult).then_inc(r_table, 1)

            dve.wait_ge(consts, NCONST)
            dve.wait_ge(src_loaded, 16)
            nc.vector.tensor_copy(src_f[:, :], src_i[:, :]).then_inc(e_conv, 1)
            dve.wait_ge(e_conv, 1)
            nc.vector.tensor_scalar(scr[0][:, :], src_f[:, :], 1.0 / TILES, 0.5 / TILES - 0.5, ALU.mult, ALU.add).then_inc(e_conv, 1)
            dve.wait_ge(e_conv, 2)
            nc.vector.tensor_scalar(scr[1][:, :], scr[0][:, :], RND, None, ALU.add).then_inc(e_conv, 1)
            dve.wait_ge(e_conv, 3)
            nc.vector.tensor_scalar(scr[2][:, :], scr[1][:, :], -RND, None, ALU.add).then_inc(e_conv, 1)
            dve.wait_ge(e_conv, 4)
            nc.vector.scalar_tensor_tensor(out=tile_of[:, :], in0=scr[2][:, :], scalar=-float(TILES), in1=src_f[:, :],
                                           op0=ALU.mult, op1=ALU.add).then_inc(e_conv, 1)
            dve.wait_ge(e_conv, 5)
            count_sort(tile_of[:, :], ECOL, TILES, SEG, [t[:, :] for t in scr], pos_f[:, :], pos_i[:, :], ESEGS,
                       ekind, ekind_i, efirst_i, 0)

            dve.wait_ge(x_loaded, 16)
            with dve.Fori(0, GROUPS) as g:
                ln_moments(tile_rows(res, g), ln_st, ln_mv, g)
                ln_finish(lnst[:, bass.ds(g * PAIR, PAIR), :], ln_exp, ln_step, ln_stats, g)
            dve.wait_ge(xs_norm, GROUPS)
            dve.wait_ge(cols_ready, 1)

            def add_rows(g, what, done):
                nc.vector.tensor_tensor(pair(res, g), pair(res, g), what, ALU.add).then_inc(done, 1)

            def affine_of(col, done):
                for k in range(KC):
                    a = nc.vector.tensor_scalar(affine[:, k, :], chunks(PT)[:, k, :], lcol[:, col + k:col + k + 1],
                                                lcol[:, col + KC + k:col + KC + k + 1], ALU.mult, ALU.add)
                a.then_inc(done, 1)

            with dve.Fori(0, LAYERS) as l:
                dve.wait_ge(b_x2, l * (2 * GROUPS))
                dve.wait_ge(b_gelu, 4 * (l * GROUPS))
                nc.vector.tensor_copy(lcol[:, 0:4 * KC].rearrange("p (w k) -> p w k", k=KC),
                                      cols[:, 0:4 * ROWS_LN].rearrange("p (w r) -> p w r", r=ROWS_LN)[:, :, bass.ds(l * KC, KC)]).then_inc(lcol_ready, 1)
                nc.vector.tensor_copy(lcol[:, 4 * KC:4 * KC + FC], cols[:, bass.ds(4 * ROWS_LN + l * FC, FC)]).then_inc(lcol_ready, 1)
                nc.vector.memset(kmax[:, :, :], -3.4e38).then_inc(lcol_ready, 1)
                nc.vector.memset(esum[:, :, :], 0.0).then_inc(lcol_ready, 1)
                split_lo(wqk[1][:, :, :], raw[:, 0:KC * 2 * D].rearrange("p (k n) -> p k n", k=KC), wqk[0][:, :, :], l + 1, (qk_hi, qk_lo))
                parameters = counted(dve, 4 * l + 4)
                dve.wait_ge(x_loaded, 16)
                dve.wait_ge(lcol_ready, parameters)

                def keys(i, live):
                    if live(0):
                        ln_moments(tile_rows(res, i), ln_st, ln_mv, ln_a(l, i))
                    if live(1):
                        dve.wait_ge(h_lo, h_a(l, i - 1))
                        dve.wait_ge(h_T, h_a(l, i - 1) + 1)
                        affine_of(0, h_aff)
                    if live(0):
                        ln_finish(lnst[:, bass.ds(i * PAIR, PAIR), :], ln_exp, ln_step, ln_stats, ln_a(l, i))
                    if live(1):
                        dve.wait_ge(h_hi, h_a(l, i - 1) + 1)
                        nc.vector.tensor_tensor(hT[1][:, :, :], affine[:, :, :], f32(hT[0][:, :, :]), ALU.subtract).then_inc(h_lo, 1)
                    if live(2):
                        n = l * GROUPS + (i - 2)
                        dve.wait_ge(a_ks, n + 1)
                        dve.wait_ge(a_max, n)
                        nc.vector.tensor_tensor(kmax[:, :, :], kmax[:, :, :], pair(ksb, i - 2), ALU.max).then_inc(a_max, 1)
                pipeline(dve, 2, keys)

                split_lo(w1[1][:, :, :], raw[:, :].rearrange("p (k n) -> p k n", k=KC), w1[0][:, :, :], l + 1, (w1_hi, w1_lo))
                dve.wait_ge(a_max, (l + 1) * GROUPS)
                nc.vector.tensor_tensor(km[:, :], kmax[:, 0, :], kmax[:, 1, :], ALU.max).then_inc(ctx_dve, 1)
                dve.wait_ge(ctx_pe, 5 * l + 1)
                nc.vector.tensor_reduce(mcol[:, :], chunks(PT, KC, P), AX, ALU.max).then_inc(ctx_dve, 1)
                dve.wait_ge(ctx_dve, 8 * l + 2)
                for k in range(KC):
                    a = nc.vector.tensor_scalar(dg[:, k, :], ident[:, :], mcol[:, k:k + 1], None, ALU.mult)
                a.then_inc(ctx_dve, 1)
                dve.wait_ge(c_mbc, l + 1)

                def key_exp(g, slot):
                    n = l * GROUPS + g
                    if not isinstance(g, int):
                        dve.wait_ge(g_esum, n - 1)
                        dve.wait_ge(g_pe, n - 1)
                    nc.vector.tensor_tensor(ek[:, slot, :, :], pair(ksb, g), mbc[:, :].unsqueeze(1).to_broadcast((P, PAIR, D)),
                                            ALU.subtract).then_inc(g_dk, 1)

                def add_exp(g, slot):
                    n = l * GROUPS + g
                    dve.wait_ge(g_ek, n + 1)
                    dve.wait_ge(g_esum, n)
                    nc.vector.tensor_tensor(esum[:, :, :], esum[:, :, :], ek[:, slot, :, :], ALU.add).then_inc(g_esum, 1)
                key_exp(0, 0)
                with dve.Fori(0, GROUPS // 2) as q:
                    key_exp(2 * q + 1, 1)
                    add_exp(2 * q, 0)
                    key_exp(2 * q + 2, 0)
                    add_exp(2 * q + 1, 1)
                add_exp(GROUPS - 1, 0)

                split_lo(w2[1][:, :, :], raw[:, :].rearrange("p (k n) -> p k n", k=FC), w2[0][:, :, :], l + 1, (w2_hi, w2_lo))
                dve.wait_ge(ctx_pe, 5 * l + 3)
                nc.vector.reciprocal(gn[:, 1, :], PS[:, 0:D]).then_inc(ctx_dve, 1)
                dve.wait_ge(ctx_dve, 8 * l + 4)
                dve.wait_ge(g_pe, (l + 1) * GROUPS)
                nc.vector.tensor_tensor(gn[:, 0, :], chunks(PQT, KC, D)[:, 0, :], gn[:, 1, :], ALU.mult).then_inc(ctx_dve, 1)
                nc.vector.tensor_tensor(gn[:, 1, :], chunks(PQT, KC, D)[:, 1, :], gn[:, 1, :], ALU.mult).then_inc(ctx_dve, 1)
                dve.wait_ge(ctx_dve, 8 * l + 6)
                for k in range(KC):
                    a = nc.vector.tensor_scalar(gn[:, k, :], gn[:, k, :], lcol[:, k:k + 1], lcol[:, KC + k:KC + k + 1], ALU.mult, ALU.add)
                a.then_inc(ctx_dve, 1)
                dve.wait_ge(ctx_pe, 5 * l + 4)
                nc.vector.tensor_tensor(ct[:, :, :], chunks(PM, KC, 128), blockmask[:, :].unsqueeze(1).to_broadcast((128, KC, 128)),
                                        ALU.mult).then_inc(ctx_dve, 1)
                dve.wait_ge(d_hi, l + 1)
                nc.vector.tensor_tensor(mmat[1][:, :, :], chunks(PS, KC, D), f32(mmat[0][:, :, :]), ALU.subtract).then_inc(d_lo, 1)
                dve.wait_ge(w_bias, 32 * l + 32)

                def rest(i, live):
                    n0, n1, n2 = (l * GROUPS + (i - d) for d in range(3))

                    def hid_lo(c):
                        dve.wait_ge(b_hhi, 4 * n2 + c + 1)
                        nc.vector.tensor_tensor(hidh[c % 2][1][:, :, :], hid[c % 2][:, :, :], f32(hidh[c % 2][0][:, :, :]),
                                                ALU.subtract).then_inc(b_hlo, 1)
                    if live(1):
                        dve.wait_ge(b_qhi, n1 + 1)
                        nc.vector.tensor_tensor(qT[1][:, :, :], chunks(PQT), f32(qT[0][:, :, :]), ALU.subtract).then_inc(b_qlo, 1)
                    if live(2):
                        hid_lo(0)
                    if live(0):
                        dve.wait_ge(h_lo, h_b(l, i))
                        if live(1):
                            dve.wait_ge(b_lo2, n1)
                        dve.wait_ge(h_T, h_b(l, i) + 1)
                        affine_of(0, h_aff)
                        dve.wait_ge(h_hi, h_b(l, i) + 1)
                        nc.vector.tensor_tensor(hT[1][:, :, :], affine[:, :, :], f32(hT[0][:, :, :]), ALU.subtract).then_inc(h_lo, 1)
                    if live(1):
                        dve.wait_ge(b_M, n1 + 1)
                        add_rows(i - 1, PM[0:P, :].rearrange("p (j d) -> p j d", j=PAIR), b_x1)
                        dve.wait_ge(b_x1, 2 * n1 + 1)
                        add_rows(i - 1, bo_b[:, :].unsqueeze(1).to_broadcast((P, PAIR, D)), b_x1)
                    if live(2):
                        hid_lo(1)
                    if live(1):
                        added = counted(dve, 2 * n1 + 2)
                        dve.wait_ge(x_loaded, 16)
                        dve.wait_ge(b_x1, added)
                        ln_moments(tile_rows(res, i - 1), ln_st, ln_mv, ln_b(l, i - 1))
                    heads = "p j (h d) -> p (j h) d"
                    if live(0):
                        dve.wait_ge(b_Q, n0 + 1)
                        q3 = PQ[0:P, :].rearrange("p (h d) -> p h d", d=DH)
                        nc.vector.tensor_reduce(qstat[:, 0, :], q3, AX, ALU.max).then_inc(b_soft, 1)
                        dve.wait_ge(b_soft, 5 * n0 + 1)
                        nc.vector.tensor_tensor(qd[:, :, :].rearrange(heads, d=DH), q3,
                                                qstat[:, 0, :].unsqueeze(2).to_broadcast((P, PAIR * HEADS, DH)),
                                                ALU.subtract).then_inc(b_soft, 1)
                    if live(1):
                        ln_finish(lnst[:, bass.ds((i - 1) * PAIR, PAIR), :], ln_exp, ln_step, ln_stats, ln_b(l, i - 1))
                    if live(2):
                        hid_lo(2)
                    if live(0):
                        dve.wait_ge(b_qe, n0 + 1)
                        nc.vector.tensor_reduce(qstat[:, 1, :], qd[:, :, :].rearrange(heads, d=DH), AX, ALU.add).then_inc(b_soft, 1)
                        dve.wait_ge(b_soft, 5 * n0 + 3)
                        nc.vector.reciprocal(qstat[:, 2, :], qstat[:, 1, :]).then_inc(b_soft, 1)
                        dve.wait_ge(b_soft, 5 * n0 + 4)
                        nc.vector.tensor_tensor(qn[:, :, :].rearrange(heads, d=DH), qd[:, :, :].rearrange(heads, d=DH),
                                                qstat[:, 2, :].unsqueeze(2).to_broadcast((P, PAIR * HEADS, DH)),
                                                ALU.mult).then_inc(b_soft, 1)
                    if live(2):
                        hid_lo(3)
                    if live(1):
                        dve.wait_ge(h_lo, h_b(l, i) + 1) if live(0) else dve.wait_ge(b_lo2, n1)
                        dve.wait_ge(b_T2, n1 + 1)
                        affine_of(2 * KC, b_aff2)
                        dve.wait_ge(b_hi2, n1 + 1)
                        nc.vector.tensor_tensor(h2T[1][:, :, :], affine[:, :, :], f32(h2T[0][:, :, :]), ALU.subtract).then_inc(b_lo2, 1)
                    if live(2):
                        dve.wait_ge(b_Y, n2 + 1)
                        add_rows(i - 2, PY[0:P, :].rearrange("p (j d) -> p j d", j=PAIR), b_x2)
                        dve.wait_ge(b_x2, 2 * n2 + 1)
                        add_rows(i - 2, b2_b[:, :].unsqueeze(1).to_broadcast((P, PAIR, D)), b_x2)
                pipeline(dve, 2, rest)

            dve.wait_ge(b_x2, 2 * LAYERS * GROUPS)
            nc.vector.memset(agg[:, :, :], 0.0).then_inc(s_ones, 1)
            for i in range(2):
                nc.vector.memset(f32(ehl[i][:, :, EA:EA + 2]), 1.0).then_inc(s_ones, 1)
            dve.wait_ge(gw_hi, 3)
            nc.vector.tensor_tensor(g1[1][:, 0:2, :], raw_g1[:, 0:2, :], f32(g1[0][:, 0:2, :]), ALU.subtract).then_inc(gw_lo, 1)
            nc.vector.tensor_tensor(g1[1][0:EA, 2, :], raw_g1[0:EA, 2, :], f32(g1[0][0:EA, 2, :]), ALU.subtract).then_inc(gw_lo, 1)
            nc.vector.tensor_tensor(g2[1][:, :, :], raw_g2[:, :, :], f32(g2[0][:, :, :]), ALU.subtract).then_inc(gw_lo, 1)
            dve.wait_ge(gcol_pe, 1)
            nc.vector.tensor_tensor(g1col[:, :], PS[:, 0:2 * GHC:2], cols[:, NROW - 1 - GHC:NROW - 1], ALU.add).then_inc(gcol_ready, 1)
            dve.wait_ge(s_ones, 3)

            def seg_add(n, par):
                tile = dve.value_load(ekind_i[0:1, bass.ds(n, 1)], min_val=0, max_val=TILES - 1)
                o = agg[:, bass.ds(tile, 1), :].rearrange("p a c -> p (a c)")
                ps = [PS, PM][par][0:P, 0:2 * EA + 2]
                dve.wait_ge(s_pe, n + 1)
                dve.wait_ge(s_add2, n)
                nc.vector.tensor_tensor(o, o, ps[:, 0:EA + 1], ALU.add).then_inc(s_add, 1)
                dve.wait_ge(s_add, n + 1)
                nc.vector.tensor_tensor(o[:, 0:EA], o[:, 0:EA], ps[:, EA + 2:2 * EA + 2], ALU.add).then_inc(s_add2, 1)

            def seg_prep(n, slot, turn):
                par = slot % 2
                dve.wait_ge(S_IN[slot], 16 * turn + 16)
                nc.vector.tensor_scalar(kb[:, par, :], rows_in[slot][:, :, EA], ekind[:, bass.ds(n, 1)], None,
                                        ALU.subtract).then_inc(s_kb, 1)
                dve.wait_ge(s_kb, n + 1)
                if not (isinstance(n, int) and n < 2):
                    dve.wait_ge(s_pe, n - 1)
                for j in range(SEGR):
                    a = nc.vector.tensor_scalar(oh[par][:, j, :], iota_node[:, :], kb[:, par, j:j + 1], None, ALU.is_equal)
                a.then_inc(s_oh, 1)
                dve.wait_ge(s_hi, n + 1)
                nc.vector.tensor_tensor(ehl[par][:, :, EA + 2:2 * EA + 2], rows_in[slot][:, :, 0:EA],
                                        f32(ehl[par][:, :, 0:EA]), ALU.subtract).then_inc(s_lo, 1)
            for n in range(4):
                seg_prep(n, n, 0)
                if n > 0:
                    seg_add(n - 1, (n - 1) % 2)
            with dve.Fori(1, ESEGS // 4) as q:
                for slot in range(4):
                    seg_prep(4 * q + slot, slot, q)
                    seg_add(4 * q + (slot - 1), (slot - 1) % 2)
            seg_prep(ESEGS - 1, 0, ESEGS // 4)
            seg_add(ESEGS - 2, 1)
            seg_add(ESEGS - 1, 0)
            dve.wait_ge(s_add2, ESEGS)

            def graph(i, live):
                if live(0):
                    par = i % 2
                    need = [counted(dve, 16 * ((i + 2 - slot) // 2)) for slot in range(2)]
                    dve.wait_ge(x_loaded, 16)
                    for slot in range(2):
                        if not (isinstance(need[slot], int) and need[slot] == 0):
                            dve.wait_ge(N_IN[slot], need[slot])
                    ln_moments([x_in[:, bass.ds(par, 1), j, :].rearrange("p a d -> p (a d)") for j in range(PAIR)], n_st, n_mv, i)
                    sums = pair(agg, i, ROW)
                    dve.wait_ge(n_T, i)
                    nc.vector.tensor_scalar(crec[:, 0, :, :], sums[:, :, EA:ROW], 1.0, None, ALU.max).then_inc(n_an, 1)
                    dve.wait_ge(n_an, 3 * i + 1)
                    nc.vector.reciprocal(crec[:, 1, :, :], crec[:, 0, :, :]).then_inc(n_an, 1)
                    dve.wait_ge(n_an, 3 * i + 2)
                    nc.vector.tensor_tensor(an[:, :, :], sums[:, :, 0:EA], crec[:, 1, :, :].to_broadcast((P, PAIR, EA)), ALU.mult).then_inc(n_an, 1)
                    ln_finish(gst[:, :, :], n_r0, n_nw, n_stats, i)
                if live(1):
                    for c in range(2):
                        dve.wait_ge(n_hhi, 2 * (i - 1) + c + 1)
                        nc.vector.tensor_tensor(ghh[c][1][:, :, :], ghid[c][:, :, :], f32(ghh[c][0][:, :, :]), ALU.subtract).then_inc(n_hlo, 1)
                if live(0):
                    dve.wait_ge(n_hi, 2 * i + 2)
                    nc.vector.tensor_tensor(cT[1][:, 0:2, :], chunks(PT), f32(cT[0][:, 0:2, :]), ALU.subtract).then_inc(n_lo, 1)
                    nc.vector.tensor_tensor(cT[1][0:EA, 2, :], PS[0:EA, 0:GT], f32(cT[0][0:EA, 2, :]), ALU.subtract).then_inc(n_lo, 1)
                if live(1):
                    g = i - 1
                    dve.wait_ge(n_Y, g + 1)
                    add_rows(g, PY[0:P, :].rearrange("p (j d) -> p j d", j=PAIR), n_y)
                    dve.wait_ge(n_y, 3 * g + 1)
                    add_rows(g, x_in[:, bass.ds(g % 2, 1), :, :].rearrange("p a j d -> p (a j) d"), n_y)
                    dve.wait_ge(n_y, 3 * g + 2)
                    add_rows(g, gb2_b[:, :].unsqueeze(1).to_broadcast((P, PAIR, D)), n_y)
                    added = counted(dve, 3 * g + 3)
                    dve.wait_ge(x_loaded, 16)
                    dve.wait_ge(n_y, added)
                    ln_moments(tile_rows(res, g), o_st, o_mv, g)
                if live(2):
                    g = i - 2
                    dve.wait_ge(n_log, g + 1)
                    nc.vector.tensor_tensor(logit[:, :, :], PM[0:P, 0:PAIR * EXP].rearrange("p (j e) -> p j e", j=PAIR),
                                            rb_b[:, :].unsqueeze(1).to_broadcast((P, PAIR, EXP)), ALU.add).then_inc(n_top, 1)
                    biased, found = counted(dve, 6 * g + 1), counted(dve, 6 * g + 3)
                    dve.wait_ge(rw_raw, 32)
                    dve.wait_ge(n_top, biased)
                    for j in range(PAIR):
                        nc.vector.max(best[:, j, :], logit[:, j, :]).then_inc(n_top, 1)
                    dve.wait_ge(rw_raw, 32)
                    dve.wait_ge(n_top, found)
                    for j in range(PAIR):
                        nc.vector.max_index(besti[:, j, :], best[:, j, :], logit[:, j, :]).then_inc(n_top, 1)
                    dve.wait_ge(n_top, 6 * g + 5)
                    nc.vector.tensor_copy(res[:, bass.ds(g * PAIR, PAIR), D + 3], besti[:, :, 0]).then_inc(n_top, 1)
                if live(1):
                    ln_finish(res[:, bass.ds((i - 1) * PAIR, PAIR), D:D + 2], o_r0, o_nw, o_stats, i - 1)
            pipeline(dve, 2, graph)

            dve.wait_ge(n_top, 6 * GROUPS)
            nc.vector.tensor_copy(fexp[:, :], res[:, :, D + 3]).then_inc(e_conv, 1)
            dve.wait_ge(e_conv, 6)
            count_sort(fexp[:, :], TILES, EXP, P, [t[:, :] for t in fscr], fpos[:, :], fpos_i[:, :], FSEGS,
                       fkind, fkind_i, ffirst_i, 1)
            nc.vector.memset(hsT[EH:EH + 1, :], 1.0).then_inc(f_bias, 1)

            def expert(n, slot, turn):
                y = yin[slot]
                dve.wait_ge(f_T, n + 1)
                nc.vector.tensor_copy(zsT[:, :, :], chunks(PT, KC, P)).then_inc(f_zT, 1)
                dve.wait_ge(f_idx, 2 * n)
                dve.wait_ge(F_IN[slot], 16 * turn + 16)
                nc.vector.tensor_scalar(omiss[:, :], y[:, D + 3:D + 4], fkind[0:P, bass.ds(n, 1)], float(4 * N),
                                        ALU.not_equal, ALU.mult).then_inc(f_idx, 1)
                dve.wait_ge(f_idx, 2 * n + 1)
                dve.wait_ge(F_OUT[slot], 16 * turn)
                nc.vector.tensor_tensor(oidx[slot][:, :], omiss[:, :], y[:, D + 2:D + 3], ALU.add).then_inc(f_idx, 1)
                dve.wait_ge(f_o, n + 1)
                nc.vector.scalar_tensor_tensor(out=orow[slot][:, :], in0=PY[0:P, 0:D], scalar=0.0, in1=y[:, 0:D],
                                               op0=ALU.max, op1=ALU.add).then_inc(f_row, 1)
            with dve.Fori(0, FSEGS // 3) as q:
                for slot in range(3):
                    expert(3 * q + slot, slot, q)

        @block.tensor
        def _(pe):
            def transposes(o, i, n, k=KC):
                for j in range(PAIR):
                    for c in range(k):
                        a = nc.tensor.transpose(o[0:128, c, j * n:(j + 1) * n], i[:, j, c * 128:(c + 1) * 128], ident[0:n, 0:n])
                return a

            pe.wait_ge(consts, NCONST)
            pe.wait_ge(rows_loaded, 7 * 16)
            nc.tensor.transpose(PS[:, 0:NROW], colrows[:, :], ident[0:NROW, 0:NROW]).then_inc(cols_T, 1)

            def count_sort(nk, segs, turn):
                pe.wait_ge(r_cnt, TILES if turn == 0 else TILES + nk)
                pe.wait_ge(cols_ready, 1)
                mm(PS[0:P, 0:nk], tri[0:P, 0:P], cnt[:, 0:nk], True, True)
                mm(PS[0:P, 64:64 + nk], ones[0:P, 0:P], cnt[:, 0:nk], True, True)
                mm(PS[0:nk, 128:130], cnt[:, 0:nk], ones[0:P, 0:2], True, True).then_inc(sort_pe, 1)
                pe.wait_ge(sort_dve, SORT_DVE * turn + 5)
                mm(PS[0:nk, 130:131], tri[0:nk, 0:nk], kcol[0:nk, 0:1], True, True).then_inc(sort_pe, 1)
                pe.wait_ge(sort_dve, SORT_DVE * turn + 10)
                pe.wait_ge(sort_dve, SORT_DVE * turn + 4)
                mm(PS[:, 0:segs], ones[0:nk, :], cmp[0:nk, 0:segs], True, True).then_inc(sort_pe, 1)
            count_sort(TILES, ESEGS, 0)

            with pe.Fori(0, LAYERS) as l:
                pe.wait_ge(qk_lo, l + 1)

                def keys(i, live):
                    if live(1):
                        pe.wait_ge(h_xh, h_a(l, i - 1) + 1)
                        pe.wait_ge(h_aff, h_a(l, i - 1))
                        transposes(chunks(PT), xh[0], P).then_inc(h_T, 1)
                    if live(2):
                        n = l * GROUPS + (i - 2)
                        pe.wait_ge(h_lo, h_a(l, i - 2) + 1)
                        pe.wait_ge(a_ks, n)
                        for j in range(PAIR):
                            for k in range(KC):
                                a = mm3(PQ[0:P, j * D:(j + 1) * D], at(hT, slice(None), k, slice(j * P, (j + 1) * P)),
                                        at(wqk, slice(None), k, slice(D, 2 * D)), k == 0, k == KC - 1)
                        a.then_inc(a_K, 1)
                pipeline(pe, 2, keys)

                pe.wait_ge(ctx_dve, 8 * l + 1)
                for k in range(KC):
                    a = nc.tensor.transpose(PT[:, k * P:(k + 1) * P], km[:, k * 128:(k + 1) * 128], ident[0:P, 0:P])
                a.then_inc(ctx_pe, 1)
                pe.wait_ge(ctx_dve, 8 * l + 3)
                pe.wait_ge(sort_dve, 11)
                mm(PS[0:P, 0:D], ones[:, 0:P], dg[:, :, :].rearrange("p k n -> p (k n)"), True, True).then_inc(ctx_pe, 1)

                def weighted(g, slot):
                    n = l * GROUPS + g
                    pe.wait_ge(g_ek, n + 1)
                    pe.wait_ge(g_xh, n + 1)
                    for j in range(PAIR):
                        for k in range(KC):
                            a = mm(PQT[:, k * D:(k + 1) * D], xh[slot][:, j, k * 128:(k + 1) * 128], ek[:, slot, j, :],
                                   isinstance(g, int) and g == 0 and j == 0 and k == 0, False)
                    a.then_inc(g_pe, 1)
                weighted(0, 0)
                with pe.Fori(0, GROUPS // 2) as q:
                    weighted(2 * q + 1, 1)
                    weighted(2 * q + 2, 0)

                pe.wait_ge(g_esum, (l + 1) * GROUPS)
                for j in range(PAIR):
                    a = mm(PS[:, 0:D], ones[0:P, :], esum[:, j, :], j == 0, j == PAIR - 1)
                a.then_inc(ctx_pe, 1)
                pe.wait_ge(ctx_dve, 8 * l + 7)
                pe.wait_ge(w_vo, 32 * l + 32)
                for h in range(KC):
                    for k in range(KC):
                        a = mm(PM[:, h * 128:(h + 1) * 128], raw_vo[:, 0, k, h * 128:(h + 1) * 128],
                               gn[:, k, h * 128:(h + 1) * 128], k == 0, k == KC - 1)
                a.then_inc(ctx_pe, 1)
                pe.wait_ge(ctx_dve, 8 * l + 8)
                for h in range(KC):
                    a = mm(PS[:, h * D:(h + 1) * D], ct[:, h, :], raw_vo[:, 1, h, :], True, True)
                a.then_inc(ctx_pe, 1)
                pe.wait_ge(d_lo, l + 1)
                pe.wait_ge(w1_lo, l + 1)
                pe.wait_ge(w2_lo, l + 1)

                def rest(i, live):
                    n0, n1, n2 = (l * GROUPS + (i - d) for d in range(3))

                    def up(c):
                        for m in range(2):
                            for k in range(KC):
                                a = mm3(chunks(PH[c % 2])[:, m, :], at(w1, slice(None), k, slice((2 * c + m) * 128, (2 * c + m + 1) * 128)),
                                        at(h2T, slice(None), k, slice(None)), k == 0, k == KC - 1)
                        a.then_inc(b_H, 1)

                    def down(c):
                        pe.wait_ge(b_hlo, 4 * n2 + c + 1)
                        for m in range(2):
                            for j in range(PAIR):
                                a = mm3(PY[0:P, j * D:(j + 1) * D], at(hidh[c % 2], slice(None), m, slice(j * P, (j + 1) * P)),
                                        at(w2, slice(None), 2 * c + m, slice(None)), c == 0 and m == 0 and j == 0, False)
                        if c == 3:
                            a.then_inc(b_Y, 1)
                    if live(1):
                        pe.wait_ge(b_soft, 5 * n1 + 5)
                        transposes(chunks(PQT), qn, P).then_inc(b_qT, 1)
                    if live(2):
                        pe.wait_ge(b_lo2, n2 + 1)
                        up(0)
                    if live(0):
                        pe.wait_ge(h_xh, h_b(l, i) + 1)
                        transposes(chunks(PT), xh[0], P).then_inc(h_T, 1)
                    if live(1):
                        pe.wait_ge(b_qlo, n1 + 1)
                        pe.wait_ge(b_x1, 2 * n1)
                        for j in range(PAIR):
                            for k in range(KC):
                                a = mm3(PM[0:P, j * D:(j + 1) * D], at(qT, slice(None), k, slice(j * P, (j + 1) * P)),
                                        at(mmat, slice(None), k, slice(None)), k == 0, k == KC - 1)
                        a.then_inc(b_M, 1)
                    if live(2):
                        up(1)
                        pe.wait_ge(b_x2, 2 * n2)
                        down(0)
                    if live(0):
                        pe.wait_ge(h_lo, h_b(l, i) + 1)
                        for j in range(PAIR):
                            for k in range(KC):
                                a = mm3(PQ[0:P, j * D:(j + 1) * D], at(hT, slice(None), k, slice(j * P, (j + 1) * P)),
                                        at(wqk, slice(None), k, slice(0, D)), k == 0, k == KC - 1)
                        a.then_inc(b_Q, 1)
                    if live(2):
                        up(2)
                        down(1)
                        up(3)
                        down(2)
                    if live(1):
                        pe.wait_ge(b_xh2, n1 + 1)
                        transposes(chunks(PT), xh[1], P).then_inc(b_T2, 1)
                    if live(2):
                        down(3)
                pipeline(pe, 2, rest)

            pe.wait_ge(gw_raw, 80)
            for c in range(GHC):
                a = mm(PS[:, 2 * c:2 * c + 1], raw_gu[:, c * 128:(c + 1) * 128], cols[:, NROW - 1:NROW], True, True)
            a.then_inc(gcol_pe, 1)
            pe.wait_ge(rw_raw, 32)
            for k in range(KC):
                a = nc.tensor.transpose(PT[:, k * EXP:(k + 1) * EXP], rw_in[:, k * 128:(k + 1) * 128], ident[0:EXP, 0:EXP])
            a.then_inc(rw_T, 1)

            pe.wait_ge(gcol_ready, 1)
            pe.wait_ge(s_ones, 3)

            def segment(n, par):
                pe.wait_ge(s_oh, n + 1)
                pe.wait_ge(s_lo, n + 1)
                if not (isinstance(n, int) and n < 2):
                    pe.wait_ge(s_add2, n - 1)
                for j in range(SEGR):
                    a = mm([PS, PM][par][0:P, 0:2 * EA + 2], oh[par][:, j, :], ehl[par][:, j, :], j == 0, j == SEGR - 1)
                a.then_inc(s_pe, 1)
            for n in range(4):
                segment(n, n % 2)
            with pe.Fori(1, ESEGS // 4) as q:
                for slot in range(4):
                    segment(4 * q + slot, slot % 2)
            segment(ESEGS - 1, 0)
            pe.wait_ge(gw_lo, 3)
            pe.wait_ge(s_add2, ESEGS)
            pe.wait_ge(rw_ready, 1)

            def graph(i, live):
                if live(0):
                    pe.wait_ge(n_xn, i + 1)
                    pe.wait_ge(n_an, 3 * i + 3)
                    pe.wait_ge(n_lo, 2 * i)
                    transposes(chunks(PT), xn, P)
                    for j in range(PAIR):
                        a = nc.tensor.transpose(PS[0:EA, j * P:(j + 1) * P], an[:, j, :], ident[0:P, 0:P])
                    a.then_inc(n_T, 1)
                if live(1):
                    g = i - 1
                    pe.wait_ge(n_lo, 2 * g + 2)
                    for c in range(2):
                        for m in range(2):
                            hc = slice((2 * c + m) * 128, (2 * c + m + 1) * 128)
                            for k in range(3):
                                rows = slice(0, 128 if k < 2 else EA)
                                a = mm3(chunks(PH[c])[:, m, :], at(g1, rows, k, hc), at(cT, rows, k, slice(None)), k == 0, k == 2)
                        a.then_inc(n_H, 1)
                    pe.wait_ge(n_y, 3 * g)
                    for c in range(2):
                        pe.wait_ge(n_hlo, 2 * g + c + 1)
                        for m in range(2):
                            for j in range(PAIR):
                                a = mm3(PY[0:P, j * D:(j + 1) * D], at(ghh[c], slice(None), m, slice(j * P, (j + 1) * P)),
                                        at(g2, slice(None), 2 * c + m, slice(None)), c == 0 and m == 0 and j == 0, False)
                    a.then_inc(n_Y, 1)
                if live(2):
                    g = i - 2
                    pe.wait_ge(n_z, g + 1)
                    pe.wait_ge(n_log, g)
                    transposes(chunks(PQ), zt, P).then_inc(n_zT, 1)
                    pe.wait_ge(n_zTs, g + 1)
                    pe.wait_ge(n_top, 6 * g)
                    for j in range(PAIR):
                        for k in range(KC):
                            a = mm(PM[0:P, j * EXP:(j + 1) * EXP], zT[:, k, j * P:(j + 1) * P], rwT[:, k, :], k == 0, k == KC - 1)
                    a.then_inc(n_log, 1)
            pipeline(pe, 2, graph)

            count_sort(EXP, FSEGS, 1)
            pe.wait_ge(f_w, 16 * 5)
            pe.wait_ge(f_bias, 1)

            def expert(n, slot):
                e = pe.value_load(fkind_i[0:1, bass.ds(n, 1)], min_val=0, max_val=EXP - 1)
                pe.wait_ge(f_z, n + 1)
                pe.wait_ge(f_zT, n)
                for k in range(KC):
                    a = nc.tensor.transpose(PT[:, k * P:(k + 1) * P], zs[:, k * 128:(k + 1) * 128], ident[0:P, 0:P])
                a.then_inc(f_T, 1)
                pe.wait_ge(f_zT, n + 1)
                mm(PM[0:P, 0:EH], ones[0:1, 0:P], fb1_r[0:1, bass.ds(e * EH, EH)], True, False)
                for k in range(KC):
                    a = mm(PM[0:P, 0:EH], zsT[:, k, :], fw1[:, k, bass.ds(e * EH, EH)], False, k == KC - 1)
                a.then_inc(f_h, 1)
                pe.wait_ge(f_bias, 1)
                pe.wait_ge(f_hs, n + 1)
                nc.tensor.transpose(PQT[0:EH, 0:P], hs[:, :], ident[0:P, 0:P]).then_inc(f_hT, 1)
                pe.wait_ge(f_hTs, n + 1)
                pe.wait_ge(f_row, n)
                mm(PY[0:P, 0:D], hsT[:, :], fw2[:, bass.ds(e * D, D)], True, True).then_inc(f_o, 1)
            pe.wait_ge(r_table, 2)
            with pe.Fori(0, FSEGS // 3) as q:
                for slot in range(3):
                    expert(3 * q + slot, slot)
    return nc


INPUTS = ["x", "src", "edge_attr_64", "L0_gnn_u", "L0_gnn_W1", "L0_gnn_b1", "L0_gnn_W2", "L0_gnn_b2", "L0_mix_Wq", "L0_mix_Wk",
          "L0_mix_Wv", "L0_mix_Wo", "L0_mix_bo", "L0_mix_ln1_g", "L0_mix_ln1_b", "L0_mix_W1", "L0_mix_b1", "L0_mix_W2",
          "L0_mix_b2", "L0_mix_ln2_g", "L0_mix_ln2_b", "L0_ffn_router_w", "L0_ffn_router_b", "L0_ffn_W1", "L0_ffn_b1",
          "L0_ffn_W2", "L0_ffn_b2"]


def kernel(**inputs):
    import numpy as np
    import concourse.bacc as bacc
    from concourse.bass_utils import run_bass_kernel_spmd

    nc = bacc.Bacc("TRN2", target_bir_lowering=False, num_devices=1)
    arrays, args = {}, []
    for name in INPUTS:
        a = np.ascontiguousarray(inputs[name])
        arrays[f"in_{name}"] = a
        args.append(nc.dram_tensor(f"in_{name}", a.shape, mybir.dt.from_np(a.dtype), kind="ExternalInput").ap())
    args.append(nc.dram_tensor("nodes_out", (N, D), F32, kind="ExternalOutput").ap())
    build(nc, *args)
    r = run_bass_kernel_spmd(nc, [arrays], core_ids=[0])
    return r.results[0]["nodes_out"]
```

```python
from contextlib import ExitStack

import concourse.bass as bass
from concourse import mybir

F32 = mybir.dt.float32
F32R = mybir.dt.float32r
I32 = mybir.dt.int32
U32 = mybir.dt.uint32
ALU = mybir.AluOpType
ACT = mybir.ActivationFunctionType
AX = mybir.AxisListType.X

P = 125
TILES = 50
D = 256
KC = D // 128
PAIR = 2
GROUPS = TILES // PAIR
GT = PAIR * P
N = P * TILES
LAYERS = 4
HEADS = 8
DH = D // HEADS
FF = 4 * D
FC = FF // 128
EA = 64
EDGES = 106250
ECOL = EDGES // P
ROW = EA + 1
SEG = 512
SEGR = SEG // 128
ETILES = -(-EDGES // SEG)
ESEGS = ETILES + TILES - 1
CH = 17
CHUNKS = ECOL // CH
GH = 512
GHC = GH // 128
GLOB = 128
EXP = 32
EH = 64
YROW = D + 4
FSEGS = TILES + EXP - 1
EPS = 1e-5
LN_STEPS = 17
RSQRT_MAGIC = float(0x5f3759df)
RND = 8388608.0
ROWS_LN = LAYERS * KC
NROW = 4 * ROWS_LN + LAYERS * FC + GHC + 1
NCONST = 9 + 128 // DH
SCALE = DH ** -0.25
SORT_DVE = 13
SPARE = ETILES * SEG - EDGES
SPARE_P = SPARE // 2


def build(nc, x, src, edge_attr, u, gW1, gb1, gW2, gb2, Wq, Wk, Wv, Wo, bo, ln1_g, ln1_b, mW1, mb1, mW2, mb2,
          ln2_g, ln2_b, rw, rb, fW1, fb1, fW2, fb2, out):
    edges_sorted = nc.dram_tensor("edges_sorted", (ETILES * SEG, ROW), F32, kind="Internal").ap()
    tokens_sorted = nc.dram_tensor("tokens_sorted", (N, YROW), F32, kind="Internal").ap()
    x_rows = x.rearrange("(p t) d -> p t d", t=TILES)
    edge_rows = edge_attr.rearrange("(p c) a -> p c a", c=ECOL)

    ctx = ExitStack()
    with ctx:
        def sb(name, shape, dt=F32, where=None):
            return (where or ctx).enter_context(nc.sbuf_tensor(name, shape, dt))

        def both(name, shape, where=None):
            return [sb(f"{name}_{n}", shape, F32R, where) for n in ("hi", "lo")]

        bank = [ctx.enter_context(nc.psum_tensor(f"bank{i}", [128, 512], F32)) for i in range(8)]
        PT, PQ, PQT, PM, PH0, PH1, PY, PS = bank
        PH = [PH0, PH1]

        res = sb("res", [P, TILES, YROW])
        ident = sb("ident", [128, 128])
        ones = sb("ones", [128, 128])
        tri = sb("tri", [128, 128])
        cols = sb("cols", [128, NROW])
        iota_node = sb("iota_node", [128, P])
        iota_seg = sb("iota_seg", [128, ESEGS])
        iota_part = sb("iota_part", [128, 1])
        eps = sb("eps", [128, 1])
        ekind = sb("ekind", [128, ESEGS])
        ekind_i = sb("ekind_i", [1, ESEGS], I32)
        efirst_i = sb("efirst_i", [1, ESEGS], I32)
        segtmp = sb("segtmp", [1, ESEGS])
        bn = sb("bn", [P, TILES, 6])
        lnt = sb("lnt", [P, 10, TILES])
        lnt_i = sb("lnt_i", [P, TILES], I32)
        xst = sb("xst", [P, TILES, 2])
        src_f = sb("src_f", [P, ECOL])
        pos_i = sb("pos_i", [P, ECOL], I32)
        cnt = sb("cnt", [P, TILES])
        tot = sb("tot", [P, TILES])
        totinc = sb("totinc", [P, TILES])
        base = sb("base", [P, TILES])
        kcol = sb("kcol", [TILES, 4])
        cmp = sb("cmp", [TILES, ESEGS])
        stage = sb("stage", [P, 2, CH, ROW])
        idx = sb("idx", [P, 2, CH], I32)

        layers = ExitStack()
        wqk = both("wqk", [128, KC, 2 * D], layers)
        w1 = both("w1", [128, KC, FF], layers)
        w2 = both("w2", [128, FC, D], layers)
        raw_vo = sb("raw_vo", [128, 2, KC, D], F32, layers)
        raw = sb("raw", [128, KC * FF], F32, layers)
        bo_b = sb("bo_b", [128, D], F32, layers)
        b2_b = sb("b2_b", [P, D], F32, layers)
        lcol = sb("lcol", [128, 4 * KC + FC], F32, layers)
        lnst = sb("lnst", [P, TILES, 2], F32, layers)
        xh = [sb(f"xh{i}", [P, PAIR, D], F32, layers) for i in range(2)]
        affine = sb("affine", [128, KC, GT], F32, layers)
        hT = both("hT", [128, KC, GT], layers)
        ek = sb("ek", [P, 2, PAIR, D], F32, layers)
        kmax = sb("kmax", [P, PAIR, D], F32, layers)
        km = sb("km", [P, D], F32, layers)
        mbc = sb("mbc", [P, D], F32, layers)
        esum = sb("esum", [P, PAIR, D], F32, layers)
        mcol = sb("mcol", [128, KC], F32, layers)
        blockmask = sb("blockmask", [128, 128], F32, layers)
        dg = sb("dg", [128, KC, 128], F32, layers)
        k_place = ExitStack()
        ksb = sb("ksb", [P, TILES, D], F32, k_place)
        k_place.close()
        pos_f = stage[:, 0, :, :].rearrange("p c r -> p (c r)")[:, 0:ECOL]
        tile_of = stage[:, 1, :, :].rearrange("p c r -> p (c r)")[:, 0:ECOL]
        k_place = ExitStack()
        scr = [sb(f"scr{i}", [P, ECOL], F32, k_place) for i in range(3)]
        src_i = sb("src_i", [P, ECOL], I32, k_place)
        colrows = sb("colrows", [NROW, 128], F32, k_place)
        k_place.close()
        k_place = ExitStack()
        gn = sb("gn", [128, KC, D], F32, k_place)
        ct = sb("ct", [128, KC, 128], F32, k_place)
        mmat = both("mmat", [128, KC, D], k_place)
        mprod = sb("mprod", [128, KC, D], F32, k_place)
        qd = sb("qd", [P, PAIR, D], F32, k_place)
        qn = sb("qn", [P, PAIR, D], F32, k_place)
        qstat = sb("qstat", [P, 3, PAIR * HEADS], F32, k_place)
        qT = both("qT", [128, KC, GT], k_place)
        hid = [sb(f"hid{i}", [128, 2, GT], F32, k_place) for i in range(2)]
        hidh = [both(f"hidh{i}", [128, 2, GT], k_place) for i in range(2)]
        kmask = [sb(f"kmask{i}", [P, ECOL], F32, k_place) for i in range(2)]
        krank = [sb(f"krank{i}", [P, ECOL], F32, k_place) for i in range(2)]
        k_place.close()
        layers.close()

        gnn = ExitStack()
        agg = sb("agg", [P, TILES, ROW], F32, gnn)
        g1 = both("g1", [128, 3, GH], gnn)
        g2 = both("g2", [128, GHC, D], gnn)
        raw_g1 = sb("raw_g1", [128, 3, GH], F32, gnn)
        raw_g2 = sb("raw_g2", [128, GHC, D], F32, gnn)
        raw_gu = sb("raw_gu", [128, GH], F32, gnn)
        g1col = sb("g1col", [128, GHC], F32, gnn)
        gb2_b = sb("gb2_b", [P, D], F32, gnn)
        rows_in = [sb(f"rows_in{i}", [128, SEGR, ROW], F32, gnn) for i in range(4)]
        kb = sb("kb", [128, 2, SEGR], F32, gnn)
        oh = [sb(f"oh{i}", [128, SEGR, P], F32R, gnn) for i in range(2)]
        ehl = [sb(f"ehl{i}", [128, SEGR, 2 * EA + 2], F32R, gnn) for i in range(2)]
        x_in = sb("x_in", [P, 2, PAIR, D], F32, gnn)
        xn = sb("xn", [P, PAIR, D], F32, gnn)
        an = sb("an", [P, PAIR, EA], F32, gnn)
        crec = sb("crec", [P, 2, PAIR, 1], F32, gnn)
        cT = both("cT", [128, 3, GT], gnn)
        ghid = [sb(f"ghid{i}", [128, 2, GT], F32, gnn) for i in range(2)]
        ghh = [both(f"ghh{i}", [128, 2, GT], gnn) for i in range(2)]
        zt = sb("zt", [P, PAIR, D], F32, gnn)
        zT = sb("zT", [128, KC, GT], F32, gnn)
        rwT = sb("rwT", [128, KC, EXP], F32, gnn)
        rw_in = sb("rw_in", [EXP, D], F32, gnn)
        rb_b = sb("rb_b", [P, EXP], F32, gnn)
        logit = sb("logit", [P, PAIR, EXP], F32, gnn)
        best = sb("best", [P, PAIR, 8], F32, gnn)
        besti = sb("besti", [P, PAIR, 8], U32, gnn)
        gnn.close()
        fw1 = sb("fw1", [128, KC, EXP * EH])
        fw2 = sb("fw2", [EH + 1, EXP * D])
        fb1_r = sb("fb1_r", [1, EXP * EH])
        fscr = [sb(f"fscr{i}", [P, TILES]) for i in range(3)]
        fpos = sb("fpos", [P, TILES])
        fpos_i = sb("fpos_i", [P, TILES], I32)
        fexp = sb("fexp", [P, TILES])
        fkind = sb("fkind", [128, FSEGS])
        fkind_i = sb("fkind_i", [1, FSEGS], I32)
        ffirst_i = sb("ffirst_i", [1, FSEGS], I32)
        yin = [sb(f"yin{i}", [P, YROW]) for i in range(3)]
        zs = sb("zs", [P, D])
        zsT = sb("zsT", [128, KC, P])
        hs = sb("hs", [P, EH])
        hsT = sb("hsT", [EH + 1, P])
        orow = [sb(f"orow{i}", [P, D]) for i in range(3)]
        omiss = sb("omiss", [P, 1])
        oidx = [sb(f"oidx{i}", [P, 1], I32) for i in range(3)]

        def sems(names):
            return [ctx.enter_context(nc.semaphore(n)) for n in names.split()]

        src_loaded, x_loaded, rows_loaded, w_qk, w_vo, w_1, w_2 = sems("src_loaded x_loaded rows_loaded w_qk w_vo w_1 w_2")
        w_bias, gw_raw, rw_raw, f_w, attr0, attr1 = sems("w_bias gw_raw rw_raw f_w attr0 attr1")
        consts, cols_T, cols_ready, lcol_ready, e_conv = sems("consts cols_T cols_ready lcol_ready e_conv")
        r_zero, r_cnt, r_m, r_scan, r_mul, r_acc, sort_pe = sems("r_zero r_cnt r_m r_scan r_mul r_acc sort_pe")
        e_mask, e_rank, e_mul, e_acc = sems("e_mask e_rank e_mul e_acc")
        sort_dve, r_table, pos_ready, f_posi = sems("sort_dve r_table pos_ready f_posi")
        key_staged, scattered0, scattered1, spare_rows, spare_written = sems("key_staged scattered0 scattered1 spare_rows spare_written")
        ln_st, ln_step, ln_stats = sems("ln_st ln_step ln_stats")
        qk_hi, qk_lo, w1_hi, w1_lo, w2_hi, w2_lo, gw_hi = sems("qk_hi qk_lo w1_hi w1_lo w2_hi w2_lo gw_hi")
        gw_lo, = sems("gw_lo")
        xs_norm, h_xh, h_T, h_aff, h_hi, h_lo = sems("xs_norm h_xh h_T h_aff h_hi h_lo")
        a_K, a_ks, a_max, c_mbc = sems("a_K a_ks a_max c_mbc")
        g_dk, g_ek, g_xh, g_esum, g_pe = sems("g_dk g_ek g_xh g_esum g_pe")
        ctx_pe, ctx_dve, d_hi, d_lo = sems("ctx_pe ctx_dve d_hi d_lo")
        b_Q, b_soft, b_qe, b_qT, b_qhi, b_qlo, b_M = sems("b_Q b_soft b_qe b_qT b_qhi b_qlo b_M")
        b_x1, = sems("b_x1")
        b_H, b_gelu, b_hhi, b_hlo, b_Y, b_x2 = sems("b_H b_gelu b_hhi b_hlo b_Y b_x2")
        s_in0, s_in1, s_in2, s_in3, s_kb, s_oh, s_hi = sems("s_in0 s_in1 s_in2 s_in3 s_kb s_oh s_hi")
        s_lo, s_pe, s_add, s_add2, s_ones = sems("s_lo s_pe s_add s_add2 s_ones")
        gcol_pe, gcol_ready, n_in0, n_in1, n_xn, n_an, n_T = sems("gcol_pe gcol_ready n_in0 n_in1 n_xn n_an n_T")
        n_hi, n_lo, n_H, n_relu, n_hhi, n_hlo, n_Y, n_y = sems("n_hi n_lo n_H n_relu n_hhi n_hlo n_Y n_y")
        n_z, n_zT, n_zTs, n_log, n_top, rw_T, rw_ready = sems("n_z n_zT n_zTs n_log n_top rw_T rw_ready")
        f_bias, f_ones, f_scat, f_in0, f_in1, f_in2, f_z = sems("f_bias f_ones f_scat f_in0 f_in1 f_in2 f_z")
        f_T, f_zT, f_h, f_hs, f_hT, f_hTs, f_o = sems("f_T f_zT f_h f_hs f_hT f_hTs f_o")
        f_row, f_idx, f_out0, f_out1, f_out2 = sems("f_row f_idx f_out0 f_out1 f_out2")
        ATTR, SCATTERED, S_IN = [attr0, attr1], [scattered0, scattered1], [s_in0, s_in1, s_in2, s_in3]
        N_IN, F_IN, F_OUT = [n_in0, n_in1], [f_in0, f_in1, f_in2], [f_out0, f_out1, f_out2]

        def mm(o, left, right, start, stop):
            return nc.tensor.matmul(o, left, right, start=start, stop=stop, skip_group_check=True)

        def mm3(o, left, right, start, stop):
            (lh, ll), (rh, rl) = left, right
            mm(o, lh, rh, start, False)
            mm(o, lh, rl, False, False)
            return mm(o, ll, rh, False, stop)

        def counted(eng, value):
            if isinstance(value, int):
                return value
            register = eng.alloc_register()
            eng.reg_mov(register, value)
            return register

        def at(halves, *where):
            return [h[where] for h in halves]

        def pipeline(eng, depth, body):
            for i in range(depth):
                body(i, lambda d, i=i: d <= i)
            with eng.Fori(depth, GROUPS) as i:
                body(i, lambda d: True)
            for i in range(GROUPS, GROUPS + depth):
                body(i, lambda d, i=i: i - d < GROUPS)

        LN_LAST = 1 + 2 * LAYERS + 1

        def h_keys(l, g):
            return l * (3 * GROUPS) + g

        def h_attn(l, g):
            return l * (3 * GROUPS) + (g + GROUPS)

        def h_mlp(l, g):
            return l * (3 * GROUPS) + (g + 2 * GROUPS)

        def chunks(b, k=KC, n=GT):
            return b[:, 0:k * n].rearrange("p (k n) -> p k n", k=k)

        def pair(t, g, n=D):
            return t[:, bass.ds(g * PAIR, PAIR), 0:n]

        def f32(ap):
            return ap.bitcast(F32)

        block = ctx.enter_context(nc.Block())

        @block.sync
        def _(sp):
            sp.dma_start(src_i[:, :], src.rearrange("(p c) -> p c", c=ECOL)).then_inc(src_loaded, 16)
            r = 0
            for a, n in ((ln1_g, ROWS_LN), (ln1_b, ROWS_LN), (ln2_g, ROWS_LN), (ln2_b, ROWS_LN), (mb1, LAYERS * FC)):
                sp.dma_start(colrows[r:r + n, :], a.rearrange("l (c f) -> (l c) f", f=128)).then_inc(rows_loaded, 16)
                r += n
            sp.dma_start(colrows[r:r + GHC, :], gb1.rearrange("(c f) -> c f", f=128)).then_inc(rows_loaded, 16)
            sp.dma_start(colrows[r + GHC:r + GHC + 1, :], u[0:1, :]).then_inc(rows_loaded, 16)
            sp.dma_start(res[:, :, 0:D], x_rows).then_inc(x_loaded, 16)

            def weights(w, l, n):
                return w[bass.ds(l, 1), :, :].rearrange("l (k p) n -> p (l k) n", p=128)

            with sp.Fori(0, LAYERS) as l:
                sp.wait_ge(w2_hi, l)
                sp.wait_ge(w2_lo, l)
                raw_qk = raw[:, 0:KC * 2 * D].rearrange("p (k n) -> p k n", k=KC)
                sp.dma_start(raw_qk[:, :, 0:D], weights(Wq, l, D)).then_inc(w_qk, 16)
                sp.dma_start(raw_qk[:, :, D:2 * D], weights(Wk, l, D)).then_inc(w_qk, 16)
                sp.wait_ge(ctx_pe, 5 * l)
                sp.dma_start(raw_vo[:, 0, :, :], weights(Wv, l, D)).then_inc(w_vo, 16)
                sp.dma_start(raw_vo[:, 1, :, :], weights(Wo, l, D)).then_inc(w_vo, 16)
                sp.wait_ge(qk_hi, l + 1)
                sp.wait_ge(qk_lo, l + 1)
                sp.dma_start(raw[:, :].rearrange("p (k n) -> p k n", k=KC), weights(mW1, l, FF)).then_inc(w_1, 16)
                sp.wait_ge(b_x2, l * (2 * GROUPS))
                sp.dma_start(bo_b[:, :], bo[bass.ds(l, 1), :].to_broadcast((128, D))).then_inc(w_bias, 16)
                sp.dma_start(b2_b[:, :], mb2[bass.ds(l, 1), :].to_broadcast((P, D))).then_inc(w_bias, 16)
                sp.wait_ge(w1_hi, l + 1)
                sp.wait_ge(w1_lo, l + 1)
                sp.dma_start(raw[:, :].rearrange("p (k n) -> p k n", k=FC), weights(mW2, l, D)).then_inc(w_2, 16)

            sp.wait_ge(b_x2, 2 * LAYERS * GROUPS)
            sp.wait_ge(ln_stats, LN_LAST)
            sp.dma_start(raw_g1[:, 0:2, :], gW1[0:D, :].rearrange("(k p) n -> p k n", p=128)).then_inc(gw_raw, 16)
            sp.dma_start(raw_g1[0:EA, 2, :], gW1[D:D + EA, :]).then_inc(gw_raw, 16)
            sp.dma_start(raw_gu[:, :], gW1[D + EA:D + EA + GLOB, :]).then_inc(gw_raw, 16)
            sp.dma_start(raw_g2[:, :, :], gW2.rearrange("(k p) n -> p k n", p=128)).then_inc(gw_raw, 16)
            sp.dma_start(gb2_b[:, :], gb2.rearrange("(a n) -> a n", a=1).to_broadcast((P, D))).then_inc(gw_raw, 16)
            sp.dma_start(rw_in[:, :], rw).then_inc(rw_raw, 16)
            sp.dma_start(rb_b[:, :], rb.rearrange("(a n) -> a n", a=1).to_broadcast((P, EXP))).then_inc(rw_raw, 16)

            sp.wait_ge(r_table, 1)
            for slot in range(2):
                sp.wait_ge(SCATTERED[slot], 16 * CH * (CHUNKS // 2))
            sp.wait_ge(spare_written, 16)

            def load_segment(n, slot):
                first = sp.value_load(efirst_i[0:1, bass.ds(n, 1)], min_val=0, max_val=(ETILES - 1) * SEG)
                if not (isinstance(n, int) and n < 4):
                    sp.wait_ge(s_lo, n - 3)
                    sp.wait_ge(s_kb, n - 3)
                sp.dma_start(rows_in[slot][:, :, :],
                             edges_sorted[bass.ds(first, SEG), :].rearrange("(p r) c -> p r c", r=SEGR)).then_inc(S_IN[slot], 16)

            for n in range(4):
                load_segment(n, n)
            with sp.Fori(1, ESEGS // 4) as q:
                for slot in range(4):
                    load_segment(4 * q + slot, slot)
            load_segment(ESEGS - 1, 0)

            def load_x(g, slot):
                sp.dma_start(x_in[:, slot, :, :], x_rows[:, bass.ds(g * PAIR, PAIR), :]).then_inc(N_IN[slot], 16)
            load_x(0, 0)
            load_x(1, 1)
            with sp.Fori(1, GROUPS // 2) as q:
                for slot in range(2):
                    sp.wait_ge(n_y, 3 * (2 * q + (slot - 1)))
                    load_x(2 * q + slot, slot)
            sp.wait_ge(n_y, 3 * (GROUPS - 2))
            load_x(GROUPS - 1, 0)

            sp.wait_ge(n_top, 6 * GROUPS)
            for k in range(KC):
                sp.dma_start(fw1[:, k, :].rearrange("p (e h) -> p e h", h=EH),
                             fW1[:, k * 128:(k + 1) * 128, :].rearrange("e p h -> p e h")).then_inc(f_w, 16)
            sp.dma_start(fw2[0:EH, :].rearrange("p (e h) -> p e h", h=D), fW2.rearrange("e p h -> p e h")).then_inc(f_w, 16)
            sp.dma_start(fb1_r[:, :], fb1.rearrange("(a e) h -> a (e h)", a=1)).then_inc(f_w, 16)
            sp.dma_start(fw2[EH:EH + 1, :], fb2.rearrange("(a e) h -> a (e h)", a=1)).then_inc(f_w, 16)

            sp.wait_ge(f_scat, 16 * TILES)
            sp.wait_ge(r_table, 2)

            def load_tokens(n, slot):
                first = sp.value_load(ffirst_i[0:1, bass.ds(n, 1)], min_val=0, max_val=N - P)
                rows = tokens_sorted[bass.ds(first, P), :]
                if not isinstance(n, int):
                    used, placed = counted(sp, n - 2), counted(sp, 2 * (n - 2))
                    sp.wait_ge(f_row, used)
                    sp.wait_ge(f_idx, placed)
                sp.dma_start(yin[slot][:, :], rows).then_inc(F_IN[slot], 16)
            for n in range(3):
                load_tokens(n, n)
            with sp.Fori(1, FSEGS // 3) as q:
                for slot in range(3):
                    load_tokens(3 * q + slot, slot)

        @block.gpsimd
        def _(pool):
            nc.gpsimd.memset(ones[:, :], 1.0).then_inc(consts, 1)
            nc.gpsimd.memset(eps[:, :], EPS).then_inc(consts, 1)
            nc.gpsimd.memset(blockmask[:, :], 0.0).then_inc(consts, 1)
            nc.gpsimd.memset(stage[:, 0, :, :], 0.0).then_inc(consts, 1)
            pool.wait_ge(consts, 4)
            nc.gpsimd.affine_select(out=ident[:, :], in_=ones[:, :], compare_op=ALU.is_equal, fill=0.0,
                                    base=0, pattern=[[-1, 128]], channel_multiplier=1).then_inc(consts, 1)
            nc.gpsimd.affine_select(out=tri[:, :], in_=ones[:, :], compare_op=ALU.is_gt, fill=0.0,
                                    base=0, pattern=[[1, 128]], channel_multiplier=-1).then_inc(consts, 1)
            pool.wait_ge(consts, 6)
            for h in range(128 // DH):
                nc.gpsimd.memset(blockmask[h * DH:(h + 1) * DH, h * DH:(h + 1) * DH], 1.0).then_inc(consts, 1)
            pool.wait_ge(consts, 6 + 128 // DH)
            for tile, pattern, mult in ((iota_node, [[TILES, P]], 0), (iota_seg, [[1, ESEGS]], 0), (iota_part, [[1, 1]], 1)):
                nc.gpsimd.iota(tile[:, :], pattern=pattern, base=0, channel_multiplier=mult,
                               allow_small_or_imprecise_dtypes=True).then_inc(consts, 1)
            nc.gpsimd.memset(stage[:, 0, :, EA:ROW], -1.0).then_inc(spare_rows, 1)
            pool.wait_ge(spare_rows, 1)
            pool.dma_start(edges_sorted[EDGES:ETILES * SEG, :].rearrange("(p r) c -> p r c", r=SPARE // SPARE_P),
                           stage[0:SPARE_P, 0, 0:SPARE // SPARE_P, :]).then_inc(spare_written, 16)
            pool.wait_ge(spare_written, 16)

            def load_attr(c, slot):
                pool.dma_start(stage[:, slot, :, 0:EA], edge_rows[:, bass.ds(c * CH, CH), :]).then_inc(ATTR[slot], 16)

            def scatter(q, slot):
                c = 2 * q + slot
                nc.gpsimd.tensor_copy(idx[:, slot, :], pos_i[:, bass.ds(c * CH, CH)]).then_inc(key_staged, 1)
                nc.gpsimd.tensor_copy(stage[:, slot, :, EA], src_f[:, bass.ds(c * CH, CH)]).then_inc(key_staged, 1)
                staged, loaded = counted(pool, 2 * c + 2), counted(pool, 16 * q + 16)
                pool.wait_ge(pos_ready, 1)
                pool.wait_ge(key_staged, staged)
                pool.wait_ge(ATTR[slot], loaded)
                for j in range(CH):
                    nc.gpsimd.indirect_dma_start(
                        out=edges_sorted, out_offset=bass.IndirectOffsetOnAxis(ap=idx[:, slot, j:j + 1], axis=0),
                        in_=stage[:, slot, j, :], in_offset=None).then_inc(SCATTERED[slot], 16)

            nc.gpsimd.memset(pos_f, 0.0).then_inc(e_acc, 1)

            def place(b, slot):
                pool.wait_ge(e_rank, b + 1)
                nc.gpsimd.tensor_tensor(krank[slot][:, :], krank[slot][:, :], kmask[slot][:, :], ALU.mult).then_inc(e_mul, 1)
                pool.wait_ge(e_acc, b + 1)
                pool.wait_ge(e_mul, b + 1)
                nc.gpsimd.tensor_tensor(pos_f, pos_f, krank[slot][:, :], ALU.add).then_inc(e_acc, 1)
            with pool.Fori(0, TILES // 2) as q:
                for slot in range(2):
                    place(2 * q + slot, slot)
            pool.wait_ge(pos_ready, 1)
            load_attr(0, 0)
            load_attr(1, 1)
            scatter(0, 0)
            scatter(0, 1)
            with pool.Fori(1, CHUNKS // 2) as q:
                for slot in range(2):
                    pool.wait_ge(SCATTERED[slot], 16 * CH * q)
                    load_attr(2 * q + slot, slot)
                for slot in range(2):
                    scatter(q, slot)

            nc.gpsimd.iota(res[:, :, D + 2], pattern=[[1, TILES]], base=0, channel_multiplier=TILES,
                           allow_small_or_imprecise_dtypes=True).then_inc(f_ones, 1)
            pool.wait_ge(f_ones, 1)
            pool.wait_ge(f_posi, 1)
            for t in range(TILES):
                nc.gpsimd.indirect_dma_start(
                    out=tokens_sorted, out_offset=bass.IndirectOffsetOnAxis(ap=fpos_i[:, t:t + 1], axis=0),
                    in_=res[:, t, :], in_offset=None).then_inc(f_scat, 16)

            def put(n, slot):
                rows, places = counted(pool, n + 1), counted(pool, 2 * n + 2)
                pool.wait_ge(f_scat, 16 * TILES)
                pool.wait_ge(f_row, rows)
                pool.wait_ge(f_idx, places)
                nc.gpsimd.indirect_dma_start(
                    out=out, out_offset=bass.IndirectOffsetOnAxis(ap=oidx[slot][:, :], axis=0),
                    in_=orow[slot][:, :], in_offset=None, bounds_check=N - 1, oob_is_err=False).then_inc(F_OUT[slot], 16)
            with pool.Fori(0, FSEGS // 3) as q:
                for slot in range(3):
                    put(3 * q + slot, slot)
            for slot in range(3):
                pool.wait_ge(F_OUT[slot], 16 * (FSEGS // 3))

        @block.scalar
        def _(act):
            def ident_act(o, i, **kw):
                return nc.scalar.activation(o, i, ACT.Identity, **kw)

            def normalise(o, st, g, done):
                for j in range(PAIR):
                    t = g * PAIR + j
                    a = ident_act(o[:, j, :], res[:, bass.ds(t, 1), 0:D].rearrange("p a d -> p (a d)"),
                                  scale=st[:, bass.ds(t, 1), 0:1].rearrange("p a d -> p (a d)"),
                                  bias=st[:, bass.ds(t, 1), 1:2].rearrange("p a d -> p (a d)"))
                a.then_inc(done, 1)

            def split_hi(o, i, loaded, count, done):
                act.wait_ge(loaded, count)
                nc.scalar.copy(o, i).then_inc(done, 1)

            act.wait_ge(consts, NCONST)
            act.wait_ge(cols_T, 1)
            nc.scalar.copy(cols[:, :], PS[:, 0:NROW]).then_inc(cols_ready, 1)

            act.wait_ge(ln_stats, 1)
            with act.Fori(0, GROUPS) as g:
                for j in range(PAIR):
                    t = g * PAIR + j
                    row = res[:, bass.ds(t, 1), 0:D].rearrange("p a d -> p (a d)")
                    a = ident_act(row, row, scale=xst[:, bass.ds(t, 1), 0:1].rearrange("p a d -> p (a d)"),
                                  bias=xst[:, bass.ds(t, 1), 1:2].rearrange("p a d -> p (a d)"))
                a.then_inc(xs_norm, 1)

            with act.Fori(0, LAYERS) as l:
                act.wait_ge(b_x2, l * (2 * GROUPS))
                split_hi(wqk[0][:, :, :], raw[:, 0:KC * 2 * D].rearrange("p (k n) -> p k n", k=KC), w_qk, 32 * l + 32, qk_hi)

                def affine_of(col, n):
                    act.wait_ge(h_T, n + 1)
                    act.wait_ge(h_lo, n)
                    for k in range(KC):
                        a = ident_act(affine[:, k, :], chunks(PT)[:, k, :], scale=lcol[:, col + k:col + k + 1],
                                      bias=lcol[:, col + KC + k:col + KC + k + 1])
                    a.then_inc(h_aff, 1)

                def h_high(n, read, count):
                    act.wait_ge(h_aff, n + 1)
                    act.wait_ge(read, count)
                    nc.scalar.copy(hT[0][:, :, :], affine[:, :, :]).then_inc(h_hi, 1)

                act.wait_ge(lcol_ready, 4 * l + 4)
                act.wait_ge(ln_stats, 2 * l + 2)

                def keys(i, live):
                    if live(0):
                        act.wait_ge(h_T, h_keys(l, i))
                        normalise(xh[0], lnst, i, h_xh)
                    if live(1):
                        affine_of(0, h_keys(l, i - 1))
                        h_high(h_keys(l, i - 1), a_K, l * GROUPS + (i - 1))
                    if live(2):
                        n = l * GROUPS + (i - 2)
                        act.wait_ge(a_K, n + 1)
                        nc.scalar.copy(pair(ksb, i - 2), PQ[0:P, :].rearrange("p (j d) -> p j d", j=PAIR)).then_inc(a_ks, 1)
                pipeline(act, 2, keys)

                split_hi(w1[0][:, :, :], raw[:, :].rearrange("p (k n) -> p k n", k=KC), w_1, 16 * l + 16, w1_hi)
                act.wait_ge(ctx_pe, 5 * l + 2)
                nc.scalar.copy(mbc[:, :], PS[0:P, 0:D]).then_inc(c_mbc, 1)

                def key_exp(g, slot):
                    n = l * GROUPS + g
                    if not isinstance(g, int):
                        act.wait_ge(g_pe, n - 1)
                    normalise(xh[slot], lnst, g, g_xh)
                    act.wait_ge(g_dk, n + 1)
                    nc.scalar.activation(ek[:, slot, :, :], ek[:, slot, :, :], ACT.Exp, scale=SCALE).then_inc(g_ek, 1)
                key_exp(0, 0)
                with act.Fori(0, GROUPS // 2) as q:
                    key_exp(2 * q + 1, 1)
                    key_exp(2 * q + 2, 0)

                split_hi(w2[0][:, :, :], raw[:, :].rearrange("p (k n) -> p k n", k=FC), w_2, 16 * l + 16, w2_hi)
                act.wait_ge(ctx_dve, 9 * l + 9)
                nc.scalar.copy(mmat[0][:, :, :], mprod[:, :, :]).then_inc(d_hi, 1)

                def attend(i, live):
                    if live(1):
                        affine_of(0, h_attn(l, i - 1))
                        h_high(h_attn(l, i - 1), b_Q, l * GROUPS + (i - 1))
                    if live(3):
                        n = l * GROUPS + (i - 3)
                        act.wait_ge(b_qT, n + 1)
                        act.wait_ge(b_M, n)
                        nc.scalar.copy(qT[0][:, :, :], chunks(PQT)).then_inc(b_qhi, 1)
                    if live(2):
                        act.wait_ge(b_soft, 5 * (l * GROUPS + (i - 2)) + 2)
                        nc.scalar.activation(qd[:, :, :], qd[:, :, :], ACT.Exp, scale=SCALE).then_inc(b_qe, 1)
                    if live(0):
                        act.wait_ge(h_T, h_attn(l, i))
                        normalise(xh[0], lnst, i, h_xh)
                pipeline(act, 4, attend)

                act.wait_ge(ln_stats, 2 * l + 3)

                def mlp(i, live):
                    n2 = l * GROUPS + (i - 2)

                    def gelu(c):
                        act.wait_ge(b_H, 4 * n2 + c + 1)
                        for j in range(2):
                            a = nc.scalar.activation(hid[c % 2][:, j, :], chunks(PH[c % 2])[:, j, :], ACT.Gelu,
                                                     bias=lcol[:, 4 * KC + 2 * c + j:4 * KC + 2 * c + j + 1])
                        a.then_inc(b_gelu, 1)
                        act.wait_ge(b_gelu, 4 * n2 + c + 1)
                        nc.scalar.copy(hidh[c % 2][0][:, :, :], hid[c % 2][:, :, :]).then_inc(b_hhi, 1)
                    if live(2):
                        gelu(0)
                        gelu(1)
                    if live(1):
                        affine_of(2 * KC, h_mlp(l, i - 1))
                    if live(2):
                        gelu(2)
                    if live(0):
                        act.wait_ge(h_T, h_mlp(l, i))
                        normalise(xh[0], lnst, i, h_xh)
                    if live(2):
                        gelu(3)
                    if live(1):
                        h_high(h_mlp(l, i - 1), b_H, 4 * (l * GROUPS + (i - 1)))
                pipeline(act, 3, mlp)

            act.wait_ge(gw_raw, 80)
            nc.scalar.copy(g1[0][:, 0:2, :], raw_g1[:, 0:2, :]).then_inc(gw_hi, 1)
            nc.scalar.copy(g1[0][0:EA, 2, :], raw_g1[0:EA, 2, :]).then_inc(gw_hi, 1)
            nc.scalar.copy(g2[0][:, :, :], raw_g2[:, :, :]).then_inc(gw_hi, 1)
            act.wait_ge(rw_T, 1)
            nc.scalar.copy(rwT[:, :, :], chunks(PT, KC, EXP)).then_inc(rw_ready, 1)

            def seg_hi(n, slot, turn):
                act.wait_ge(S_IN[slot], 16 * turn + 16)
                if not (isinstance(n, int) and n < 2):
                    act.wait_ge(s_pe, n - 1)
                nc.scalar.copy(ehl[slot % 2][:, :, 0:EA], rows_in[slot][:, :, 0:EA]).then_inc(s_hi, 1)
            for n in range(4):
                seg_hi(n, n, 0)
            with act.Fori(1, ESEGS // 4) as q:
                for slot in range(4):
                    seg_hi(4 * q + slot, slot, q)
            seg_hi(ESEGS - 1, 0, ESEGS // 4)

            def graph(i, live):
                if live(0):
                    act.wait_ge(n_T, i)
                    for slot in range(2):
                        act.wait_ge(N_IN[slot], 16 * ((i + 2 - slot) // 2))
                    for j in range(PAIR):
                        xin = x_in[:, bass.ds(i % 2, 1), j, :].rearrange("p a d -> p (a d)")
                        t = i * PAIR + j
                        a = ident_act(xn[:, j, :], xin, scale=xst[:, bass.ds(t, 1), 0:1].rearrange("p a d -> p (a d)"),
                                      bias=xst[:, bass.ds(t, 1), 1:2].rearrange("p a d -> p (a d)"))
                    a.then_inc(n_xn, 1)
                if live(1):
                    for c in range(2):
                        act.wait_ge(n_H, 2 * (i - 1) + c + 1)
                        for j in range(2):
                            a = nc.scalar.activation(ghid[c][:, j, :], chunks(PH[c])[:, j, :], ACT.Relu,
                                                     bias=g1col[:, 2 * c + j:2 * c + j + 1])
                        a.then_inc(n_relu, 1)
                        act.wait_ge(n_relu, 2 * (i - 1) + c + 1)
                        nc.scalar.copy(ghh[c][0][:, :, :], ghid[c][:, :, :]).then_inc(n_hhi, 1)
                if live(0):
                    act.wait_ge(n_T, i + 1)
                    act.wait_ge(n_H, 2 * i)
                    nc.scalar.copy(cT[0][:, 0:2, :], chunks(PT)).then_inc(n_hi, 1)
                    nc.scalar.copy(cT[0][0:EA, 2, :], PS[0:EA, 0:GT]).then_inc(n_hi, 1)
            pipeline(act, 1, graph)

            act.wait_ge(ln_stats, LN_LAST + 1)

            def route(i, live):
                if live(0):
                    act.wait_ge(n_zT, i)
                    for j in range(PAIR):
                        row = res[:, bass.ds(i * PAIR + j, 1), :].rearrange("p a d -> p (a d)")
                        a = ident_act(zt[:, j, :], row[:, 0:D], scale=row[:, D:D + 1], bias=row[:, D + 1:D + 2])
                    a.then_inc(n_z, 1)
                if live(1):
                    act.wait_ge(n_zT, i)
                    act.wait_ge(n_log, i - 1)
                    nc.scalar.copy(zT[:, :, :], chunks(PQ)).then_inc(n_zTs, 1)
            pipeline(act, 1, route)

            def expert(n, slot, turn):
                act.wait_ge(F_IN[slot], 16 * turn + 16)
                act.wait_ge(f_T, n)
                y = yin[slot]
                ident_act(zs[:, :], y[:, 0:D], scale=y[:, D:D + 1], bias=y[:, D + 1:D + 2]).then_inc(f_z, 1)
                act.wait_ge(f_h, n + 1)
                act.wait_ge(f_hT, n)
                nc.scalar.activation(hs[:, :], PM[0:P, 0:EH], ACT.Relu).then_inc(f_hs, 1)
                act.wait_ge(f_hT, n + 1)
                act.wait_ge(f_o, n)
                nc.scalar.copy(hsT[0:EH, :], PQT[0:EH, 0:P]).then_inc(f_hTs, 1)
            with act.Fori(0, FSEGS // 3) as q:
                for slot in range(3):
                    expert(3 * q + slot, slot, q)

        @block.vector
        def _(dve):
            def moments(tiles, t):
                for j in range(PAIR):
                    nc.vector.bn_stats(bn[:, bass.ds(t + j, 1), :].rearrange("p a d -> p (a d)"), tiles[j]).then_inc(ln_st, 1)

            def rstd_all(o, seq):
                steps = [0]

                def step(instruction):
                    instruction.then_inc(ln_step, 1)
                    steps[0] += 1

                def stepped(n=None):
                    dve.wait_ge(ln_step, LN_STEPS * seq + (n or steps[0]))
                two_mean, half_diff, m2, diff2, var_sum, var = (lnt[:, r, :] for r in range(6))
                dve.wait_ge(ln_st, TILES * (seq + 1))
                step(nc.vector.tensor_tensor(two_mean, bn[:, :, 1], bn[:, :, 4], ALU.add))
                step(nc.vector.tensor_tensor(half_diff, bn[:, :, 1], bn[:, :, 4], ALU.subtract))
                step(nc.vector.tensor_tensor(m2, bn[:, :, 2], bn[:, :, 5], ALU.add))
                stepped(2)
                step(nc.vector.tensor_tensor(diff2, half_diff, half_diff, ALU.mult))
                stepped()
                step(nc.vector.scalar_tensor_tensor(out=var_sum, in0=diff2, scalar=D / 4.0, in1=m2, op0=ALU.mult, op1=ALU.add))
                stepped()
                step(nc.vector.tensor_scalar(var, var_sum, 1.0 / D, EPS, ALU.mult, ALU.add))
                stepped()
                step(nc.vector.tensor_scalar(lnt_i[:, :], var.bitcast(I32), 1, None, ALU.logical_shift_right))
                stepped()
                y = lnt[:, 6, :]
                step(nc.vector.tensor_scalar(y.bitcast(I32), lnt_i[:, :], -1.0, RSQRT_MAGIC, ALU.mult, ALU.add))
                for r in range(3):
                    vy, h, y_next = lnt[:, 7, :], lnt[:, 8, :], (lnt[:, 9, :], lnt[:, 6, :], o[:, :, 0])[r]
                    stepped()
                    step(nc.vector.tensor_tensor(vy, var, y, ALU.mult))
                    stepped()
                    step(nc.vector.scalar_tensor_tensor(out=h, in0=vy, scalar=-0.5, in1=y, op0=ALU.mult, op1=ALU.mult))
                    stepped()
                    step(nc.vector.scalar_tensor_tensor(out=y_next, in0=h, scalar=1.5, in1=y, op0=ALU.add, op1=ALU.mult))
                    y = y_next
                stepped()
                assert steps[0] == LN_STEPS
                nc.vector.scalar_tensor_tensor(out=o[:, :, 1], in0=two_mean, scalar=-0.5, in1=o[:, :, 0],
                                               op0=ALU.mult, op1=ALU.mult).then_inc(ln_stats, 1)

            def tile_rows(t, g):
                return [t[:, bass.ds(g * PAIR + j, 1), 0:D].rearrange("p a d -> p (a d)") for j in range(PAIR)]

            def split_lo(o, i, hi, count, done):
                dve.wait_ge(done[0], count)
                nc.vector.tensor_tensor(o, i, f32(hi), ALU.subtract).then_inc(done[1], 1)

            def count_kinds(kinds, scrap, nk, width, segs, kind, kind_int, first_int, turn):
                nb = TILES * turn
                with dve.Fori(0, nk) as b:
                    dve.wait_ge(r_cnt, nb + b)
                    nc.vector.tensor_scalar(scrap, kinds, iota_seg[0:P, bass.ds(b, 1)], 0.0, ALU.is_equal, ALU.add,
                                            accum_out=cnt[:, bass.ds(b, 1)]).then_inc(r_cnt, 1)
                dve.wait_ge(sort_pe, 3 * turn + 1)
                nc.vector.tensor_copy(tot[:, 0:nk], PS[0:P, 64:64 + nk]).then_inc(sort_dve, 1)
                dve.wait_ge(sort_dve, SORT_DVE * turn + 1)
                nc.vector.tensor_tensor_scan(totinc[:, 0:nk], ones[0:P, 0:nk], tot[:, 0:nk], 0.0, ALU.mult, ALU.add).then_inc(sort_dve, 1)
                dve.wait_ge(sort_dve, SORT_DVE * turn + 2)
                nc.vector.tensor_tensor(base[:, 0:nk], totinc[:, 0:nk], tot[:, 0:nk], ALU.subtract).then_inc(sort_dve, 1)
                dve.wait_ge(sort_dve, SORT_DVE * turn + 3)
                nc.vector.tensor_tensor(base[:, 0:nk], base[:, 0:nk], PS[0:P, 0:nk], ALU.add).then_inc(sort_dve, 1)
                nc.vector.tensor_copy(kcol[0:nk, 0:1], PS[0:nk, 128:129]).then_inc(sort_dve, 1)
                dve.wait_ge(sort_dve, SORT_DVE * turn + 4)
                dve.wait_ge(sort_pe, 3 * turn + 2)
                nc.vector.tensor_scalar(kcol[0:nk, 1:2], PS[0:nk, 130:131], 1.0 / width, 0.5 / width - 0.5, ALU.mult, ALU.add).then_inc(sort_dve, 1)
                dve.wait_ge(sort_dve, SORT_DVE * turn + 6)
                nc.vector.tensor_scalar(kcol[0:nk, 2:3], kcol[0:nk, 1:2], RND, None, ALU.add).then_inc(sort_dve, 1)
                dve.wait_ge(sort_dve, SORT_DVE * turn + 7)
                nc.vector.tensor_scalar(kcol[0:nk, 3:4], kcol[0:nk, 2:3], -RND, None, ALU.add).then_inc(sort_dve, 1)
                dve.wait_ge(sort_dve, SORT_DVE * turn + 8)
                nc.vector.tensor_tensor(kcol[0:nk, 1:2], kcol[0:nk, 3:4], iota_part[0:nk, :], ALU.add).then_inc(sort_dve, 1)
                dve.wait_ge(sort_dve, SORT_DVE * turn + 9)
                nc.vector.tensor_scalar(cmp[0:nk, 0:segs], iota_seg[0:nk, 0:segs], kcol[0:nk, 1:2], None, ALU.is_ge).then_inc(sort_dve, 1)
                dve.wait_ge(sort_pe, 3 * turn + 3)
                nc.vector.tensor_scalar(kind[:, 0:segs], PS[:, 0:segs], -1.0, None, ALU.add).then_inc(sort_dve, 1)
                dve.wait_ge(sort_dve, SORT_DVE * turn + 11)
                nc.vector.tensor_copy(kind_int[:, 0:segs], kind[0:1, 0:segs]).then_inc(sort_dve, 1)
                nc.vector.tensor_tensor(segtmp[:, 0:segs], iota_seg[0:1, 0:segs], kind[0:1, 0:segs], ALU.subtract).then_inc(sort_dve, 1)
                dve.wait_ge(sort_dve, SORT_DVE * turn + 12)
                dve.wait_ge(sort_dve, SORT_DVE * turn + 13)
                nc.vector.tensor_scalar(first_int[:, 0:segs], segtmp[:, 0:segs], float(width), None, ALU.mult).then_inc(r_table, 1)

            def place_tokens(kinds, scr, pos, pos_int):
                nc.vector.memset(pos, 0.0).then_inc(r_zero, 1)
                dve.wait_ge(r_zero, 1)
                with dve.Fori(0, EXP) as b:
                    dve.wait_ge(r_acc, b)
                    nc.vector.tensor_scalar(scr[0], kinds, iota_seg[0:P, bass.ds(b, 1)], None, ALU.is_equal).then_inc(r_m, 1)
                    dve.wait_ge(r_m, b + 1)
                    nc.vector.tensor_tensor_scan(scr[1], ones[0:P, 0:TILES], scr[0],
                                                 base[:, bass.ds(b, 1)], ALU.mult, ALU.add).then_inc(r_scan, 1)
                    dve.wait_ge(r_scan, b + 1)
                    nc.vector.tensor_tensor(scr[2], scr[1], scr[0], ALU.mult).then_inc(r_mul, 1)
                    dve.wait_ge(r_mul, b + 1)
                    nc.vector.tensor_tensor(pos, pos, scr[2], ALU.add).then_inc(r_acc, 1)
                dve.wait_ge(r_acc, EXP)
                nc.vector.tensor_scalar(pos_int, pos, -1.0, None, ALU.add).then_inc(f_posi, 1)

            dve.wait_ge(consts, NCONST)
            dve.wait_ge(src_loaded, 16)
            nc.vector.tensor_copy(src_f[:, :], src_i[:, :]).then_inc(e_conv, 1)
            dve.wait_ge(e_conv, 1)
            nc.vector.tensor_scalar(scr[0][:, :], src_f[:, :], 1.0 / TILES, 0.5 / TILES - 0.5, ALU.mult, ALU.add).then_inc(e_conv, 1)
            dve.wait_ge(e_conv, 2)
            nc.vector.tensor_scalar(scr[1][:, :], scr[0][:, :], RND, None, ALU.add).then_inc(e_conv, 1)
            dve.wait_ge(e_conv, 3)
            nc.vector.tensor_scalar(scr[2][:, :], scr[1][:, :], -RND, None, ALU.add).then_inc(e_conv, 1)
            dve.wait_ge(e_conv, 4)
            nc.vector.scalar_tensor_tensor(out=tile_of, in0=scr[2][:, :], scalar=-float(TILES), in1=src_f[:, :],
                                           op0=ALU.mult, op1=ALU.add).then_inc(e_conv, 1)
            dve.wait_ge(e_conv, 5)
            count_kinds(tile_of, scr[0][:, :], TILES, SEG, ESEGS, ekind, ekind_i, efirst_i, 0)

            dve.wait_ge(x_loaded, 16)
            with dve.Fori(0, GROUPS) as g:
                moments(tile_rows(res, g), g * PAIR)
            rstd_all(xst, 0)
            dve.wait_ge(ln_stats, 1)
            with dve.Fori(0, GROUPS) as g:
                normalised = counted(dve, g + 1)
                dve.wait_ge(x_loaded, 16)
                dve.wait_ge(xs_norm, normalised)
                moments(tile_rows(res, g), g * PAIR)
            rstd_all(lnst, 1)
            dve.wait_ge(cols_ready, 1)

            def add_rows(g, what, done):
                nc.vector.tensor_tensor(pair(res, g), pair(res, g), what, ALU.add).then_inc(done, 1)

            def h_low(n):
                dve.wait_ge(h_hi, n + 1)
                nc.vector.tensor_tensor(hT[1][:, :, :], affine[:, :, :], f32(hT[0][:, :, :]), ALU.subtract).then_inc(h_lo, 1)

            def kind_mask(b, slot):
                if not (isinstance(b, int) and b < 2):
                    dve.wait_ge(e_acc, b)
                nc.vector.tensor_scalar(kmask[slot][:, :], tile_of, iota_seg[0:P, bass.ds(b, 1)], None, ALU.is_equal).then_inc(e_mask, 1)

            def kind_rank(b, slot):
                dve.wait_ge(e_mask, b + 1)
                nc.vector.tensor_tensor_scan(krank[slot][:, :], ones[0:P, 0:1].to_broadcast((P, ECOL)), kmask[slot][:, :],
                                             base[:, bass.ds(b, 1)], ALU.mult, ALU.add).then_inc(e_rank, 1)

            def layer(l, sorting):
                dve.wait_ge(b_x2, l * (2 * GROUPS))
                dve.wait_ge(b_gelu, 4 * (l * GROUPS))
                nc.vector.tensor_copy(lcol[:, 0:4 * KC].rearrange("p (w k) -> p w k", k=KC),
                                      cols[:, 0:4 * ROWS_LN].rearrange("p (w r) -> p w r", r=ROWS_LN)[:, :, bass.ds(l * KC, KC)]).then_inc(lcol_ready, 1)
                nc.vector.tensor_copy(lcol[:, 4 * KC:4 * KC + FC], cols[:, bass.ds(4 * ROWS_LN + l * FC, FC)]).then_inc(lcol_ready, 1)
                nc.vector.memset(kmax[:, :, :], -3.4e38).then_inc(lcol_ready, 1)
                nc.vector.memset(esum[:, :, :], 0.0).then_inc(lcol_ready, 1)
                split_lo(wqk[1][:, :, :], raw[:, 0:KC * 2 * D].rearrange("p (k n) -> p k n", k=KC), wqk[0][:, :, :], l + 1, (qk_hi, qk_lo))
                dve.wait_ge(lcol_ready, 4 * l + 4)

                def keys(i, live):
                    if live(1):
                        h_low(h_keys(l, i - 1))
                    if live(2):
                        n = l * GROUPS + (i - 2)
                        dve.wait_ge(a_ks, n + 1)
                        dve.wait_ge(a_max, n)
                        nc.vector.tensor_tensor(kmax[:, :, :], kmax[:, :, :], pair(ksb, i - 2), ALU.max).then_inc(a_max, 1)
                pipeline(dve, 2, keys)

                split_lo(w1[1][:, :, :], raw[:, :].rearrange("p (k n) -> p k n", k=KC), w1[0][:, :, :], l + 1, (w1_hi, w1_lo))
                dve.wait_ge(a_max, (l + 1) * GROUPS)
                nc.vector.tensor_tensor(km[:, :], kmax[:, 0, :], kmax[:, 1, :], ALU.max).then_inc(ctx_dve, 1)
                dve.wait_ge(ctx_pe, 5 * l + 1)
                nc.vector.tensor_reduce(mcol[:, :], chunks(PT, KC, P), AX, ALU.max).then_inc(ctx_dve, 1)
                dve.wait_ge(ctx_dve, 9 * l + 2)
                for k in range(KC):
                    a = nc.vector.tensor_scalar(dg[:, k, :], ident[:, :], mcol[:, k:k + 1], None, ALU.mult)
                a.then_inc(ctx_dve, 1)
                dve.wait_ge(c_mbc, l + 1)

                def key_exp(g, slot):
                    n = l * GROUPS + g
                    if not isinstance(g, int):
                        dve.wait_ge(g_esum, n - 1)
                        dve.wait_ge(g_pe, n - 1)
                    nc.vector.tensor_tensor(ek[:, slot, :, :], pair(ksb, g), mbc[:, :].unsqueeze(1).to_broadcast((P, PAIR, D)),
                                            ALU.subtract).then_inc(g_dk, 1)

                def add_exp(g, slot):
                    n = l * GROUPS + g
                    dve.wait_ge(g_ek, n + 1)
                    dve.wait_ge(g_esum, n)
                    nc.vector.tensor_tensor(esum[:, :, :], esum[:, :, :], ek[:, slot, :, :], ALU.add).then_inc(g_esum, 1)
                key_exp(0, 0)
                with dve.Fori(0, GROUPS // 2) as q:
                    key_exp(2 * q + 1, 1)
                    add_exp(2 * q, 0)
                    key_exp(2 * q + 2, 0)
                    add_exp(2 * q + 1, 1)
                add_exp(GROUPS - 1, 0)

                split_lo(w2[1][:, :, :], raw[:, :].rearrange("p (k n) -> p k n", k=FC), w2[0][:, :, :], l + 1, (w2_hi, w2_lo))
                dve.wait_ge(ctx_pe, 5 * l + 3)
                nc.vector.reciprocal(gn[:, 1, :], PS[:, 0:D]).then_inc(ctx_dve, 1)
                dve.wait_ge(ctx_dve, 9 * l + 4)
                dve.wait_ge(g_pe, (l + 1) * GROUPS)
                nc.vector.tensor_tensor(gn[:, 0, :], chunks(PQT, KC, D)[:, 0, :], gn[:, 1, :], ALU.mult).then_inc(ctx_dve, 1)
                nc.vector.tensor_tensor(gn[:, 1, :], chunks(PQT, KC, D)[:, 1, :], gn[:, 1, :], ALU.mult).then_inc(ctx_dve, 1)
                dve.wait_ge(ctx_dve, 9 * l + 6)
                for k in range(KC):
                    a = nc.vector.tensor_scalar(gn[:, k, :], gn[:, k, :], lcol[:, k:k + 1], lcol[:, KC + k:KC + k + 1], ALU.mult, ALU.add)
                a.then_inc(ctx_dve, 1)
                dve.wait_ge(ctx_pe, 5 * l + 4)
                nc.vector.tensor_tensor(ct[:, :, :], chunks(PM, KC, 128), blockmask[:, :].unsqueeze(1).to_broadcast((128, KC, 128)),
                                        ALU.mult).then_inc(ctx_dve, 1)
                dve.wait_ge(w_bias, 32 * l + 32)
                dve.wait_ge(ctx_pe, 5 * l + 5)
                nc.vector.scalar_tensor_tensor(out=mprod[:, :, :], in0=bo_b[:, :].unsqueeze(1).to_broadcast((128, KC, D)),
                                               scalar=1.0 / HEADS, in1=chunks(PS, KC, D), op0=ALU.mult, op1=ALU.add).then_inc(ctx_dve, 1)
                dve.wait_ge(d_hi, l + 1)
                nc.vector.tensor_tensor(mmat[1][:, :, :], mprod[:, :, :], f32(mmat[0][:, :, :]), ALU.subtract).then_inc(d_lo, 1)

                heads = "p j (h d) -> p (j h) d"
                dve.wait_ge(ln_stats, 2 * l + 2)

                def attend(i, live):
                    n2, n3, n4 = (l * GROUPS + (i - d) for d in (2, 3, 4))
                    if live(2):
                        dve.wait_ge(b_Q, n2 + 1)
                        q3 = PQ[0:P, :].rearrange("p (h d) -> p h d", d=DH)
                        nc.vector.tensor_reduce(qstat[:, 0, :], q3, AX, ALU.max).then_inc(b_soft, 1)
                        dve.wait_ge(b_soft, 5 * n2 + 1)
                        nc.vector.tensor_tensor(qd[:, :, :].rearrange(heads, d=DH), q3,
                                                qstat[:, 0, :].unsqueeze(2).to_broadcast((P, PAIR * HEADS, DH)),
                                                ALU.subtract).then_inc(b_soft, 1)
                    if live(4):
                        dve.wait_ge(b_M, n4 + 1)
                        add_rows(i - 4, PM[0:P, :].rearrange("p (j d) -> p j d", j=PAIR), b_x1)
                    if live(1):
                        h_low(h_attn(l, i - 1))
                    if live(3):
                        dve.wait_ge(b_qhi, n3 + 1)
                        nc.vector.tensor_tensor(qT[1][:, :, :], chunks(PQT), f32(qT[0][:, :, :]), ALU.subtract).then_inc(b_qlo, 1)
                    if live(4):
                        added = counted(dve, n4 + 1)
                        dve.wait_ge(x_loaded, 16)
                        dve.wait_ge(b_x1, added)
                        moments(tile_rows(res, i - 4), (i - 4) * PAIR)
                    if live(2):
                        dve.wait_ge(b_qe, n2 + 1)
                        nc.vector.tensor_reduce(qstat[:, 1, :], qd[:, :, :].rearrange(heads, d=DH), AX, ALU.add).then_inc(b_soft, 1)
                        dve.wait_ge(b_soft, 5 * n2 + 3)
                        nc.vector.reciprocal(qstat[:, 2, :], qstat[:, 1, :]).then_inc(b_soft, 1)
                        dve.wait_ge(b_qT, n2)
                        dve.wait_ge(b_soft, 5 * n2 + 4)
                        nc.vector.tensor_tensor(qn[:, :, :].rearrange(heads, d=DH), qd[:, :, :].rearrange(heads, d=DH),
                                                qstat[:, 2, :].unsqueeze(2).to_broadcast((P, PAIR * HEADS, DH)),
                                                ALU.mult).then_inc(b_soft, 1)
                pipeline(dve, 4, attend)
                rstd_all(lnst, 2 * l + 2)
                dve.wait_ge(ln_stats, 2 * l + 3)

                def mlp(i, live):
                    n2, n3 = l * GROUPS + (i - 2), l * GROUPS + (i - 3)

                    def hid_lo(c):
                        dve.wait_ge(b_hhi, 4 * n2 + c + 1)
                        nc.vector.tensor_tensor(hidh[c % 2][1][:, :, :], hid[c % 2][:, :, :], f32(hidh[c % 2][0][:, :, :]),
                                                ALU.subtract).then_inc(b_hlo, 1)
                    if live(3):
                        dve.wait_ge(b_Y, n3 + 1)
                        add_rows(i - 3, PY[0:P, :].rearrange("p (j d) -> p j d", j=PAIR), b_x2)
                        dve.wait_ge(b_x2, 2 * n3 + 1)
                        add_rows(i - 3, b2_b[:, :].unsqueeze(1).to_broadcast((P, PAIR, D)), b_x2)
                    if live(2):
                        hid_lo(0)
                    if sorting and live(0):
                        kind_mask(2 * i, 0)
                        kind_rank(2 * i, 0)
                    if live(2):
                        hid_lo(1)
                    if live(3):
                        added = counted(dve, 2 * n3 + 2)
                        dve.wait_ge(x_loaded, 16)
                        dve.wait_ge(b_x2, added)
                        moments(tile_rows(res, i - 3), (i - 3) * PAIR)
                    if sorting and live(0):
                        kind_mask(2 * i + 1, 1)
                    if live(2):
                        hid_lo(2)
                    if sorting and live(0):
                        kind_rank(2 * i + 1, 1)
                    if live(2):
                        hid_lo(3)
                    if live(1):
                        h_low(h_mlp(l, i - 1))
                pipeline(dve, 3, mlp)
                if sorting:
                    dve.wait_ge(e_acc, TILES + 1)
                    nc.vector.tensor_scalar(pos_i[:, :], pos_f, -1.0, None, ALU.add).then_inc(pos_ready, 1)
                rstd_all(lnst, 2 * l + 3)

            layer(0, True)
            with dve.Fori(1, LAYERS) as l:
                layer(l, False)

            dve.wait_ge(b_x2, 2 * LAYERS * GROUPS)
            dve.wait_ge(ln_stats, LN_LAST)
            nc.vector.memset(agg[:, :, :], 0.0).then_inc(s_ones, 1)
            for i in range(2):
                nc.vector.memset(f32(ehl[i][:, :, EA:EA + 2]), 1.0).then_inc(s_ones, 1)
            dve.wait_ge(gw_hi, 3)
            nc.vector.tensor_tensor(g1[1][:, 0:2, :], raw_g1[:, 0:2, :], f32(g1[0][:, 0:2, :]), ALU.subtract).then_inc(gw_lo, 1)
            nc.vector.tensor_tensor(g1[1][0:EA, 2, :], raw_g1[0:EA, 2, :], f32(g1[0][0:EA, 2, :]), ALU.subtract).then_inc(gw_lo, 1)
            nc.vector.tensor_tensor(g2[1][:, :, :], raw_g2[:, :, :], f32(g2[0][:, :, :]), ALU.subtract).then_inc(gw_lo, 1)
            dve.wait_ge(gcol_pe, 1)
            nc.vector.tensor_tensor(g1col[:, :], PS[:, 0:2 * GHC:2], cols[:, NROW - 1 - GHC:NROW - 1], ALU.add).then_inc(gcol_ready, 1)
            dve.wait_ge(s_ones, 3)

            def seg_add(n, par):
                tile = dve.value_load(ekind_i[0:1, bass.ds(n, 1)], min_val=0, max_val=TILES - 1)
                o = agg[:, bass.ds(tile, 1), :].rearrange("p a c -> p (a c)")
                ps = [PS, PM][par][0:P, 0:2 * EA + 2]
                dve.wait_ge(s_pe, n + 1)
                dve.wait_ge(s_add2, n)
                nc.vector.tensor_tensor(o, o, ps[:, 0:EA + 1], ALU.add).then_inc(s_add, 1)
                dve.wait_ge(s_add, n + 1)
                nc.vector.tensor_tensor(o[:, 0:EA], o[:, 0:EA], ps[:, EA + 2:2 * EA + 2], ALU.add).then_inc(s_add2, 1)

            def seg_prep(n, slot, turn):
                par = slot % 2
                dve.wait_ge(S_IN[slot], 16 * turn + 16)
                nc.vector.tensor_scalar(kb[:, par, :], rows_in[slot][:, :, EA], ekind[:, bass.ds(n, 1)], None,
                                        ALU.subtract).then_inc(s_kb, 1)
                dve.wait_ge(s_kb, n + 1)
                if not (isinstance(n, int) and n < 2):
                    dve.wait_ge(s_pe, n - 1)
                for j in range(SEGR):
                    a = nc.vector.tensor_scalar(oh[par][:, j, :], iota_node[:, :], kb[:, par, j:j + 1], None, ALU.is_equal)
                a.then_inc(s_oh, 1)
                dve.wait_ge(s_hi, n + 1)
                nc.vector.tensor_tensor(ehl[par][:, :, EA + 2:2 * EA + 2], rows_in[slot][:, :, 0:EA],
                                        f32(ehl[par][:, :, 0:EA]), ALU.subtract).then_inc(s_lo, 1)
            for n in range(4):
                seg_prep(n, n, 0)
                if n > 0:
                    seg_add(n - 1, (n - 1) % 2)
            with dve.Fori(1, ESEGS // 4) as q:
                for slot in range(4):
                    seg_prep(4 * q + slot, slot, q)
                    seg_add(4 * q + (slot - 1), (slot - 1) % 2)
            seg_prep(ESEGS - 1, 0, ESEGS // 4)
            seg_add(ESEGS - 2, 1)
            seg_add(ESEGS - 1, 0)
            dve.wait_ge(s_add2, ESEGS)

            def graph(i, live):
                if live(0):
                    sums = pair(agg, i, ROW)
                    dve.wait_ge(n_T, i)
                    nc.vector.tensor_scalar(crec[:, 0, :, :], sums[:, :, EA:ROW], 1.0, None, ALU.max).then_inc(n_an, 1)
                    dve.wait_ge(n_an, 3 * i + 1)
                    nc.vector.reciprocal(crec[:, 1, :, :], crec[:, 0, :, :]).then_inc(n_an, 1)
                    dve.wait_ge(n_an, 3 * i + 2)
                    nc.vector.tensor_tensor(an[:, :, :], sums[:, :, 0:EA], crec[:, 1, :, :].to_broadcast((P, PAIR, EA)), ALU.mult).then_inc(n_an, 1)
                if live(1):
                    for c in range(2):
                        dve.wait_ge(n_hhi, 2 * (i - 1) + c + 1)
                        nc.vector.tensor_tensor(ghh[c][1][:, :, :], ghid[c][:, :, :], f32(ghh[c][0][:, :, :]), ALU.subtract).then_inc(n_hlo, 1)
                if live(0):
                    dve.wait_ge(n_hi, 2 * i + 2)
                    nc.vector.tensor_tensor(cT[1][:, 0:2, :], chunks(PT), f32(cT[0][:, 0:2, :]), ALU.subtract).then_inc(n_lo, 1)
                    nc.vector.tensor_tensor(cT[1][0:EA, 2, :], PS[0:EA, 0:GT], f32(cT[0][0:EA, 2, :]), ALU.subtract).then_inc(n_lo, 1)
                if live(1):
                    g = i - 1
                    dve.wait_ge(n_Y, g + 1)
                    add_rows(g, PY[0:P, :].rearrange("p (j d) -> p j d", j=PAIR), n_y)
                    dve.wait_ge(n_y, 3 * g + 1)
                    add_rows(g, x_in[:, bass.ds(g % 2, 1), :, :].rearrange("p a j d -> p (a j) d"), n_y)
                    dve.wait_ge(n_y, 3 * g + 2)
                    add_rows(g, gb2_b[:, :].unsqueeze(1).to_broadcast((P, PAIR, D)), n_y)
                    added = counted(dve, 3 * g + 3)
                    dve.wait_ge(x_loaded, 16)
                    dve.wait_ge(n_y, added)
                    moments(tile_rows(res, g), g * PAIR)
            pipeline(dve, 1, graph)
            rstd_all(res[:, :, D:D + 2], LN_LAST)

            with dve.Fori(0, GROUPS) as g:
                dve.wait_ge(n_log, g + 1)
                dve.wait_ge(n_top, 6 * g)
                nc.vector.tensor_tensor(logit[:, :, :], PM[0:P, 0:PAIR * EXP].rearrange("p (j e) -> p j e", j=PAIR),
                                        rb_b[:, :].unsqueeze(1).to_broadcast((P, PAIR, EXP)), ALU.add).then_inc(n_top, 1)
                biased, found = counted(dve, 6 * g + 1), counted(dve, 6 * g + 3)
                dve.wait_ge(rw_raw, 32)
                dve.wait_ge(n_top, biased)
                for j in range(PAIR):
                    nc.vector.max(best[:, j, :], logit[:, j, :]).then_inc(n_top, 1)
                dve.wait_ge(rw_raw, 32)
                dve.wait_ge(n_top, found)
                for j in range(PAIR):
                    nc.vector.max_index(besti[:, j, :], best[:, j, :], logit[:, j, :]).then_inc(n_top, 1)
                dve.wait_ge(n_top, 6 * g + 5)
                nc.vector.tensor_copy(res[:, bass.ds(g * PAIR, PAIR), D + 3], besti[:, :, 0]).then_inc(n_top, 1)

            dve.wait_ge(n_top, 6 * GROUPS)
            nc.vector.tensor_copy(fexp[:, :], res[:, :, D + 3]).then_inc(e_conv, 1)
            dve.wait_ge(e_conv, 6)
            count_kinds(fexp[:, :], fscr[0][:, :], EXP, P, FSEGS, fkind, fkind_i, ffirst_i, 1)
            place_tokens(fexp[:, :], [t[:, :] for t in fscr], fpos[:, :], fpos_i[:, :])
            nc.vector.memset(hsT[EH:EH + 1, :], 1.0).then_inc(f_bias, 1)

            def expert(n, slot, turn):
                y = yin[slot]
                dve.wait_ge(f_T, n + 1)
                nc.vector.tensor_copy(zsT[:, :, :], chunks(PT, KC, P)).then_inc(f_zT, 1)
                dve.wait_ge(f_idx, 2 * n)
                dve.wait_ge(F_IN[slot], 16 * turn + 16)
                nc.vector.tensor_scalar(omiss[:, :], y[:, D + 3:D + 4], fkind[0:P, bass.ds(n, 1)], float(4 * N),
                                        ALU.not_equal, ALU.mult).then_inc(f_idx, 1)
                dve.wait_ge(f_idx, 2 * n + 1)
                dve.wait_ge(F_OUT[slot], 16 * turn)
                nc.vector.tensor_tensor(oidx[slot][:, :], omiss[:, :], y[:, D + 2:D + 3], ALU.add).then_inc(f_idx, 1)
                dve.wait_ge(f_o, n + 1)
                nc.vector.scalar_tensor_tensor(out=orow[slot][:, :], in0=PY[0:P, 0:D], scalar=0.0, in1=y[:, 0:D],
                                               op0=ALU.max, op1=ALU.add).then_inc(f_row, 1)
            with dve.Fori(0, FSEGS // 3) as q:
                for slot in range(3):
                    expert(3 * q + slot, slot, q)

        @block.tensor
        def _(pe):
            def transposes(o, i, n, k=KC):
                for j in range(PAIR):
                    for c in range(k):
                        a = nc.tensor.transpose(o[0:128, c, j * n:(j + 1) * n], i[:, j, c * 128:(c + 1) * 128], ident[0:n, 0:n])
                return a

            pe.wait_ge(consts, NCONST)
            pe.wait_ge(rows_loaded, 7 * 16)
            nc.tensor.transpose(PS[:, 0:NROW], colrows[:, :], ident[0:NROW, 0:NROW]).then_inc(cols_T, 1)

            def count_kinds(nk, segs, turn):
                pe.wait_ge(r_cnt, TILES if turn == 0 else TILES + nk)
                pe.wait_ge(cols_ready, 1)
                mm(PS[0:P, 0:nk], tri[0:P, 0:P], cnt[:, 0:nk], True, True)
                mm(PS[0:P, 64:64 + nk], ones[0:P, 0:P], cnt[:, 0:nk], True, True)
                mm(PS[0:nk, 128:130], cnt[:, 0:nk], ones[0:P, 0:2], True, True).then_inc(sort_pe, 1)
                pe.wait_ge(sort_dve, SORT_DVE * turn + 5)
                mm(PS[0:nk, 130:131], tri[0:nk, 0:nk], kcol[0:nk, 0:1], True, True).then_inc(sort_pe, 1)
                pe.wait_ge(sort_dve, SORT_DVE * turn + 10)
                pe.wait_ge(sort_dve, SORT_DVE * turn + 4)
                mm(PS[:, 0:segs], ones[0:nk, :], cmp[0:nk, 0:segs], True, True).then_inc(sort_pe, 1)
            count_kinds(TILES, ESEGS, 0)

            def xhat_T(n):
                pe.wait_ge(h_xh, n + 1)
                pe.wait_ge(h_aff, n)
                transposes(chunks(PT), xh[0], P).then_inc(h_T, 1)

            with pe.Fori(0, LAYERS) as l:
                pe.wait_ge(qk_lo, l + 1)

                def keys(i, live):
                    if live(1):
                        xhat_T(h_keys(l, i - 1))
                    if live(2):
                        n = l * GROUPS + (i - 2)
                        pe.wait_ge(h_lo, h_keys(l, i - 2) + 1)
                        pe.wait_ge(a_ks, n)
                        for j in range(PAIR):
                            for k in range(KC):
                                a = mm3(PQ[0:P, j * D:(j + 1) * D], at(hT, slice(None), k, slice(j * P, (j + 1) * P)),
                                        at(wqk, slice(None), k, slice(D, 2 * D)), k == 0, k == KC - 1)
                        a.then_inc(a_K, 1)
                pipeline(pe, 2, keys)

                pe.wait_ge(ctx_dve, 9 * l + 1)
                for k in range(KC):
                    a = nc.tensor.transpose(PT[:, k * P:(k + 1) * P], km[:, k * 128:(k + 1) * 128], ident[0:P, 0:P])
                a.then_inc(ctx_pe, 1)
                pe.wait_ge(ctx_dve, 9 * l + 3)
                pe.wait_ge(sort_dve, 11)
                mm(PS[0:P, 0:D], ones[:, 0:P], dg[:, :, :].rearrange("p k n -> p (k n)"), True, True).then_inc(ctx_pe, 1)

                def weighted(g, slot):
                    n = l * GROUPS + g
                    pe.wait_ge(g_ek, n + 1)
                    pe.wait_ge(g_xh, n + 1)
                    for j in range(PAIR):
                        for k in range(KC):
                            a = mm(PQT[:, k * D:(k + 1) * D], xh[slot][:, j, k * 128:(k + 1) * 128], ek[:, slot, j, :],
                                   isinstance(g, int) and g == 0 and j == 0 and k == 0, False)
                    a.then_inc(g_pe, 1)
                weighted(0, 0)
                with pe.Fori(0, GROUPS // 2) as q:
                    weighted(2 * q + 1, 1)
                    weighted(2 * q + 2, 0)

                pe.wait_ge(g_esum, (l + 1) * GROUPS)
                for j in range(PAIR):
                    a = mm(PS[:, 0:D], ones[0:P, :], esum[:, j, :], j == 0, j == PAIR - 1)
                a.then_inc(ctx_pe, 1)
                pe.wait_ge(ctx_dve, 9 * l + 7)
                pe.wait_ge(w_vo, 32 * l + 32)
                for h in range(KC):
                    for k in range(KC):
                        a = mm(PM[:, h * 128:(h + 1) * 128], raw_vo[:, 0, k, h * 128:(h + 1) * 128],
                               gn[:, k, h * 128:(h + 1) * 128], k == 0, k == KC - 1)
                a.then_inc(ctx_pe, 1)
                pe.wait_ge(ctx_dve, 9 * l + 8)
                for h in range(KC):
                    a = mm(PS[:, h * D:(h + 1) * D], ct[:, h, :], raw_vo[:, 1, h, :], True, True)
                a.then_inc(ctx_pe, 1)
                pe.wait_ge(d_lo, l + 1)
                pe.wait_ge(w1_lo, l + 1)
                pe.wait_ge(w2_lo, l + 1)

                def attend(i, live):
                    n1, n3 = l * GROUPS + (i - 1), l * GROUPS + (i - 3)
                    if live(1):
                        xhat_T(h_attn(l, i - 1))
                    if live(3):
                        pe.wait_ge(b_soft, 5 * n3 + 5)
                        pe.wait_ge(b_qlo, n3)
                        transposes(chunks(PQT), qn, P).then_inc(b_qT, 1)
                    if live(1):
                        pe.wait_ge(h_lo, h_attn(l, i - 1) + 1)
                        if live(2):
                            pe.wait_ge(b_soft, 5 * n1 - 3)
                        for j in range(PAIR):
                            for k in range(KC):
                                a = mm3(PQ[0:P, j * D:(j + 1) * D], at(hT, slice(None), k, slice(j * P, (j + 1) * P)),
                                        at(wqk, slice(None), k, slice(0, D)), k == 0, k == KC - 1)
                        a.then_inc(b_Q, 1)
                    if live(3):
                        pe.wait_ge(b_qlo, n3 + 1)
                        pe.wait_ge(b_x1, n3)
                        for j in range(PAIR):
                            for k in range(KC):
                                a = mm3(PM[0:P, j * D:(j + 1) * D], at(qT, slice(None), k, slice(j * P, (j + 1) * P)),
                                        at(mmat, slice(None), k, slice(None)), k == 0, k == KC - 1)
                        a.then_inc(b_M, 1)
                pipeline(pe, 4, attend)

                def mlp(i, live):
                    n2 = l * GROUPS + (i - 2)

                    def up(c):
                        for m in range(2):
                            for k in range(KC):
                                a = mm3(chunks(PH[c % 2])[:, m, :], at(w1, slice(None), k, slice((2 * c + m) * 128, (2 * c + m + 1) * 128)),
                                        at(hT, slice(None), k, slice(None)), k == 0, k == KC - 1)
                        a.then_inc(b_H, 1)

                    def down(c):
                        pe.wait_ge(b_hlo, 4 * n2 + c + 1)
                        for m in range(2):
                            for j in range(PAIR):
                                a = mm3(PY[0:P, j * D:(j + 1) * D], at(hidh[c % 2], slice(None), m, slice(j * P, (j + 1) * P)),
                                        at(w2, slice(None), 2 * c + m, slice(None)), c == 0 and m == 0 and j == 0, False)
                        if c == 3:
                            a.then_inc(b_Y, 1)
                    if live(2):
                        pe.wait_ge(h_lo, h_mlp(l, i - 2) + 1)
                        up(0)
                        up(1)
                    if live(1):
                        xhat_T(h_mlp(l, i - 1))
                    if live(2):
                        if live(3):
                            pe.wait_ge(b_x2, 2 * n2 - 1)
                        down(0)
                        up(2)
                        down(1)
                        up(3)
                        down(2)
                        down(3)
                pipeline(pe, 3, mlp)

            pe.wait_ge(gw_raw, 80)
            for c in range(GHC):
                a = mm(PS[:, 2 * c:2 * c + 1], raw_gu[:, c * 128:(c + 1) * 128], cols[:, NROW - 1:NROW], True, True)
            a.then_inc(gcol_pe, 1)
            pe.wait_ge(rw_raw, 32)
            for k in range(KC):
                a = nc.tensor.transpose(PT[:, k * EXP:(k + 1) * EXP], rw_in[:, k * 128:(k + 1) * 128], ident[0:EXP, 0:EXP])
            a.then_inc(rw_T, 1)

            pe.wait_ge(gcol_ready, 1)
            pe.wait_ge(s_ones, 3)

            def segment(n, par):
                pe.wait_ge(s_oh, n + 1)
                pe.wait_ge(s_lo, n + 1)
                if not (isinstance(n, int) and n < 2):
                    pe.wait_ge(s_add2, n - 1)
                for j in range(SEGR):
                    a = mm([PS, PM][par][0:P, 0:2 * EA + 2], oh[par][:, j, :], ehl[par][:, j, :], j == 0, j == SEGR - 1)
                a.then_inc(s_pe, 1)
            for n in range(4):
                segment(n, n % 2)
            with pe.Fori(1, ESEGS // 4) as q:
                for slot in range(4):
                    segment(4 * q + slot, slot % 2)
            segment(ESEGS - 1, 0)
            pe.wait_ge(gw_lo, 3)
            pe.wait_ge(s_add2, ESEGS)
            pe.wait_ge(rw_ready, 1)

            def graph(i, live):
                if live(0):
                    pe.wait_ge(n_xn, i + 1)
                    pe.wait_ge(n_an, 3 * i + 3)
                    pe.wait_ge(n_lo, 2 * i)
                    transposes(chunks(PT), xn, P)
                    for j in range(PAIR):
                        a = nc.tensor.transpose(PS[0:EA, j * P:(j + 1) * P], an[:, j, :], ident[0:P, 0:P])
                    a.then_inc(n_T, 1)
                if live(1):
                    g = i - 1
                    pe.wait_ge(n_lo, 2 * g + 2)
                    for c in range(2):
                        for m in range(2):
                            hc = slice((2 * c + m) * 128, (2 * c + m + 1) * 128)
                            for k in range(3):
                                rows = slice(0, 128 if k < 2 else EA)
                                a = mm3(chunks(PH[c])[:, m, :], at(g1, rows, k, hc), at(cT, rows, k, slice(None)), k == 0, k == 2)
                        a.then_inc(n_H, 1)
                    pe.wait_ge(n_y, 3 * g)
                    for c in range(2):
                        pe.wait_ge(n_hlo, 2 * g + c + 1)
                        for m in range(2):
                            for j in range(PAIR):
                                a = mm3(PY[0:P, j * D:(j + 1) * D], at(ghh[c], slice(None), m, slice(j * P, (j + 1) * P)),
                                        at(g2, slice(None), 2 * c + m, slice(None)), c == 0 and m == 0 and j == 0, False)
                    a.then_inc(n_Y, 1)
            pipeline(pe, 1, graph)

            def route(i, live):
                if live(0):
                    pe.wait_ge(n_z, i + 1)
                    pe.wait_ge(n_zTs, i)
                    transposes(chunks(PQ), zt, P).then_inc(n_zT, 1)
                if live(1):
                    g = i - 1
                    pe.wait_ge(n_zTs, g + 1)
                    pe.wait_ge(n_top, 6 * g)
                    for j in range(PAIR):
                        for k in range(KC):
                            a = mm(PM[0:P, j * EXP:(j + 1) * EXP], zT[:, k, j * P:(j + 1) * P], rwT[:, k, :], k == 0, k == KC - 1)
                    a.then_inc(n_log, 1)
            pipeline(pe, 1, route)

            count_kinds(EXP, FSEGS, 1)
            pe.wait_ge(f_w, 16 * 5)
            pe.wait_ge(f_bias, 1)

            def expert(n, slot):
                e = pe.value_load(fkind_i[0:1, bass.ds(n, 1)], min_val=0, max_val=EXP - 1)
                pe.wait_ge(f_z, n + 1)
                pe.wait_ge(f_zT, n)
                for k in range(KC):
                    a = nc.tensor.transpose(PT[:, k * P:(k + 1) * P], zs[:, k * 128:(k + 1) * 128], ident[0:P, 0:P])
                a.then_inc(f_T, 1)
                pe.wait_ge(f_zT, n + 1)
                mm(PM[0:P, 0:EH], ones[0:1, 0:P], fb1_r[0:1, bass.ds(e * EH, EH)], True, False)
                for k in range(KC):
                    a = mm(PM[0:P, 0:EH], zsT[:, k, :], fw1[:, k, bass.ds(e * EH, EH)], False, k == KC - 1)
                a.then_inc(f_h, 1)
                pe.wait_ge(f_bias, 1)
                pe.wait_ge(f_hs, n + 1)
                nc.tensor.transpose(PQT[0:EH, 0:P], hs[:, :], ident[0:P, 0:P]).then_inc(f_hT, 1)
                pe.wait_ge(f_hTs, n + 1)
                pe.wait_ge(f_row, n)
                mm(PY[0:P, 0:D], hsT[:, :], fw2[:, bass.ds(e * D, D)], True, True).then_inc(f_o, 1)
            pe.wait_ge(r_table, 2)
            with pe.Fori(0, FSEGS // 3) as q:
                for slot in range(3):
                    expert(3 * q + slot, slot)
    return nc


INPUTS = ["x", "src", "edge_attr_64", "L0_gnn_u", "L0_gnn_W1", "L0_gnn_b1", "L0_gnn_W2", "L0_gnn_b2", "L0_mix_Wq", "L0_mix_Wk",
          "L0_mix_Wv", "L0_mix_Wo", "L0_mix_bo", "L0_mix_ln1_g", "L0_mix_ln1_b", "L0_mix_W1", "L0_mix_b1", "L0_mix_W2",
          "L0_mix_b2", "L0_mix_ln2_g", "L0_mix_ln2_b", "L0_ffn_router_w", "L0_ffn_router_b", "L0_ffn_W1", "L0_ffn_b1",
          "L0_ffn_W2", "L0_ffn_b2"]


def kernel(**inputs):
    import numpy as np
    import concourse.bacc as bacc
    from concourse.bass_utils import run_bass_kernel_spmd

    nc = bacc.Bacc("TRN2", target_bir_lowering=False, num_devices=1)
    arrays, args = {}, []
    for name in INPUTS:
        a = np.ascontiguousarray(inputs[name])
        arrays[f"in_{name}"] = a
        args.append(nc.dram_tensor(f"in_{name}", a.shape, mybir.dt.from_np(a.dtype), kind="ExternalInput").ap())
    args.append(nc.dram_tensor("nodes_out", (N, D), F32, kind="ExternalOutput").ap())
    build(nc, *args)
    r = run_bass_kernel_spmd(nc, [arrays], core_ids=[0])
    return r.results[0]["nodes_out"]
```

```python
from contextlib import ExitStack

import concourse.bass as bass
from concourse import mybir

F32 = mybir.dt.float32
F32R = mybir.dt.float32r
I32 = mybir.dt.int32
U32 = mybir.dt.uint32
ALU = mybir.AluOpType
ACT = mybir.ActivationFunctionType
AX = mybir.AxisListType.X

P = 125
TILES = 50
D = 256
KC = D // 128
PAIR = 2
GROUPS = TILES // PAIR
GT = PAIR * P
N = P * TILES
LAYERS = 4
HEADS = 8
DH = D // HEADS
FF = 4 * D
FC = FF // 128
EA = 64
EDGES = 106250
ECOL = EDGES // P
ROW = EA + 1
SEG = 1024
SEGR = SEG // 128
ETILES = -(-EDGES // SEG)
ESEGS = ETILES + TILES - 1
CH = 17
CHUNKS = ECOL // CH
GH = 512
GHC = GH // 128
GLOB = 128
EXP = 32
EH = 64
YROW = D + 4
FSEGS = TILES + EXP - 1
RIN = 8
AHEAD = 5
YIN = 9
OUTS = 3
EPS = 1e-5
LN_STEPS = 17
RSQRT_MAGIC = float(0x5f3759df)
RND = 8388608.0
ROWS_LN = LAYERS * KC
NROW = 4 * ROWS_LN + LAYERS * FC + GHC + 1
NCONST = 8 + 128 // DH
SCALE = DH ** -0.25
SORT_DVE = 13
SPARE = ETILES * SEG - EDGES
SPARE_P = SPARE // 2


def build(nc, x, src, edge_attr, u, gW1, gb1, gW2, gb2, Wq, Wk, Wv, Wo, bo, ln1_g, ln1_b, mW1, mb1, mW2, mb2,
          ln2_g, ln2_b, rw, rb, fW1, fb1, fW2, fb2, out):
    edges_sorted = nc.dram_tensor("edges_sorted", (ETILES * SEG, ROW), F32, kind="Internal").ap()
    tokens_sorted = nc.dram_tensor("tokens_sorted", (N, YROW), F32, kind="Internal").ap()
    x_rows = x.rearrange("(p t) d -> p t d", t=TILES)
    edge_rows = edge_attr.rearrange("(p c) a -> p c a", c=ECOL)

    ctx = ExitStack()
    with ctx:
        def sb(name, shape, dt=F32, where=None):
            return (where or ctx).enter_context(nc.sbuf_tensor(name, shape, dt))

        def both(name, shape, where=None):
            return [sb(f"{name}_{n}", shape, F32R, where) for n in ("hi", "lo")]

        bank = [ctx.enter_context(nc.psum_tensor(f"bank{i}", [128, 512], F32)) for i in range(8)]
        PT, PQ, PQT, PM, PH0, PH1, PY, PS = bank
        PH = [PH0, PH1]
        SEG_BANK = [PS, PM, PQ, PQT]

        res = sb("res", [P, TILES, YROW])
        ident = sb("ident", [128, 128])
        ones = sb("ones", [128, 128])
        tri = sb("tri", [128, 128])
        cols = sb("cols", [128, NROW])
        iota_node = sb("iota_node", [128, P])
        iota_seg = sb("iota_seg", [128, ESEGS])
        iota_part = sb("iota_part", [128, 1])
        ekind = sb("ekind", [128, ESEGS])
        ekind_i = sb("ekind_i", [1, ESEGS], I32)
        efirst_i = sb("efirst_i", [1, ESEGS], I32)
        segtmp = sb("segtmp", [1, ESEGS])
        bn = sb("bn", [P, TILES, 6])
        lnt = sb("lnt", [P, 8, TILES])
        lnt_i = sb("lnt_i", [P, TILES], I32)
        xst = sb("xst", [P, TILES, 2])
        src_f = sb("src_f", [P, ECOL])
        pos_i = sb("pos_i", [P, ECOL], I32)
        cnt = sb("cnt", [P, TILES])
        tot = sb("tot", [P, TILES])
        totinc = sb("totinc", [P, TILES])
        base = sb("base", [P, TILES])
        kcol = sb("kcol", [TILES, 4])
        cmp = sb("cmp", [TILES, ESEGS])
        staging = sb("staging", [128, 2, CH, ROW])
        stage = staging[0:P, :, :, :]
        idx = sb("idx", [P, 2, CH], I32)

        layers = ExitStack()
        wqk = both("wqk", [128, KC, 2 * D], layers)
        w1 = both("w1", [128, KC, FF], layers)
        w2 = both("w2", [128, FC, D], layers)
        raw_vo = sb("raw_vo", [128, 2, KC, D], F32, layers)
        raw = sb("raw", [128, KC * FF], F32, layers)
        bo_b = sb("bo_b", [128, D], F32, layers)
        b2_b = sb("b2_b", [P, D], F32, layers)
        lcol = sb("lcol", [128, 4 * KC + FC], F32, layers)
        lnst = sb("lnst", [P, TILES, 2], F32, layers)
        xh = [sb(f"xh{i}", [P, PAIR, D], F32, layers) for i in range(2)]
        affine = sb("affine", [128, KC, GT], F32, layers)
        hT = both("hT", [128, KC, GT], layers)
        ek = sb("ek", [P, 2, PAIR, D], F32, layers)
        kmax = sb("kmax", [P, PAIR, D], F32, layers)
        km = sb("km", [P, D], F32, layers)
        mbc = sb("mbc", [P, D], F32, layers)
        esum = sb("esum", [P, PAIR, D], F32, layers)
        mcol = sb("mcol", [128, KC], F32, layers)
        blockmask = sb("blockmask", [128, 128], F32, layers)
        dg = sb("dg", [128, KC, 128], F32, layers)
        k_place = ExitStack()
        ksb = sb("ksb", [P, TILES, D], F32, k_place)
        k_place.close()
        pos_f = stage[:, 0, :, :].rearrange("p c r -> p (c r)")[:, 0:ECOL]
        tile_of = stage[:, 1, :, :].rearrange("p c r -> p (c r)")[:, 0:ECOL]
        k_place = ExitStack()
        scr = [sb(f"scr{i}", [P, ECOL], F32, k_place) for i in range(3)]
        src_i = sb("src_i", [P, ECOL], I32, k_place)
        colrows = sb("colrows", [NROW, 128], F32, k_place)
        k_place.close()
        k_place = ExitStack()
        gn = sb("gn", [128, KC, D], F32, k_place)
        ct = sb("ct", [128, KC, 128], F32, k_place)
        mmat = both("mmat", [128, KC, D], k_place)
        mprod = sb("mprod", [128, KC, D], F32, k_place)
        qd = sb("qd", [P, PAIR, D], F32, k_place)
        qn = sb("qn", [P, PAIR, D], F32, k_place)
        qstat = sb("qstat", [P, 3, PAIR * HEADS], F32, k_place)
        qT = both("qT", [128, KC, GT], k_place)
        hid = [sb(f"hid{i}", [128, 2, GT], F32, k_place) for i in range(2)]
        hidh = [both(f"hidh{i}", [128, 2, GT], k_place) for i in range(2)]
        kmask = [sb(f"kmask{i}", [P, ECOL], F32, k_place) for i in range(2)]
        krank = [sb(f"krank{i}", [P, ECOL], F32, k_place) for i in range(2)]
        k_place.close()
        layers.close()

        fw1 = sb("fw1", [128, KC, EXP * EH])
        seg_place = ExitStack()
        oh = [sb(f"oh{i}", [128, SEGR, P], F32R, seg_place) for i in range(4)]
        ehl = [sb(f"ehl{i}", [128, SEGR, 2 * EA + 2], F32R, seg_place) for i in range(4)]
        seg_place.close()
        fw2 = sb("fw2", [EH + 1, EXP * D])
        gnn = ExitStack()
        agg = sb("agg", [P, TILES, 2 * EA + 2], F32, gnn)
        g1 = both("g1", [128, 3, GH], gnn)
        g2 = both("g2", [128, GHC, D], gnn)
        g1col = sb("g1col", [128, GHC], F32, gnn)
        gb2_b = sb("gb2_b", [P, D], F32, gnn)
        an = sb("an", [P, PAIR, EA], F32, gnn)
        asum = sb("asum", [P, PAIR, EA], F32, gnn)
        crec = sb("crec", [P, 2, PAIR, 1], F32, gnn)
        rwT = sb("rwT", [128, KC, EXP], F32, gnn)
        rb_b = sb("rb_b", [P, EXP], F32, gnn)
        logit = sb("logit", [P, PAIR, EXP], F32, gnn)
        best = sb("best", [P, PAIR, 8], F32, gnn)
        besti = sb("besti", [P, PAIR, 8], U32, gnn)
        staged_rows = staging[:, :, :, :].rearrange("p s c r -> p (s c r)")
        staged = stage.rearrange("p s c r -> p (s c r)")
        x_in = staged[:, 0:2 * PAIR * D].rearrange("p (s j d) -> p s j d", s=2, j=PAIR)
        xn = staged[:, 2 * PAIR * D:3 * PAIR * D].rearrange("p (j d) -> p j d", j=PAIR)
        rw_in = staged[0:EXP, 3 * PAIR * D:3 * PAIR * D + D]
        early = ExitStack()
        raw_g1 = sb("raw_g1", [128, 3, GH], F32, early)
        raw_g2 = sb("raw_g2", [128, GHC, D], F32, early)
        raw_gu = sb("raw_gu", [128, GH], F32, early)
        rows_in = [sb(f"rows_in{i}", [128, SEGR, ROW], F32, early) for i in range(4)]
        rows_in += [staged_rows[:, i * SEGR * ROW:(i + 1) * SEGR * ROW].rearrange("p (r c) -> p r c", r=SEGR) for i in range(4)]
        kb = sb("kb", [128, 4, SEGR], F32, early)
        early.close()
        late = ExitStack()
        cT = both("cT", [128, 3, GT], late)
        ghid = [sb(f"ghid{i}", [128, 2, GT], F32, late) for i in range(2)]
        ghh = [both(f"ghh{i}", [128, 2, GT], late) for i in range(2)]
        zt = sb("zt", [P, PAIR, D], F32, late)
        zT = sb("zT", [128, KC, GT], F32, late)
        late.close()
        gnn.close()
        fb1_r = sb("fb1_r", [EXP, EH])
        fb1T = sb("fb1T", [EH, EXP])
        fmask = sb("fmask", [P, EXP, TILES])
        frank = sb("frank", [P, EXP, TILES])
        fprod = sb("fprod", [P, EXP, TILES])
        fbase = sb("fbase", [P, 2, EXP])
        fpos = sb("fpos", [P, TILES])
        fpos_i = sb("fpos_i", [P, TILES], I32)
        fexp = sb("fexp", [P, TILES])
        fkind = sb("fkind", [128, FSEGS])
        fkind_i = sb("fkind_i", [1, FSEGS], I32)
        ffirst_i = sb("ffirst_i", [1, FSEGS], I32)
        yin = [sb(f"yin{i}", [P, YROW]) for i in range(YIN)]
        zs = sb("zs", [P, D])
        zsT = sb("zsT", [128, KC, P])
        hs = sb("hs", [P, EH])
        hsT = sb("hsT", [EH + 1, P])
        orow = [sb(f"orow{i}", [P, D]) for i in range(3)]
        omiss = sb("omiss", [P, 1])
        oidx = [sb(f"oidx{i}", [P, 1], I32) for i in range(3)]

        def sems(names):
            return [ctx.enter_context(nc.semaphore(n)) for n in names.split()]

        src_loaded, x_loaded, rows_loaded, w_qk, w_vo, w_1, w_2 = sems("src_loaded x_loaded rows_loaded w_qk w_vo w_1 w_2")
        w_bias, gw_raw, rw_raw, f_w, attr0, attr1 = sems("w_bias gw_raw rw_raw f_w attr0 attr1")
        consts, cols_T, cols_ready, lcol_ready, e_conv = sems("consts cols_T cols_ready lcol_ready e_conv")
        r_zero, r_cnt, r_m, r_scan, r_mul, r_acc, sort_pe = sems("r_zero r_cnt r_m r_scan r_mul r_acc sort_pe")
        e_mask, e_rank, e_mul, e_acc = sems("e_mask e_rank e_mul e_acc")
        sort_dve, r_table, pos_ready, f_posi = sems("sort_dve r_table pos_ready f_posi")
        key_staged, scattered0, scattered1, spare_rows, spare_written = sems("key_staged scattered0 scattered1 spare_rows spare_written")
        ln_st, ln_step, ln_stats = sems("ln_st ln_step ln_stats")
        qk_hi, qk_lo, w1_hi, w1_lo, w2_hi, w2_lo, gw_hi = sems("qk_hi qk_lo w1_hi w1_lo w2_hi w2_lo gw_hi")
        gw_lo, = sems("gw_lo")
        xs_norm, h_xh, h_T, h_aff, h_hi, h_lo = sems("xs_norm h_xh h_T h_aff h_hi h_lo")
        a_K, a_ks, a_max, c_mbc = sems("a_K a_ks a_max c_mbc")
        g_dk, g_ek, g_xh, g_esum, g_pe = sems("g_dk g_ek g_xh g_esum g_pe")
        ctx_pe, ctx_dve, d_hi, d_lo = sems("ctx_pe ctx_dve d_hi d_lo")
        b_Q, b_soft, b_qe, b_qT, b_qhi, b_qlo, b_M = sems("b_Q b_soft b_qe b_qT b_qhi b_qlo b_M")
        b_x1, = sems("b_x1")
        b_H, b_gelu, b_hhi, b_hlo, b_Y, b_x2 = sems("b_H b_gelu b_hhi b_hlo b_Y b_x2")
        S_IN = [ctx.enter_context(nc.semaphore(f"s_in{i}")) for i in range(RIN)]
        s_kb, s_oh, s_hi = sems("s_kb s_oh s_hi")
        s_lo, s_pe, s_add, s_ones = sems("s_lo s_pe s_add s_ones")
        gcol_pe, gcol_ready, n_in0, n_in1, n_xn, n_an, n_T = sems("gcol_pe gcol_ready n_in0 n_in1 n_xn n_an n_T")
        n_hi, n_lo, n_H, n_relu, n_hhi, n_hlo, n_Y, n_x, n_y = sems("n_hi n_lo n_H n_relu n_hhi n_hlo n_Y n_x n_y")
        n_z, n_zT, n_zTs, n_log, n_top, rw_T, rw_ready = sems("n_z n_zT n_zTs n_log n_top rw_T rw_ready")
        F_IN = [ctx.enter_context(nc.semaphore(f"f_in{i}")) for i in range(YIN)]
        f_bias, f_ones, f_scat, f_z, f_bT, f_bTs = sems("f_bias f_ones f_scat f_z f_bT f_bTs")
        f_T, f_zT, f_h, f_hs, f_hT, f_hTs, f_o = sems("f_T f_zT f_h f_hs f_hT f_hTs f_o")
        f_row, f_idx, f_out0, f_out1, f_out2 = sems("f_row f_idx f_out0 f_out1 f_out2")
        ATTR, SCATTERED = [attr0, attr1], [scattered0, scattered1]
        N_IN, F_OUT = [n_in0, n_in1], [f_out0, f_out1, f_out2]

        def mm(o, left, right, start, stop):
            return nc.tensor.matmul(o, left, right, start=start, stop=stop, skip_group_check=True)

        def mm3(o, left, right, start, stop):
            (lh, ll), (rh, rl) = left, right
            mm(o, lh, rh, start, False)
            mm(o, lh, rl, False, False)
            return mm(o, ll, rh, False, stop)

        def counted(eng, value):
            if isinstance(value, int):
                return value
            register = eng.alloc_register()
            eng.reg_mov(register, value)
            return register

        hTk = [hT, [w1[0][:, :, 0:GT], w1[1][:, :, 0:GT]]]

        def at(halves, *where):
            return [h[where] for h in halves]

        def pipeline(eng, depth, body):
            for i in range(depth):
                body(i, lambda d, i=i: d <= i)
            with eng.Fori(depth, GROUPS) as i:
                body(i, lambda d: True)
            for i in range(GROUPS, GROUPS + depth):
                body(i, lambda d, i=i: i - d < GROUPS)

        def key_pipeline(eng, depth, body):
            for i in range(3):
                body(i, lambda d, i=i: d <= i, i % 2)
            with eng.Fori(1, GROUPS // 2) as q:
                body(2 * q + 1, lambda d: True, 1)
                body(2 * q + 2, lambda d: True, 0)
            for i in range(GROUPS, GROUPS + depth):
                body(i, lambda d, i=i: i - d < GROUPS, i % 2)

        def segments(eng, depth, body):
            def step(q, r, live):
                body(live, lambda d: (YIN * q + (r - d), (r - d) % YIN, q if r >= d else q - 1,
                                      (r - d) % OUTS, YIN // OUTS * q + (r - d) // OUTS))
            for r in range(YIN):
                step(0, r, lambda d, r=r: d <= r)
            with eng.Fori(1, FSEGS // YIN) as q:
                for r in range(YIN):
                    step(q, r, lambda d: True)
            for r in range(depth):
                step(FSEGS // YIN, r, lambda d, r=r: d > r)

        LN_LAST = 1 + 2 * LAYERS + 1

        def h_keys(l, g):
            return l * (3 * GROUPS) + g

        def h_attn(l, g):
            return l * (3 * GROUPS) + (g + GROUPS)

        def h_mlp(l, g):
            return l * (3 * GROUPS) + (g + 2 * GROUPS)

        def chunks(b, k=KC, n=GT):
            return b[:, 0:k * n].rearrange("p (k n) -> p k n", k=k)

        def pair(t, g, n=D):
            return t[:, bass.ds(g * PAIR, PAIR), 0:n]

        def f32(ap):
            return ap.bitcast(F32)

        def load_segment(eng, n, slot):
            first = eng.value_load(efirst_i[0:1, bass.ds(n, 1)], min_val=0, max_val=(ETILES - 1) * SEG)
            if not (isinstance(n, int) and n < RIN):
                eng.wait_ge(s_lo, n - (RIN - 1))
                eng.wait_ge(s_kb, n - (RIN - 1))
            eng.dma_start(rows_in[slot][:, :, :],
                          edges_sorted[bass.ds(first, SEG), :].rearrange("(p r) c -> p r c", r=SEGR)).then_inc(S_IN[slot], 16)

        block = ctx.enter_context(nc.Block())

        @block.sync
        def _(sp):
            sp.dma_start(src_i[:, :], src.rearrange("(p c) -> p c", c=ECOL)).then_inc(src_loaded, 16)
            r = 0
            for a, n in ((ln1_g, ROWS_LN), (ln1_b, ROWS_LN), (ln2_g, ROWS_LN), (ln2_b, ROWS_LN), (mb1, LAYERS * FC)):
                sp.dma_start(colrows[r:r + n, :], a.rearrange("l (c f) -> (l c) f", f=128)).then_inc(rows_loaded, 16)
                r += n
            sp.dma_start(colrows[r:r + GHC, :], gb1.rearrange("(c f) -> c f", f=128)).then_inc(rows_loaded, 16)
            sp.dma_start(colrows[r + GHC:r + GHC + 1, :], u[0:1, :]).then_inc(rows_loaded, 16)
            sp.dma_start(res[:, :, 0:D], x_rows).then_inc(x_loaded, 16)

            def weights(w, l, n):
                return w[bass.ds(l, 1), :, :].rearrange("l (k p) n -> p (l k) n", p=128)

            with sp.Fori(0, LAYERS) as l:
                sp.wait_ge(w2_hi, l)
                sp.wait_ge(w2_lo, l)
                raw_qk = raw[:, 0:KC * 2 * D].rearrange("p (k n) -> p k n", k=KC)
                sp.dma_start(raw_qk[:, :, 0:D], weights(Wq, l, D)).then_inc(w_qk, 16)
                sp.dma_start(raw_qk[:, :, D:2 * D], weights(Wk, l, D)).then_inc(w_qk, 16)
                sp.wait_ge(ctx_pe, 5 * l)
                sp.dma_start(raw_vo[:, 0, :, :], weights(Wv, l, D)).then_inc(w_vo, 16)
                sp.dma_start(raw_vo[:, 1, :, :], weights(Wo, l, D)).then_inc(w_vo, 16)
                sp.wait_ge(qk_hi, l + 1)
                sp.wait_ge(qk_lo, l + 1)
                sp.dma_start(raw[:, :].rearrange("p (k n) -> p k n", k=KC), weights(mW1, l, FF)).then_inc(w_1, 16)
                sp.wait_ge(b_x2, l * (2 * GROUPS))
                sp.dma_start(bo_b[:, :], bo[bass.ds(l, 1), :].to_broadcast((128, D))).then_inc(w_bias, 16)
                sp.dma_start(b2_b[:, :], mb2[bass.ds(l, 1), :].to_broadcast((P, D))).then_inc(w_bias, 16)
                sp.wait_ge(w1_hi, l + 1)
                sp.wait_ge(w1_lo, l + 1)
                sp.dma_start(raw[:, :].rearrange("p (k n) -> p k n", k=FC), weights(mW2, l, D)).then_inc(w_2, 16)

            sp.wait_ge(b_x2, 2 * LAYERS * GROUPS)
            sp.wait_ge(ln_stats, LN_LAST)
            sp.wait_ge(r_table, 1)
            for slot in range(2):
                sp.wait_ge(SCATTERED[slot], 16 * CH * (CHUNKS // 2))
            sp.wait_ge(spare_written, 16)

            for n in range(RIN):
                load_segment(sp, n, n)
            sp.dma_start(raw_g1[:, 0:2, :], gW1[0:D, :].rearrange("(k p) n -> p k n", p=128)).then_inc(gw_raw, 16)
            sp.dma_start(raw_g1[0:EA, 2, :], gW1[D:D + EA, :]).then_inc(gw_raw, 16)
            sp.dma_start(raw_gu[:, :], gW1[D + EA:D + EA + GLOB, :]).then_inc(gw_raw, 16)
            sp.dma_start(raw_g2[:, :, :], gW2.rearrange("(k p) n -> p k n", p=128)).then_inc(gw_raw, 16)
            sp.dma_start(gb2_b[:, :], gb2.rearrange("(a n) -> a n", a=1).to_broadcast((P, D))).then_inc(gw_raw, 16)
            sp.dma_start(rb_b[:, :], rb.rearrange("(a n) -> a n", a=1).to_broadcast((P, EXP))).then_inc(rw_raw, 16)

            for k in range(KC):
                sp.dma_start(fw1[:, k, :].rearrange("p (e h) -> p e h", h=EH),
                             fW1[:, k * 128:(k + 1) * 128, :].rearrange("e p h -> p e h")).then_inc(f_w, 16)

            with sp.Fori(1, ESEGS // RIN) as q:
                for slot in range(0, RIN, 2):
                    load_segment(sp, RIN * q + slot, slot)
            load_segment(sp, ESEGS - 1, 0)

            sp.wait_ge(s_lo, ESEGS)
            sp.wait_ge(s_kb, ESEGS)

            def load_x(g, slot):
                sp.dma_start(x_in[:, slot, :, :], x_rows[:, bass.ds(g * PAIR, PAIR), :]).then_inc(N_IN[slot], 16)
            load_x(0, 0)
            load_x(1, 1)
            sp.dma_start(rw_in, rw).then_inc(rw_raw, 16)
            sp.wait_ge(s_pe, ESEGS)
            sp.dma_start(fw2[0:EH, :].rearrange("p (e h) -> p e h", h=D), fW2.rearrange("e p h -> p e h")).then_inc(f_w, 16)
            sp.dma_start(fw2[EH:EH + 1, :], fb2.rearrange("(a e) h -> a (e h)", a=1)).then_inc(f_w, 16)
            with sp.Fori(1, GROUPS // 2) as q:
                for slot in range(2):
                    sp.wait_ge(n_x, 2 * (2 * q + (slot - 1)) - 1)
                    sp.wait_ge(n_xn, 2 * q + (slot - 1))
                    load_x(2 * q + slot, slot)
            sp.wait_ge(n_x, 2 * (GROUPS - 2) - 1)
            sp.wait_ge(n_xn, GROUPS - 2)
            load_x(GROUPS - 1, 0)

            sp.wait_ge(n_top, 6 * GROUPS)
            sp.dma_start(fb1_r[:, :], fb1).then_inc(f_w, 16)

            sp.wait_ge(f_scat, 16 * TILES)
            sp.wait_ge(r_table, 2)

            def load_tokens(n, slot):
                first = sp.value_load(ffirst_i[0:1, bass.ds(n, 1)], min_val=0, max_val=N - P)
                rows = tokens_sorted[bass.ds(first, P), :]
                if not isinstance(n, int):
                    used, placed = counted(sp, n - (YIN - 1)), counted(sp, 2 * (n - (YIN - 1)))
                    sp.wait_ge(f_row, used)
                    sp.wait_ge(f_idx, placed)
                sp.dma_start(yin[slot][:, :], rows).then_inc(F_IN[slot], 16)
            for n in range(YIN):
                load_tokens(n, n)
            with sp.Fori(1, FSEGS // YIN) as q:
                for slot in range(YIN):
                    load_tokens(YIN * q + slot, slot)

        @block.gpsimd
        def _(pool):
            nc.gpsimd.memset(ones[:, :], 1.0).then_inc(consts, 1)
            nc.gpsimd.memset(blockmask[:, :], 0.0).then_inc(consts, 1)
            nc.gpsimd.memset(stage[:, 0, :, :], 0.0).then_inc(consts, 1)
            pool.wait_ge(consts, 3)
            nc.gpsimd.affine_select(out=ident[:, :], in_=ones[:, :], compare_op=ALU.is_equal, fill=0.0,
                                    base=0, pattern=[[-1, 128]], channel_multiplier=1).then_inc(consts, 1)
            nc.gpsimd.affine_select(out=tri[:, :], in_=ones[:, :], compare_op=ALU.is_gt, fill=0.0,
                                    base=0, pattern=[[1, 128]], channel_multiplier=-1).then_inc(consts, 1)
            pool.wait_ge(consts, 5)
            for h in range(128 // DH):
                nc.gpsimd.memset(blockmask[h * DH:(h + 1) * DH, h * DH:(h + 1) * DH], 1.0).then_inc(consts, 1)
            pool.wait_ge(consts, 5 + 128 // DH)
            for tile, pattern, mult in ((iota_node, [[TILES, P]], 0), (iota_seg, [[1, ESEGS]], 0), (iota_part, [[1, 1]], 1)):
                nc.gpsimd.iota(tile[:, :], pattern=pattern, base=0, channel_multiplier=mult,
                               allow_small_or_imprecise_dtypes=True).then_inc(consts, 1)
            nc.gpsimd.memset(stage[:, 0, :, EA:ROW], -1.0).then_inc(spare_rows, 1)
            pool.wait_ge(spare_rows, 1)
            pool.dma_start(edges_sorted[EDGES:ETILES * SEG, :].rearrange("(p r) c -> p r c", r=SPARE // SPARE_P),
                           stage[0:SPARE_P, 0, 0:SPARE // SPARE_P, :]).then_inc(spare_written, 16)
            pool.wait_ge(spare_written, 16)

            def load_attr(c, slot):
                pool.dma_start(stage[:, slot, :, 0:EA], edge_rows[:, bass.ds(c * CH, CH), :]).then_inc(ATTR[slot], 16)

            def scatter(q, slot):
                c = 2 * q + slot
                nc.gpsimd.tensor_copy(idx[:, slot, :], pos_i[:, bass.ds(c * CH, CH)]).then_inc(key_staged, 1)
                nc.gpsimd.tensor_copy(stage[:, slot, :, EA], src_f[:, bass.ds(c * CH, CH)]).then_inc(key_staged, 1)
                staged, loaded = counted(pool, 2 * c + 2), counted(pool, 16 * q + 16)
                pool.wait_ge(pos_ready, 1)
                pool.wait_ge(key_staged, staged)
                pool.wait_ge(ATTR[slot], loaded)
                for j in range(CH):
                    nc.gpsimd.indirect_dma_start(
                        out=edges_sorted, out_offset=bass.IndirectOffsetOnAxis(ap=idx[:, slot, j:j + 1], axis=0),
                        in_=stage[:, slot, j, :], in_offset=None).then_inc(SCATTERED[slot], 16)

            nc.gpsimd.memset(pos_f, 0.0).then_inc(e_acc, 1)

            def place(b, slot):
                pool.wait_ge(e_rank, b + 1)
                nc.gpsimd.tensor_tensor(krank[slot][:, :], krank[slot][:, :], kmask[slot][:, :], ALU.mult).then_inc(e_mul, 1)
                pool.wait_ge(e_acc, b + 1)
                pool.wait_ge(e_mul, b + 1)
                nc.gpsimd.tensor_tensor(pos_f, pos_f, krank[slot][:, :], ALU.add).then_inc(e_acc, 1)
            with pool.Fori(0, TILES // 2) as q:
                for slot in range(2):
                    place(2 * q + slot, slot)
            pool.wait_ge(pos_ready, 1)
            load_attr(0, 0)
            load_attr(1, 1)
            scatter(0, 0)
            scatter(0, 1)
            with pool.Fori(1, CHUNKS // 2) as q:
                for slot in range(2):
                    pool.wait_ge(SCATTERED[slot], 16 * CH * q)
                    load_attr(2 * q + slot, slot)
                for slot in range(2):
                    scatter(q, slot)

            pool.wait_ge(r_table, 1)
            pool.wait_ge(b_x2, 2 * LAYERS * GROUPS)
            pool.wait_ge(ln_stats, LN_LAST)
            nc.gpsimd.memset(agg[:, :, :], 0.0).then_inc(s_ones, 1)

            def seg_low(n, slot, turn):
                loaded, used = counted(pool, 16 * turn + 16), counted(pool, n - 3)
                tile = ekind[:, bass.ds(n, 1)].to_broadcast((128, SEGR))
                pool.wait_ge(spare_written, 16)
                pool.wait_ge(S_IN[slot], loaded)
                if not (isinstance(n, int) and n < 4):
                    pool.wait_ge(s_oh, used)
                nc.gpsimd.tensor_tensor(kb[:, slot % 4, :], rows_in[slot][:, :, EA], tile, ALU.subtract).then_inc(s_kb, 1)
                if not (isinstance(n, int) and n < 4):
                    pool.wait_ge(s_pe, n - 3)
                pool.wait_ge(s_hi, n + 1)
                nc.gpsimd.tensor_tensor(ehl[slot % 4][:, :, EA + 2:2 * EA + 2], rows_in[slot][:, :, 0:EA],
                                        f32(ehl[slot % 4][:, :, 0:EA]), ALU.subtract).then_inc(s_lo, 1)
            for n in range(RIN):
                seg_low(n, n, 0)
            with pool.Fori(1, ESEGS // RIN) as q:
                for slot in range(RIN):
                    seg_low(RIN * q + slot, slot, q)
            seg_low(ESEGS - 1, 0, ESEGS // RIN)

            nc.gpsimd.iota(res[:, :, D + 2], pattern=[[1, TILES]], base=0, channel_multiplier=TILES,
                           allow_small_or_imprecise_dtypes=True).then_inc(f_ones, 1)
            pool.wait_ge(f_ones, 1)
            pool.wait_ge(f_posi, 1)
            for t in range(TILES):
                nc.gpsimd.indirect_dma_start(
                    out=tokens_sorted, out_offset=bass.IndirectOffsetOnAxis(ap=fpos_i[:, t:t + 1], axis=0),
                    in_=res[:, t, :], in_offset=None).then_inc(f_scat, 16)

            def put(n, slot):
                rows, places = counted(pool, n + 1), counted(pool, 2 * n + 2)
                pool.wait_ge(f_scat, 16 * TILES)
                pool.wait_ge(f_row, rows)
                pool.wait_ge(f_idx, places)
                nc.gpsimd.indirect_dma_start(
                    out=out, out_offset=bass.IndirectOffsetOnAxis(ap=oidx[slot][:, :], axis=0),
                    in_=orow[slot][:, :], in_offset=None, bounds_check=N - 1, oob_is_err=False).then_inc(F_OUT[slot], 16)
            with pool.Fori(0, FSEGS // OUTS) as q:
                for slot in range(OUTS):
                    put(OUTS * q + slot, slot)
            for slot in range(OUTS):
                pool.wait_ge(F_OUT[slot], 16 * (FSEGS // OUTS))

        @block.scalar
        def _(act):
            def ident_act(o, i, **kw):
                return nc.scalar.activation(o, i, ACT.Identity, **kw)

            def normalise(o, st, g, done):
                for j in range(PAIR):
                    t = g * PAIR + j
                    a = ident_act(o[:, j, :], res[:, bass.ds(t, 1), 0:D].rearrange("p a d -> p (a d)"),
                                  scale=st[:, bass.ds(t, 1), 0:1].rearrange("p a d -> p (a d)"),
                                  bias=st[:, bass.ds(t, 1), 1:2].rearrange("p a d -> p (a d)"))
                a.then_inc(done, 1)

            def split_hi(o, i, loaded, count, done):
                act.wait_ge(loaded, count)
                nc.scalar.copy(o, i).then_inc(done, 1)

            act.wait_ge(consts, NCONST)
            act.wait_ge(cols_T, 1)
            nc.scalar.copy(cols[:, :], PS[:, 0:NROW]).then_inc(cols_ready, 1)

            act.wait_ge(ln_stats, 1)
            with act.Fori(0, GROUPS) as g:
                for j in range(PAIR):
                    t = g * PAIR + j
                    row = res[:, bass.ds(t, 1), 0:D].rearrange("p a d -> p (a d)")
                    a = ident_act(row, row, scale=xst[:, bass.ds(t, 1), 0:1].rearrange("p a d -> p (a d)"),
                                  bias=xst[:, bass.ds(t, 1), 1:2].rearrange("p a d -> p (a d)"))
                a.then_inc(xs_norm, 1)

            with act.Fori(0, LAYERS) as l:
                act.wait_ge(b_x2, l * (2 * GROUPS))
                split_hi(wqk[0][:, :, :], raw[:, 0:KC * 2 * D].rearrange("p (k n) -> p k n", k=KC), w_qk, 32 * l + 32, qk_hi)

                def affine_of(col, n):
                    act.wait_ge(h_T, n + 1)
                    act.wait_ge(h_lo, n)
                    for k in range(KC):
                        a = ident_act(affine[:, k, :], chunks(PT)[:, k, :], scale=lcol[:, col + k:col + k + 1],
                                      bias=lcol[:, col + KC + k:col + KC + k + 1])
                    a.then_inc(h_aff, 1)

                def h_high(n, read, count):
                    act.wait_ge(h_aff, n + 1)
                    act.wait_ge(read, count)
                    nc.scalar.copy(hT[0][:, :, :], affine[:, :, :]).then_inc(h_hi, 1)

                act.wait_ge(lcol_ready, 4 * l + 4)
                act.wait_ge(ln_stats, 2 * l + 2)

                def keys(i, live, par):
                    if live(0):
                        act.wait_ge(h_T, h_keys(l, i))
                        normalise(xh[0], lnst, i, h_xh)
                    if live(1):
                        act.wait_ge(h_aff, h_keys(l, i - 1) + 1)
                        if live(3):
                            act.wait_ge(a_K, l * GROUPS + (i - 2))
                        nc.scalar.copy(hTk[(par - 1) % 2][0][:, :, :], affine[:, :, :]).then_inc(h_hi, 1)
                    if live(2):
                        n = l * GROUPS + (i - 2)
                        act.wait_ge(a_K, n + 1)
                        nc.scalar.copy(pair(ksb, i - 2), PQ[0:P, :].rearrange("p (j d) -> p j d", j=PAIR)).then_inc(a_ks, 1)
                key_pipeline(act, 2, keys)

                split_hi(w1[0][:, :, :], raw[:, :].rearrange("p (k n) -> p k n", k=KC), w_1, 16 * l + 16, w1_hi)
                act.wait_ge(ctx_pe, 5 * l + 2)
                nc.scalar.copy(mbc[:, :], PS[0:P, 0:D]).then_inc(c_mbc, 1)

                def key_exp(g, slot):
                    n = l * GROUPS + g
                    if not isinstance(g, int):
                        act.wait_ge(g_pe, n - 1)
                    normalise(xh[slot], lnst, g, g_xh)
                    act.wait_ge(g_dk, n + 1)
                    nc.scalar.activation(ek[:, slot, :, :], ek[:, slot, :, :], ACT.Exp, scale=SCALE).then_inc(g_ek, 1)
                key_exp(0, 0)
                with act.Fori(0, GROUPS // 2) as q:
                    key_exp(2 * q + 1, 1)
                    key_exp(2 * q + 2, 0)

                split_hi(w2[0][:, :, :], raw[:, :].rearrange("p (k n) -> p k n", k=FC), w_2, 16 * l + 16, w2_hi)
                act.wait_ge(ctx_dve, 9 * l + 9)
                nc.scalar.copy(mmat[0][:, :, :], mprod[:, :, :]).then_inc(d_hi, 1)

                def attend(i, live):
                    if live(1):
                        affine_of(0, h_attn(l, i - 1))
                        h_high(h_attn(l, i - 1), b_Q, l * GROUPS + (i - 1))
                    if live(2):
                        act.wait_ge(b_soft, 5 * (l * GROUPS + (i - 2)) + 2)
                        nc.scalar.activation(qd[:, :, :], qd[:, :, :], ACT.Exp, scale=SCALE).then_inc(b_qe, 1)
                    if live(4):
                        act.wait_ge(b_M, l * GROUPS + (i - 4) + 1)
                        nc.scalar.copy(pair(res, i - 4), PM[0:P, :].rearrange("p (j d) -> p j d", j=PAIR)).then_inc(b_x1, 1)
                    if live(3):
                        n = l * GROUPS + (i - 3)
                        act.wait_ge(b_qT, n + 1)
                        act.wait_ge(b_M, n)
                        nc.scalar.copy(qT[0][:, :, :], chunks(PQT)).then_inc(b_qhi, 1)
                    if live(0):
                        act.wait_ge(h_T, h_attn(l, i))
                        normalise(xh[0], lnst, i, h_xh)
                pipeline(act, 4, attend)

                act.wait_ge(ln_stats, 2 * l + 3)

                def mlp(i, live):
                    n2 = l * GROUPS + (i - 2)

                    def gelu(c):
                        if c >= 2 or live(3):
                            act.wait_ge(b_Y, 4 * n2 + c - 1)
                        act.wait_ge(b_H, 4 * n2 + c + 1)
                        for j in range(2):
                            a = nc.scalar.activation(hid[c % 2][:, j, :], chunks(PH[c % 2])[:, j, :], ACT.Gelu,
                                                     bias=lcol[:, 4 * KC + 2 * c + j:4 * KC + 2 * c + j + 1])
                        a.then_inc(b_gelu, 1)
                        act.wait_ge(b_gelu, 4 * n2 + c + 1)
                        nc.scalar.copy(hidh[c % 2][0][:, :, :], hid[c % 2][:, :, :]).then_inc(b_hhi, 1)
                    if live(2):
                        gelu(0)
                        gelu(1)
                    if live(1):
                        affine_of(2 * KC, h_mlp(l, i - 1))
                    if live(0):
                        act.wait_ge(h_T, h_mlp(l, i))
                        normalise(xh[0], lnst, i, h_xh)
                    if live(2):
                        gelu(2)
                    if live(1):
                        h_high(h_mlp(l, i - 1), b_H, 4 * (l * GROUPS + (i - 1)))
                    if live(2):
                        gelu(3)
                pipeline(act, 3, mlp)

            def seg_hi(n, slot, turn):
                act.wait_ge(S_IN[slot], 16 * turn + 16)
                if not (isinstance(n, int) and n < 4):
                    act.wait_ge(s_pe, n - 3)
                nc.scalar.copy(ehl[slot % 4][:, :, 0:EA], rows_in[slot][:, :, 0:EA]).then_inc(s_hi, 1)
            def seg_ahead(n, slot):
                if slot % 2 == 0:
                    load_segment(act, n + AHEAD, (slot + AHEAD) % RIN)
            for n in range(RIN):
                seg_hi(n, n, 0)
                if n + AHEAD > RIN:
                    seg_ahead(n, n)
            with act.Fori(1, ESEGS // RIN - 1) as q:
                for slot in range(RIN):
                    seg_hi(RIN * q + slot, slot, q)
                    seg_ahead(RIN * q + slot, slot)
            for n in range(ESEGS - 1 - RIN, ESEGS):
                seg_hi(n, n % RIN, n // RIN)
                if n + AHEAD < ESEGS - 1:
                    seg_ahead(n, n % RIN)

            act.wait_ge(gw_raw, 80)
            nc.scalar.copy(g1[0][:, 0:2, :], raw_g1[:, 0:2, :]).then_inc(gw_hi, 1)
            nc.scalar.copy(g1[0][0:EA, 2, :], raw_g1[0:EA, 2, :]).then_inc(gw_hi, 1)
            nc.scalar.copy(g2[0][:, :, :], raw_g2[:, :, :]).then_inc(gw_hi, 1)
            act.wait_ge(rw_T, 1)
            nc.scalar.copy(rwT[:, :, :], chunks(PT, KC, EXP)).then_inc(rw_ready, 1)

            def graph(i, live):
                if live(2):
                    for c in range(2):
                        act.wait_ge(n_H, 2 * (i - 2) + c + 1)
                        if live(3):
                            act.wait_ge(n_hlo, 2 * (i - 3) + c + 1)
                        for j in range(2):
                            a = nc.scalar.activation(ghid[c][:, j, :], chunks(PH[c])[:, j, :], ACT.Relu,
                                                     bias=g1col[:, 2 * c + j:2 * c + j + 1])
                        a.then_inc(n_relu, 1)
                if live(1):
                    act.wait_ge(n_T, i)
                    act.wait_ge(n_H, 2 * (i - 1))
                    nc.scalar.copy(cT[0][:, 0:2, :], chunks(PT)).then_inc(n_hi, 1)
                    nc.scalar.copy(cT[0][0:EA, 2, :], PS[0:EA, 0:GT]).then_inc(n_hi, 1)
                if live(0):
                    act.wait_ge(n_T, i)
                    for slot in range(2):
                        act.wait_ge(N_IN[slot], 16 * ((i + 2 - slot) // 2))
                    for j in range(PAIR):
                        xin = x_in[:, bass.ds(i % 2, 1), j, :].rearrange("p a d -> p (a d)")
                        t = i * PAIR + j
                        a = ident_act(xn[:, j, :], xin, scale=xst[:, bass.ds(t, 1), 0:1].rearrange("p a d -> p (a d)"),
                                      bias=xst[:, bass.ds(t, 1), 1:2].rearrange("p a d -> p (a d)"))
                    a.then_inc(n_xn, 1)
                if live(2):
                    for c in range(2):
                        act.wait_ge(n_relu, 2 * (i - 2) + c + 1)
                        if live(3):
                            act.wait_ge(n_Y, 2 * (i - 3) + c + 1)
                        nc.scalar.copy(ghh[c][0][:, :, :], ghid[c][:, :, :]).then_inc(n_hhi, 1)
            pipeline(act, 3, graph)

            act.wait_ge(ln_stats, LN_LAST + 1)

            def route(i, live):
                if live(0):
                    act.wait_ge(n_zT, i)
                    for j in range(PAIR):
                        row = res[:, bass.ds(i * PAIR + j, 1), :].rearrange("p a d -> p (a d)")
                        a = ident_act(zt[:, j, :], row[:, 0:D], scale=row[:, D:D + 1], bias=row[:, D + 1:D + 2])
                    a.then_inc(n_z, 1)
                if live(1):
                    act.wait_ge(n_zT, i)
                    act.wait_ge(n_log, i - 1)
                    nc.scalar.copy(zT[:, :, :], chunks(PQ)).then_inc(n_zTs, 1)
            pipeline(act, 1, route)

            def expert(live, seg):
                if live(3):
                    n = seg(3)[0]
                    e = act.value_load(fkind_i[0:1, bass.ds(n, 1)], min_val=0, max_val=EXP - 1)
                    transposed, used = counted(act, n + 1), counted(act, n)
                    act.wait_ge(f_bT, 1)
                    act.wait_ge(f_hT, transposed)
                    act.wait_ge(f_o, used)
                    nc.scalar.activation(hsT[0:EH, :], PQT[0:EH, 0:P], ACT.Relu, bias=fb1T[:, bass.ds(e, 1)]).then_inc(f_hTs, 1)
                if live(2):
                    n = seg(2)[0]
                    act.wait_ge(f_h, n + 1)
                    act.wait_ge(f_hT, n)
                    nc.scalar.copy(hs[:, :], PM[0:P, 0:EH]).then_inc(f_hs, 1)
                if live(0):
                    n, slot, turn, _, _ = seg(0)
                    act.wait_ge(F_IN[slot], 16 * turn + 16)
                    act.wait_ge(f_T, n)
                    y = yin[slot]
                    ident_act(zs[:, :], y[:, 0:D], scale=y[:, D:D + 1], bias=y[:, D + 1:D + 2]).then_inc(f_z, 1)
            act.wait_ge(f_bT, 1)
            act.wait_ge(n_top, 6 * GROUPS)
            nc.scalar.copy(fb1T[:, :], PH0[0:EH, 0:EXP]).then_inc(f_bTs, 1)
            act.wait_ge(f_bTs, 1)
            act.wait_ge(r_table, 2)
            segments(act, 3, expert)

        @block.vector
        def _(dve):
            def moments(tiles, t):
                for j in range(PAIR):
                    nc.vector.bn_stats(bn[:, bass.ds(t + j, 1), :].rearrange("p a d -> p (a d)"), tiles[j]).then_inc(ln_st, 1)

            def rstd_all(o, seq):
                steps = [0]

                def step(instruction):
                    instruction.then_inc(ln_step, 1)
                    steps[0] += 1

                def stepped(n=None):
                    dve.wait_ge(ln_step, LN_STEPS * seq + (n or steps[0]))
                two_mean, half_diff, m2, diff2, var_sum, var = (lnt[:, r, :] for r in range(6))
                dve.wait_ge(ln_st, TILES * (seq + 1))
                step(nc.vector.tensor_tensor(two_mean, bn[:, :, 1], bn[:, :, 4], ALU.add))
                step(nc.vector.tensor_tensor(half_diff, bn[:, :, 1], bn[:, :, 4], ALU.subtract))
                step(nc.vector.tensor_tensor(m2, bn[:, :, 2], bn[:, :, 5], ALU.add))
                stepped(2)
                step(nc.vector.tensor_tensor(diff2, half_diff, half_diff, ALU.mult))
                stepped()
                step(nc.vector.scalar_tensor_tensor(out=var_sum, in0=diff2, scalar=D / 4.0, in1=m2, op0=ALU.mult, op1=ALU.add))
                stepped()
                step(nc.vector.tensor_scalar(var, var_sum, 1.0 / D, EPS, ALU.mult, ALU.add))
                stepped()
                step(nc.vector.tensor_scalar(lnt_i[:, :], var.bitcast(I32), 1, None, ALU.logical_shift_right))
                stepped()
                y = lnt[:, 6, :]
                step(nc.vector.tensor_scalar(y.bitcast(I32), lnt_i[:, :], -1.0, RSQRT_MAGIC, ALU.mult, ALU.add))
                for r in range(3):
                    vy, h, y_next = lnt[:, 1, :], lnt[:, 2, :], (lnt[:, 7, :], lnt[:, 6, :], o[:, :, 0])[r]
                    stepped()
                    step(nc.vector.tensor_tensor(vy, var, y, ALU.mult))
                    stepped()
                    step(nc.vector.scalar_tensor_tensor(out=h, in0=vy, scalar=-0.5, in1=y, op0=ALU.mult, op1=ALU.mult))
                    stepped()
                    step(nc.vector.scalar_tensor_tensor(out=y_next, in0=h, scalar=1.5, in1=y, op0=ALU.add, op1=ALU.mult))
                    y = y_next
                stepped()
                assert steps[0] == LN_STEPS
                nc.vector.scalar_tensor_tensor(out=o[:, :, 1], in0=two_mean, scalar=-0.5, in1=o[:, :, 0],
                                               op0=ALU.mult, op1=ALU.mult).then_inc(ln_stats, 1)

            def tile_rows(t, g):
                return [t[:, bass.ds(g * PAIR + j, 1), 0:D].rearrange("p a d -> p (a d)") for j in range(PAIR)]

            def split_lo(o, i, hi, count, done):
                dve.wait_ge(done[0], count)
                nc.vector.tensor_tensor(o, i, f32(hi), ALU.subtract).then_inc(done[1], 1)

            def kind_tables(nk, width, segs, kind, kind_int, first_int, turn):
                dve.wait_ge(sort_pe, 3 * turn + 1)
                nc.vector.tensor_copy(tot[:, 0:nk], PS[0:P, 64:64 + nk]).then_inc(sort_dve, 1)
                dve.wait_ge(sort_dve, SORT_DVE * turn + 1)
                nc.vector.tensor_tensor_scan(totinc[:, 0:nk], ones[0:P, 0:nk], tot[:, 0:nk], 0.0, ALU.mult, ALU.add).then_inc(sort_dve, 1)
                dve.wait_ge(sort_dve, SORT_DVE * turn + 2)
                nc.vector.tensor_tensor(base[:, 0:nk], totinc[:, 0:nk], tot[:, 0:nk], ALU.subtract).then_inc(sort_dve, 1)
                dve.wait_ge(sort_dve, SORT_DVE * turn + 3)
                nc.vector.tensor_tensor(base[:, 0:nk], base[:, 0:nk], PS[0:P, 0:nk], ALU.add).then_inc(sort_dve, 1)
                nc.vector.tensor_copy(kcol[0:nk, 0:1], PS[0:nk, 128:129]).then_inc(sort_dve, 1)
                dve.wait_ge(sort_dve, SORT_DVE * turn + 4)
                dve.wait_ge(sort_pe, 3 * turn + 2)
                nc.vector.tensor_scalar(kcol[0:nk, 1:2], PS[0:nk, 130:131], 1.0 / width, 0.5 / width - 0.5, ALU.mult, ALU.add).then_inc(sort_dve, 1)
                dve.wait_ge(sort_dve, SORT_DVE * turn + 6)
                nc.vector.tensor_scalar(kcol[0:nk, 2:3], kcol[0:nk, 1:2], RND, None, ALU.add).then_inc(sort_dve, 1)
                dve.wait_ge(sort_dve, SORT_DVE * turn + 7)
                nc.vector.tensor_scalar(kcol[0:nk, 3:4], kcol[0:nk, 2:3], -RND, None, ALU.add).then_inc(sort_dve, 1)
                dve.wait_ge(sort_dve, SORT_DVE * turn + 8)
                nc.vector.tensor_tensor(kcol[0:nk, 1:2], kcol[0:nk, 3:4], iota_part[0:nk, :], ALU.add).then_inc(sort_dve, 1)
                dve.wait_ge(sort_dve, SORT_DVE * turn + 9)
                nc.vector.tensor_scalar(cmp[0:nk, 0:segs], iota_seg[0:nk, 0:segs], kcol[0:nk, 1:2], None, ALU.is_ge).then_inc(sort_dve, 1)
                dve.wait_ge(sort_pe, 3 * turn + 3)
                nc.vector.tensor_scalar(kind[:, 0:segs], PS[:, 0:segs], -1.0, None, ALU.add).then_inc(sort_dve, 1)
                dve.wait_ge(sort_dve, SORT_DVE * turn + 11)
                nc.vector.tensor_copy(kind_int[:, 0:segs], kind[0:1, 0:segs]).then_inc(sort_dve, 1)
                nc.vector.tensor_tensor(segtmp[:, 0:segs], iota_seg[0:1, 0:segs], kind[0:1, 0:segs], ALU.subtract).then_inc(sort_dve, 1)
                dve.wait_ge(sort_dve, SORT_DVE * turn + 12)
                dve.wait_ge(sort_dve, SORT_DVE * turn + 13)
                nc.vector.tensor_scalar(first_int[:, 0:segs], segtmp[:, 0:segs], float(width), None, ALU.mult).then_inc(r_table, 1)

            def count_edges(first, last):
                with dve.Fori(first, last) as b:
                    dve.wait_ge(r_cnt, b)
                    nc.vector.tensor_scalar(scr[0][:, :], tile_of, iota_seg[0:P, bass.ds(b, 1)], 0.0, ALU.is_equal, ALU.add,
                                            accum_out=cnt[:, bass.ds(b, 1)]).then_inc(r_cnt, 1)

            dve.wait_ge(consts, NCONST)
            dve.wait_ge(src_loaded, 16)
            nc.vector.tensor_copy(src_f[:, :], src_i[:, :]).then_inc(e_conv, 1)
            dve.wait_ge(e_conv, 1)
            nc.vector.tensor_scalar(scr[0][:, :], src_f[:, :], 1.0 / TILES, 0.5 / TILES - 0.5, ALU.mult, ALU.add).then_inc(e_conv, 1)
            dve.wait_ge(e_conv, 2)
            nc.vector.tensor_scalar(scr[1][:, :], scr[0][:, :], RND, None, ALU.add).then_inc(e_conv, 1)
            dve.wait_ge(e_conv, 3)
            nc.vector.tensor_scalar(scr[2][:, :], scr[1][:, :], -RND, None, ALU.add).then_inc(e_conv, 1)
            dve.wait_ge(e_conv, 4)
            nc.vector.scalar_tensor_tensor(out=tile_of, in0=scr[2][:, :], scalar=-float(TILES), in1=src_f[:, :],
                                           op0=ALU.mult, op1=ALU.add).then_inc(e_conv, 1)
            dve.wait_ge(e_conv, 5)
            count_edges(0, TILES // 2)

            dve.wait_ge(x_loaded, 16)
            with dve.Fori(0, GROUPS) as g:
                moments(tile_rows(res, g), g * PAIR)
            rstd_all(xst, 0)
            dve.wait_ge(ln_stats, 1)
            count_edges(TILES // 2, TILES)
            kind_tables(TILES, SEG, ESEGS, ekind, ekind_i, efirst_i, 0)
            with dve.Fori(0, GROUPS) as g:
                normalised = counted(dve, g + 1)
                dve.wait_ge(x_loaded, 16)
                dve.wait_ge(xs_norm, normalised)
                moments(tile_rows(res, g), g * PAIR)
            rstd_all(lnst, 1)
            dve.wait_ge(cols_ready, 1)

            def add_rows(g, what, done):
                nc.vector.tensor_tensor(pair(res, g), pair(res, g), what, ALU.add).then_inc(done, 1)

            def h_low(n, halves=hT):
                dve.wait_ge(h_hi, n + 1)
                nc.vector.tensor_tensor(halves[1][:, :, :], affine[:, :, :], f32(halves[0][:, :, :]), ALU.subtract).then_inc(h_lo, 1)

            def kind_mask(b, slot):
                if not (isinstance(b, int) and b < 2):
                    dve.wait_ge(e_acc, b)
                nc.vector.tensor_scalar(kmask[slot][:, :], tile_of, iota_seg[0:P, bass.ds(b, 1)], None, ALU.is_equal).then_inc(e_mask, 1)

            def kind_rank(b, slot):
                dve.wait_ge(e_mask, b + 1)
                nc.vector.tensor_tensor_scan(krank[slot][:, :], ones[0:P, 0:1].to_broadcast((P, ECOL)), kmask[slot][:, :],
                                             base[:, bass.ds(b, 1)], ALU.mult, ALU.add).then_inc(e_rank, 1)

            def layer(l, sorting):
                dve.wait_ge(b_x2, l * (2 * GROUPS))
                dve.wait_ge(b_gelu, 4 * (l * GROUPS))
                nc.vector.tensor_copy(lcol[:, 0:4 * KC].rearrange("p (w k) -> p w k", k=KC),
                                      cols[:, 0:4 * ROWS_LN].rearrange("p (w r) -> p w r", r=ROWS_LN)[:, :, bass.ds(l * KC, KC)]).then_inc(lcol_ready, 1)
                nc.vector.tensor_copy(lcol[:, 4 * KC:4 * KC + FC], cols[:, bass.ds(4 * ROWS_LN + l * FC, FC)]).then_inc(lcol_ready, 1)
                nc.vector.memset(kmax[:, :, :], -3.4e38).then_inc(lcol_ready, 1)
                nc.vector.memset(esum[:, :, :], 0.0).then_inc(lcol_ready, 1)
                split_lo(wqk[1][:, :, :], raw[:, 0:KC * 2 * D].rearrange("p (k n) -> p k n", k=KC), wqk[0][:, :, :], l + 1, (qk_hi, qk_lo))
                dve.wait_ge(lcol_ready, 4 * l + 4)

                def keys(i, live, par):
                    if live(1):
                        n = h_keys(l, i - 1)
                        dve.wait_ge(h_lo, n)
                        dve.wait_ge(h_T, n + 1)
                        for k in range(KC):
                            a = nc.vector.tensor_scalar(affine[:, k, :], chunks(PT)[:, k, :], lcol[:, k:k + 1],
                                                        lcol[:, KC + k:KC + k + 1], ALU.mult, ALU.add)
                        a.then_inc(h_aff, 1)
                    if live(3):
                        n = l * GROUPS + (i - 3)
                        dve.wait_ge(a_max, n)
                        dve.wait_ge(a_ks, n + 1)
                        nc.vector.tensor_tensor(kmax[:, :, :], kmax[:, :, :], pair(ksb, i - 3), ALU.max).then_inc(a_max, 1)
                    if live(1):
                        h_low(h_keys(l, i - 1), hTk[(par - 1) % 2])
                key_pipeline(dve, 3, keys)

                split_lo(w1[1][:, :, :], raw[:, :].rearrange("p (k n) -> p k n", k=KC), w1[0][:, :, :], l + 1, (w1_hi, w1_lo))
                dve.wait_ge(a_max, (l + 1) * GROUPS)
                nc.vector.tensor_tensor(km[:, :], kmax[:, 0, :], kmax[:, 1, :], ALU.max).then_inc(ctx_dve, 1)
                dve.wait_ge(ctx_pe, 5 * l + 1)
                nc.vector.tensor_reduce(mcol[:, :], chunks(PT, KC, P), AX, ALU.max).then_inc(ctx_dve, 1)
                dve.wait_ge(ctx_dve, 9 * l + 2)
                for k in range(KC):
                    a = nc.vector.tensor_scalar(dg[:, k, :], ident[:, :], mcol[:, k:k + 1], None, ALU.mult)
                a.then_inc(ctx_dve, 1)
                dve.wait_ge(c_mbc, l + 1)

                def key_exp(g, slot):
                    n = l * GROUPS + g
                    if not isinstance(g, int):
                        dve.wait_ge(g_esum, n - 1)
                        dve.wait_ge(g_pe, n - 1)
                    nc.vector.tensor_tensor(ek[:, slot, :, :], pair(ksb, g), mbc[:, :].unsqueeze(1).to_broadcast((P, PAIR, D)),
                                            ALU.subtract).then_inc(g_dk, 1)

                def add_exp(g, slot):
                    n = l * GROUPS + g
                    dve.wait_ge(g_ek, n + 1)
                    dve.wait_ge(g_esum, n)
                    nc.vector.tensor_tensor(esum[:, :, :], esum[:, :, :], ek[:, slot, :, :], ALU.add).then_inc(g_esum, 1)
                key_exp(0, 0)
                with dve.Fori(0, GROUPS // 2) as q:
                    key_exp(2 * q + 1, 1)
                    add_exp(2 * q, 0)
                    key_exp(2 * q + 2, 0)
                    add_exp(2 * q + 1, 1)
                add_exp(GROUPS - 1, 0)

                split_lo(w2[1][:, :, :], raw[:, :].rearrange("p (k n) -> p k n", k=FC), w2[0][:, :, :], l + 1, (w2_hi, w2_lo))
                dve.wait_ge(ctx_pe, 5 * l + 3)
                nc.vector.reciprocal(gn[:, 1, :], PS[:, 0:D]).then_inc(ctx_dve, 1)
                dve.wait_ge(ctx_dve, 9 * l + 4)
                dve.wait_ge(g_pe, (l + 1) * GROUPS)
                nc.vector.tensor_tensor(gn[:, 0, :], chunks(PQT, KC, D)[:, 0, :], gn[:, 1, :], ALU.mult).then_inc(ctx_dve, 1)
                nc.vector.tensor_tensor(gn[:, 1, :], chunks(PQT, KC, D)[:, 1, :], gn[:, 1, :], ALU.mult).then_inc(ctx_dve, 1)
                dve.wait_ge(ctx_dve, 9 * l + 6)
                for k in range(KC):
                    a = nc.vector.tensor_scalar(gn[:, k, :], gn[:, k, :], lcol[:, k:k + 1], lcol[:, KC + k:KC + k + 1], ALU.mult, ALU.add)
                a.then_inc(ctx_dve, 1)
                dve.wait_ge(ctx_pe, 5 * l + 4)
                nc.vector.tensor_tensor(ct[:, :, :], chunks(PM, KC, 128), blockmask[:, :].unsqueeze(1).to_broadcast((128, KC, 128)),
                                        ALU.mult).then_inc(ctx_dve, 1)
                dve.wait_ge(w_bias, 32 * l + 32)
                dve.wait_ge(ctx_pe, 5 * l + 5)
                nc.vector.scalar_tensor_tensor(out=mprod[:, :, :], in0=bo_b[:, :].unsqueeze(1).to_broadcast((128, KC, D)),
                                               scalar=1.0 / HEADS, in1=chunks(PS, KC, D), op0=ALU.mult, op1=ALU.add).then_inc(ctx_dve, 1)
                dve.wait_ge(d_hi, l + 1)
                nc.vector.tensor_tensor(mmat[1][:, :, :], mprod[:, :, :], f32(mmat[0][:, :, :]), ALU.subtract).then_inc(d_lo, 1)

                heads = "p j (h d) -> p (j h) d"
                dve.wait_ge(ln_stats, 2 * l + 2)

                def attend(i, live):
                    n2, n3, n4, n5 = (l * GROUPS + (i - d) for d in (2, 3, 4, 5))
                    if live(4):
                        dve.wait_ge(b_qhi, n4 + 1)
                        nc.vector.tensor_tensor(qT[1][:, :, :], chunks(PQT), f32(qT[0][:, :, :]), ALU.subtract).then_inc(b_qlo, 1)
                    if live(3):
                        dve.wait_ge(b_qe, n3 + 1)
                        nc.vector.tensor_reduce(qstat[:, 1, :], qd[:, :, :].rearrange(heads, d=DH), AX, ALU.add).then_inc(b_soft, 1)
                        dve.wait_ge(b_soft, 5 * n3 + 3)
                        nc.vector.reciprocal(qstat[:, 2, :], qstat[:, 1, :]).then_inc(b_soft, 1)
                        dve.wait_ge(b_qT, n3)
                        dve.wait_ge(b_soft, 5 * n3 + 4)
                        nc.vector.tensor_tensor(qn[:, :, :].rearrange(heads, d=DH), qd[:, :, :].rearrange(heads, d=DH),
                                                qstat[:, 2, :].unsqueeze(2).to_broadcast((P, PAIR * HEADS, DH)),
                                                ALU.mult).then_inc(b_soft, 1)
                    if live(2):
                        dve.wait_ge(b_Q, n2 + 1)
                        q3 = PQ[0:P, :].rearrange("p (h d) -> p h d", d=DH)
                        nc.vector.tensor_reduce(qstat[:, 0, :], q3, AX, ALU.max).then_inc(b_soft, 1)
                        if live(3):
                            dve.wait_ge(b_soft, 5 * n3 + 5)
                        dve.wait_ge(b_soft, 5 * n2 + 1)
                        nc.vector.tensor_tensor(qd[:, :, :].rearrange(heads, d=DH), q3,
                                                qstat[:, 0, :].unsqueeze(2).to_broadcast((P, PAIR * HEADS, DH)),
                                                ALU.subtract).then_inc(b_soft, 1)
                    if live(5):
                        added = counted(dve, n5 + 1)
                        dve.wait_ge(x_loaded, 16)
                        dve.wait_ge(b_x1, added)
                        moments(tile_rows(res, i - 5), (i - 5) * PAIR)
                    if live(1):
                        h_low(h_attn(l, i - 1))
                pipeline(dve, 5, attend)
                rstd_all(lnst, 2 * l + 2)
                dve.wait_ge(ln_stats, 2 * l + 3)

                def mlp(i, live):
                    n2, n3 = l * GROUPS + (i - 2), l * GROUPS + (i - 3)

                    def hid_lo(c):
                        dve.wait_ge(b_hhi, 4 * n2 + c + 1)
                        nc.vector.tensor_tensor(hidh[c % 2][1][:, :, :], hid[c % 2][:, :, :], f32(hidh[c % 2][0][:, :, :]),
                                                ALU.subtract).then_inc(b_hlo, 1)
                    if live(2):
                        hid_lo(0)
                    if live(3):
                        dve.wait_ge(b_Y, 4 * n3 + 4)
                        add_rows(i - 3, PY[0:P, :].rearrange("p (j d) -> p j d", j=PAIR), b_x2)
                        dve.wait_ge(b_x2, 2 * n3 + 1)
                        add_rows(i - 3, b2_b[:, :].unsqueeze(1).to_broadcast((P, PAIR, D)), b_x2)
                    if sorting and live(0):
                        kind_mask(2 * i, 0)
                    if live(2):
                        hid_lo(1)
                    if sorting and live(0):
                        kind_rank(2 * i, 0)
                        kind_mask(2 * i + 1, 1)
                    if live(3):
                        added = counted(dve, 2 * n3 + 2)
                        dve.wait_ge(x_loaded, 16)
                        dve.wait_ge(b_x2, added)
                        moments(tile_rows(res, i - 3), (i - 3) * PAIR)
                    if live(2):
                        hid_lo(2)
                    if live(1):
                        h_low(h_mlp(l, i - 1))
                    if live(2):
                        hid_lo(3)
                    if sorting and live(0):
                        kind_rank(2 * i + 1, 1)
                pipeline(dve, 3, mlp)
                if sorting:
                    dve.wait_ge(e_acc, TILES + 1)
                    nc.vector.tensor_scalar(pos_i[:, :], pos_f, -1.0, None, ALU.add).then_inc(pos_ready, 1)
                rstd_all(lnst, 2 * l + 3)

            layer(0, True)
            with dve.Fori(1, LAYERS) as l:
                layer(l, False)

            dve.wait_ge(b_x2, 2 * LAYERS * GROUPS)
            dve.wait_ge(ln_stats, LN_LAST)
            for i in range(4):
                nc.vector.memset(f32(ehl[i][:, :, EA:EA + 2]), 1.0).then_inc(s_ones, 1)
            dve.wait_ge(s_ones, 5)

            def seg_tiles(n, count):
                _, tiles = nc.values_load_multi_w_load_instructions(
                    ekind_i[0:1, bass.ds(n, count)], engines=[mybir.EngineType.DVE], min_val=0, max_val=TILES - 1)
                return tiles

            def seg_add(n, slot, tile):
                o = agg[:, bass.ds(tile, 1), :].rearrange("p a c -> p (a c)")
                dve.wait_ge(s_pe, n + 1)
                dve.wait_ge(s_add, n)
                nc.vector.tensor_tensor(o, o, SEG_BANK[slot][0:P, 0:2 * EA + 2], ALU.add).then_inc(s_add, 1)

            def seg_prep(n, slot):
                dve.wait_ge(s_kb, n + 1)
                if not (isinstance(n, int) and n < 4):
                    dve.wait_ge(s_pe, n - 3)
                nc.vector.tensor_tensor(oh[slot][:, :, :], iota_node[:, :].unsqueeze(1).to_broadcast((128, SEGR, P)),
                                        kb[:, slot, :].unsqueeze(2).to_broadcast((128, SEGR, P)), ALU.is_equal).then_inc(s_oh, 1)
            for n in range(4):
                seg_prep(n, n)
            for n, tile in enumerate(seg_tiles(0, 2)):
                seg_add(n, n, tile)
            with dve.Fori(1, ESEGS // 4) as q:
                tiles = seg_tiles(4 * q - 2, 4)
                for slot in range(4):
                    seg_prep(4 * q + slot, slot)
                    seg_add(4 * q + (slot - 2), (slot - 2) % 4, tiles[slot])
            seg_prep(ESEGS - 1, 0)
            for n, tile in enumerate(seg_tiles(ESEGS - 3, 3), ESEGS - 3):
                seg_add(n, n % 4, tile)
            dve.wait_ge(s_add, ESEGS)

            dve.wait_ge(gw_hi, 3)
            nc.vector.tensor_tensor(g1[1][:, 0:2, :], raw_g1[:, 0:2, :], f32(g1[0][:, 0:2, :]), ALU.subtract).then_inc(gw_lo, 1)
            nc.vector.tensor_tensor(g1[1][0:EA, 2, :], raw_g1[0:EA, 2, :], f32(g1[0][0:EA, 2, :]), ALU.subtract).then_inc(gw_lo, 1)
            nc.vector.tensor_tensor(g2[1][:, :, :], raw_g2[:, :, :], f32(g2[0][:, :, :]), ALU.subtract).then_inc(gw_lo, 1)
            dve.wait_ge(gcol_pe, 1)
            nc.vector.tensor_tensor(g1col[:, :], PS[:, 0:2 * GHC:2], cols[:, NROW - 1 - GHC:NROW - 1], ALU.add).then_inc(gcol_ready, 1)

            def graph(i, live):
                if live(4):
                    g = i - 4
                    dve.wait_ge(n_x, 2 * g + 2)
                    dve.wait_ge(n_Y, 2 * g + 2)
                    add_rows(g, PY[0:P, :].rearrange("p (j d) -> p j d", j=PAIR), n_y)
                if live(0):
                    for slot in range(2):
                        dve.wait_ge(N_IN[slot], 16 * ((i + 2 - slot) // 2))
                    add_rows(i, x_in[:, bass.ds(i % 2, 1), :, :].rearrange("p a j d -> p (a j) d"), n_x)
                    sums = pair(agg, i, 2 * EA + 2)
                    dve.wait_ge(n_an, 4 * i)
                    nc.vector.tensor_scalar(crec[:, 0, :, :], sums[:, :, EA:EA + 1], 1.0, None, ALU.max).then_inc(n_an, 1)
                    nc.vector.tensor_tensor(asum[:, :, :], sums[:, :, 0:EA], sums[:, :, EA + 2:2 * EA + 2], ALU.add).then_inc(n_an, 1)
                    dve.wait_ge(n_an, 4 * i + 1)
                    nc.vector.reciprocal(crec[:, 1, :, :], crec[:, 0, :, :]).then_inc(n_an, 1)
                    dve.wait_ge(n_an, 4 * i + 3)
                    dve.wait_ge(n_T, i)
                    nc.vector.tensor_tensor(an[:, :, :], asum[:, :, :], crec[:, 1, :, :].to_broadcast((P, PAIR, EA)), ALU.mult).then_inc(n_an, 1)
                    dve.wait_ge(n_x, 2 * i + 1)
                    add_rows(i, gb2_b[:, :].unsqueeze(1).to_broadcast((P, PAIR, D)), n_x)
                if live(4):
                    added = counted(dve, i - 3)
                    dve.wait_ge(x_loaded, 16)
                    dve.wait_ge(n_y, added)
                    moments(tile_rows(res, i - 4), (i - 4) * PAIR)
                if live(1):
                    dve.wait_ge(n_hi, 2 * i)
                    nc.vector.tensor_tensor(cT[1][:, 0:2, :], chunks(PT), f32(cT[0][:, 0:2, :]), ALU.subtract).then_inc(n_lo, 1)
                    nc.vector.tensor_tensor(cT[1][0:EA, 2, :], PS[0:EA, 0:GT], f32(cT[0][0:EA, 2, :]), ALU.subtract).then_inc(n_lo, 1)
                if live(2):
                    for c in range(2):
                        dve.wait_ge(n_hhi, 2 * (i - 2) + c + 1)
                        nc.vector.tensor_tensor(ghh[c][1][:, :, :], ghid[c][:, :, :], f32(ghh[c][0][:, :, :]), ALU.subtract).then_inc(n_hlo, 1)
            pipeline(dve, 4, graph)
            rstd_all(res[:, :, D:D + 2], LN_LAST)

            with dve.Fori(0, GROUPS) as g:
                dve.wait_ge(n_log, g + 1)
                dve.wait_ge(n_top, 6 * g)
                nc.vector.tensor_tensor(logit[:, :, :], PM[0:P, 0:PAIR * EXP].rearrange("p (j e) -> p j e", j=PAIR),
                                        rb_b[:, :].unsqueeze(1).to_broadcast((P, PAIR, EXP)), ALU.add).then_inc(n_top, 1)
                biased, found = counted(dve, 6 * g + 1), counted(dve, 6 * g + 3)
                dve.wait_ge(rw_raw, 32)
                dve.wait_ge(n_top, biased)
                for j in range(PAIR):
                    nc.vector.max(best[:, j, :], logit[:, j, :]).then_inc(n_top, 1)
                dve.wait_ge(rw_raw, 32)
                dve.wait_ge(n_top, found)
                for j in range(PAIR):
                    nc.vector.max_index(besti[:, j, :], best[:, j, :], logit[:, j, :]).then_inc(n_top, 1)
                dve.wait_ge(n_top, 6 * g + 5)
                nc.vector.tensor_copy(res[:, bass.ds(g * PAIR, PAIR), D + 3], besti[:, :, 0]).then_inc(n_top, 1)

            dve.wait_ge(n_top, 6 * GROUPS)
            nc.vector.tensor_copy(fexp[:, :], res[:, :, D + 3]).then_inc(e_conv, 1)
            dve.wait_ge(e_conv, 6)
            def by_token(a):
                return a.unsqueeze(2).to_broadcast((P, EXP, TILES))

            def by_expert(a):
                return a.unsqueeze(1).to_broadcast((P, EXP, TILES))

            def flat(t):
                return t[:, :, :].rearrange("p e t -> p (e t)")
            nc.vector.tensor_tensor(fmask[:, :, :], by_token(iota_seg[0:P, 0:EXP]), by_expert(fexp[:, :]), ALU.is_equal).then_inc(r_m, 1)
            dve.wait_ge(r_m, 1)
            nc.vector.tensor_reduce(cnt[:, 0:EXP], fmask[:, :, :], AX, ALU.add).then_inc(r_cnt, 1)
            nc.vector.tensor_tensor_scan(flat(frank), ones[0:P, 0:1].to_broadcast((P, EXP * TILES)), flat(fmask), 0.0,
                                         ALU.mult, ALU.add).then_inc(r_scan, 1)
            dve.wait_ge(r_cnt, TILES + 1)
            nc.vector.tensor_tensor_scan(fbase[:, 0, :], ones[0:P, 0:EXP], cnt[:, 0:EXP], 0.0, ALU.mult, ALU.add).then_inc(r_zero, 1)
            kind_tables(EXP, P, FSEGS, fkind, fkind_i, ffirst_i, 1)
            dve.wait_ge(r_zero, 1)
            nc.vector.tensor_tensor(fbase[:, 1, :], base[:, 0:EXP], fbase[:, 0, :], ALU.subtract).then_inc(r_zero, 1)
            dve.wait_ge(r_zero, 2)
            nc.vector.tensor_tensor(fbase[:, 0, :], fbase[:, 1, :], cnt[:, 0:EXP], ALU.add).then_inc(r_zero, 1)
            dve.wait_ge(r_zero, 3)
            dve.wait_ge(r_scan, 1)
            nc.vector.tensor_tensor(fprod[:, :, :], frank[:, :, :], by_token(fbase[:, 0, :]), ALU.add).then_inc(r_acc, 1)
            dve.wait_ge(r_acc, 1)
            nc.vector.tensor_tensor(frank[:, :, :], fprod[:, :, :], fmask[:, :, :], ALU.mult).then_inc(r_mul, 1)
            dve.wait_ge(r_mul, 1)
            nc.vector.tensor_reduce(fpos[:, :], frank[:, :, :].rearrange("p e t -> p t e"), AX, ALU.add).then_inc(r_mul, 1)
            dve.wait_ge(r_mul, 2)
            nc.vector.tensor_scalar(fpos_i[:, :], fpos[:, :], -1.0, None, ALU.add).then_inc(f_posi, 1)
            nc.vector.memset(hsT[EH:EH + 1, :], 1.0).then_inc(f_bias, 1)

            def expert(live, seg):
                if live(4):
                    n, slot, turn, oslot, oturn = seg(4)
                    y = yin[slot]
                    dve.wait_ge(f_idx, 2 * n)
                    dve.wait_ge(F_IN[slot], 16 * turn + 16)
                    nc.vector.tensor_scalar(omiss[:, :], y[:, D + 3:D + 4], fkind[0:P, bass.ds(n, 1)], float(4 * N),
                                            ALU.not_equal, ALU.mult).then_inc(f_idx, 1)
                    dve.wait_ge(f_idx, 2 * n + 1)
                    dve.wait_ge(F_OUT[oslot], 16 * oturn)
                    nc.vector.tensor_tensor(oidx[oslot][:, :], omiss[:, :], y[:, D + 2:D + 3], ALU.add).then_inc(f_idx, 1)
                    dve.wait_ge(f_o, n + 1)
                    nc.vector.scalar_tensor_tensor(out=orow[oslot][:, :], in0=PY[0:P, 0:D], scalar=0.0, in1=y[:, 0:D],
                                                   op0=ALU.max, op1=ALU.add).then_inc(f_row, 1)
                if live(1):
                    dve.wait_ge(f_T, seg(1)[0] + 1)
                    nc.vector.tensor_copy(zsT[:, :, :], chunks(PT, KC, P)).then_inc(f_zT, 1)
            segments(dve, 4, expert)

        @block.tensor
        def _(pe):
            def transposes(o, i, n, k=KC):
                for j in range(PAIR):
                    for c in range(k):
                        a = nc.tensor.transpose(o[0:128, c, j * n:(j + 1) * n], i[:, j, c * 128:(c + 1) * 128], ident[0:n, 0:n])
                return a

            pe.wait_ge(consts, NCONST)
            pe.wait_ge(rows_loaded, 7 * 16)
            nc.tensor.transpose(PS[:, 0:NROW], colrows[:, :], ident[0:NROW, 0:NROW]).then_inc(cols_T, 1)

            def count_kinds(nk, segs, turn):
                pe.wait_ge(r_cnt, TILES + turn)
                pe.wait_ge(cols_ready, 1)
                mm(PS[0:P, 0:nk], tri[0:P, 0:P], cnt[:, 0:nk], True, True)
                mm(PS[0:P, 64:64 + nk], ones[0:P, 0:P], cnt[:, 0:nk], True, True)
                mm(PS[0:nk, 128:130], cnt[:, 0:nk], ones[0:P, 0:2], True, True).then_inc(sort_pe, 1)
                pe.wait_ge(sort_dve, SORT_DVE * turn + 5)
                mm(PS[0:nk, 130:131], tri[0:nk, 0:nk], kcol[0:nk, 0:1], True, True).then_inc(sort_pe, 1)
                pe.wait_ge(sort_dve, SORT_DVE * turn + 10)
                pe.wait_ge(sort_dve, SORT_DVE * turn + 4)
                mm(PS[:, 0:segs], ones[0:nk, :], cmp[0:nk, 0:segs], True, True).then_inc(sort_pe, 1)
            count_kinds(TILES, ESEGS, 0)

            def xhat_T(n):
                pe.wait_ge(h_xh, n + 1)
                pe.wait_ge(h_aff, n)
                transposes(chunks(PT), xh[0], P).then_inc(h_T, 1)

            with pe.Fori(0, LAYERS) as l:
                pe.wait_ge(qk_lo, l + 1)

                def keys(i, live, par):
                    if live(1):
                        xhat_T(h_keys(l, i - 1))
                    if live(2):
                        n = l * GROUPS + (i - 2)
                        pe.wait_ge(h_lo, h_keys(l, i - 2) + 1)
                        pe.wait_ge(a_ks, n)
                        for j in range(PAIR):
                            for k in range(KC):
                                a = mm3(PQ[0:P, j * D:(j + 1) * D], at(hTk[par], slice(None), k, slice(j * P, (j + 1) * P)),
                                        at(wqk, slice(None), k, slice(D, 2 * D)), k == 0, k == KC - 1)
                        a.then_inc(a_K, 1)
                key_pipeline(pe, 2, keys)

                pe.wait_ge(ctx_dve, 9 * l + 1)
                for k in range(KC):
                    a = nc.tensor.transpose(PT[:, k * P:(k + 1) * P], km[:, k * 128:(k + 1) * 128], ident[0:P, 0:P])
                a.then_inc(ctx_pe, 1)
                pe.wait_ge(ctx_dve, 9 * l + 3)
                pe.wait_ge(sort_dve, 11)
                mm(PS[0:P, 0:D], ones[:, 0:P], dg[:, :, :].rearrange("p k n -> p (k n)"), True, True).then_inc(ctx_pe, 1)

                def weighted(g, slot):
                    n = l * GROUPS + g
                    pe.wait_ge(g_ek, n + 1)
                    pe.wait_ge(g_xh, n + 1)
                    for j in range(PAIR):
                        for k in range(KC):
                            a = mm(PQT[:, k * D:(k + 1) * D], xh[slot][:, j, k * 128:(k + 1) * 128], ek[:, slot, j, :],
                                   isinstance(g, int) and g == 0 and j == 0 and k == 0, False)
                    a.then_inc(g_pe, 1)
                weighted(0, 0)
                with pe.Fori(0, GROUPS // 2) as q:
                    weighted(2 * q + 1, 1)
                    weighted(2 * q + 2, 0)

                pe.wait_ge(g_esum, (l + 1) * GROUPS)
                for j in range(PAIR):
                    a = mm(PS[:, 0:D], ones[0:P, :], esum[:, j, :], j == 0, j == PAIR - 1)
                a.then_inc(ctx_pe, 1)
                pe.wait_ge(ctx_dve, 9 * l + 7)
                pe.wait_ge(w_vo, 32 * l + 32)
                for h in range(KC):
                    for k in range(KC):
                        a = mm(PM[:, h * 128:(h + 1) * 128], raw_vo[:, 0, k, h * 128:(h + 1) * 128],
                               gn[:, k, h * 128:(h + 1) * 128], k == 0, k == KC - 1)
                a.then_inc(ctx_pe, 1)
                pe.wait_ge(ctx_dve, 9 * l + 8)
                for h in range(KC):
                    a = mm(PS[:, h * D:(h + 1) * D], ct[:, h, :], raw_vo[:, 1, h, :], True, True)
                a.then_inc(ctx_pe, 1)
                pe.wait_ge(d_lo, l + 1)
                pe.wait_ge(w1_lo, l + 1)
                pe.wait_ge(w2_lo, l + 1)

                def attend(i, live):
                    n2, n3, n4 = (l * GROUPS + (i - d) for d in (2, 3, 4))
                    if live(2):
                        pe.wait_ge(h_lo, h_attn(l, i - 2) + 1)
                        if live(3):
                            pe.wait_ge(b_soft, 5 * n3 + 2)
                        for j in range(PAIR):
                            for k in range(KC):
                                a = mm3(PQ[0:P, j * D:(j + 1) * D], at(hT, slice(None), k, slice(j * P, (j + 1) * P)),
                                        at(wqk, slice(None), k, slice(0, D)), k == 0, k == KC - 1)
                        a.then_inc(b_Q, 1)
                    if live(1):
                        xhat_T(h_attn(l, i - 1))
                    if live(4):
                        pe.wait_ge(b_qlo, n4 + 1)
                        pe.wait_ge(b_x1, n4)
                        for j in range(PAIR):
                            for k in range(KC):
                                mm3(PM[0:P, j * D:(j + 1) * D], at(qT, slice(None), k, slice(j * P, (j + 1) * P)),
                                    at(mmat, slice(None), k, slice(None)), k == 0, False)
                            a = mm(PM[0:P, j * D:(j + 1) * D], ident[0:P, 0:P],
                                   res[:, bass.ds((i - 4) * PAIR + j, 1), 0:D].rearrange("p a d -> p (a d)"), False, True)
                        a.then_inc(b_M, 1)
                    if live(3):
                        pe.wait_ge(b_soft, 5 * n3 + 5)
                        pe.wait_ge(b_qlo, n3)
                        transposes(chunks(PQT), qn, P).then_inc(b_qT, 1)
                pipeline(pe, 4, attend)

                def mlp(i, live):
                    n2, n3 = l * GROUPS + (i - 2), l * GROUPS + (i - 3)

                    def up(c):
                        if c >= 2 or live(3):
                            pe.wait_ge(b_gelu, 4 * n2 + c - 1)
                        for m in range(2):
                            for k in range(KC):
                                a = mm3(chunks(PH[c % 2])[:, m, :], at(w1, slice(None), k, slice((2 * c + m) * 128, (2 * c + m + 1) * 128)),
                                        at(hT, slice(None), k, slice(None)), k == 0, k == KC - 1)
                        a.then_inc(b_H, 1)

                    def down(c, n):
                        pe.wait_ge(b_hlo, 4 * n + c + 1)
                        for m in range(2):
                            for j in range(PAIR):
                                a = mm3(PY[0:P, j * D:(j + 1) * D], at(hidh[c % 2], slice(None), m, slice(j * P, (j + 1) * P)),
                                        at(w2, slice(None), 2 * c + m, slice(None)), c == 0 and m == 0 and j == 0, False)
                        a.then_inc(b_Y, 1)
                    if live(2):
                        pe.wait_ge(h_lo, h_mlp(l, i - 2) + 1)
                        up(0)
                    if live(3):
                        down(3, n3)
                    if live(2):
                        up(1)
                    if live(1):
                        xhat_T(h_mlp(l, i - 1))
                    if live(2):
                        up(2)
                        if live(3):
                            pe.wait_ge(b_x2, 2 * n2 - 1)
                        down(0, n2)
                        up(3)
                        down(1, n2)
                        down(2, n2)
                pipeline(pe, 3, mlp)

            pe.wait_ge(s_ones, 5)

            def segment(n, slot):
                pe.wait_ge(s_oh, n + 1)
                pe.wait_ge(s_lo, n + 1)
                if not (isinstance(n, int) and n < 4):
                    pe.wait_ge(s_add, n - 3)
                for j in range(SEGR):
                    a = mm(SEG_BANK[slot][0:P, 0:2 * EA + 2], oh[slot][:, j, :], ehl[slot][:, j, :], j == 0, j == SEGR - 1)
                a.then_inc(s_pe, 1)
            for n in range(4):
                segment(n, n)
            with pe.Fori(1, ESEGS // 4) as q:
                for slot in range(4):
                    segment(4 * q + slot, slot)
            segment(ESEGS - 1, 0)
            pe.wait_ge(s_add, ESEGS)
            pe.wait_ge(gw_raw, 80)
            for c in range(GHC):
                a = mm(PS[:, 2 * c:2 * c + 1], raw_gu[:, c * 128:(c + 1) * 128], cols[:, NROW - 1:NROW], True, True)
            a.then_inc(gcol_pe, 1)
            pe.wait_ge(rw_raw, 32)
            for k in range(KC):
                a = nc.tensor.transpose(PT[:, k * EXP:(k + 1) * EXP], rw_in[:, k * 128:(k + 1) * 128], ident[0:EXP, 0:EXP])
            a.then_inc(rw_T, 1)

            pe.wait_ge(gcol_ready, 1)
            pe.wait_ge(gw_lo, 3)
            pe.wait_ge(rw_ready, 1)

            def graph(i, live):
                if live(2):
                    g = i - 2
                    pe.wait_ge(n_lo, 2 * g + 2)
                    for c in range(2):
                        if live(3):
                            pe.wait_ge(n_relu, 2 * g + c - 1)
                        for m in range(2):
                            hc = slice((2 * c + m) * 128, (2 * c + m + 1) * 128)
                            for k in range(3):
                                rows = slice(0, 128 if k < 2 else EA)
                                a = mm3(chunks(PH[c])[:, m, :], at(g1, rows, k, hc), at(cT, rows, k, slice(None)), k == 0, k == 2)
                        a.then_inc(n_H, 1)
                if live(1):
                    pe.wait_ge(n_xn, i)
                    pe.wait_ge(n_an, 4 * i)
                    pe.wait_ge(n_lo, 2 * i - 2)
                    transposes(chunks(PT), xn, P)
                    for j in range(PAIR):
                        a = nc.tensor.transpose(PS[0:EA, j * P:(j + 1) * P], an[:, j, :], ident[0:P, 0:P])
                    a.then_inc(n_T, 1)
                if live(3):
                    g = i - 3
                    pe.wait_ge(n_y, g)
                    for c in range(2):
                        pe.wait_ge(n_hlo, 2 * g + c + 1)
                        for m in range(2):
                            for j in range(PAIR):
                                a = mm3(PY[0:P, j * D:(j + 1) * D], at(ghh[c], slice(None), m, slice(j * P, (j + 1) * P)),
                                        at(g2, slice(None), 2 * c + m, slice(None)), c == 0 and m == 0 and j == 0, False)
                        a.then_inc(n_Y, 1)
            pipeline(pe, 3, graph)

            def route(i, live):
                if live(0):
                    pe.wait_ge(n_z, i + 1)
                    pe.wait_ge(n_zTs, i)
                    transposes(chunks(PQ), zt, P).then_inc(n_zT, 1)
                if live(1):
                    g = i - 1
                    pe.wait_ge(n_zTs, g + 1)
                    pe.wait_ge(n_top, 6 * g)
                    for j in range(PAIR):
                        for k in range(KC):
                            a = mm(PM[0:P, j * EXP:(j + 1) * EXP], zT[:, k, j * P:(j + 1) * P], rwT[:, k, :], k == 0, k == KC - 1)
                    a.then_inc(n_log, 1)
            pipeline(pe, 1, route)

            count_kinds(EXP, FSEGS, 1)
            pe.wait_ge(f_w, 16 * 5)
            pe.wait_ge(f_bias, 1)

            def expert(live, seg):
                if live(4):
                    n = seg(4)[0]
                    e = pe.value_load(fkind_i[0:1, bass.ds(n, 1)], min_val=0, max_val=EXP - 1)
                    pe.wait_ge(f_hTs, n + 1)
                    pe.wait_ge(f_row, n)
                    mm(PY[0:P, 0:D], hsT[:, :], fw2[:, bass.ds(e * D, D)], True, True).then_inc(f_o, 1)
                if live(3):
                    hidden = counted(pe, seg(3)[0] + 1)
                    pe.wait_ge(f_bias, 1)
                    pe.wait_ge(f_hs, hidden)
                    nc.tensor.transpose(PQT[0:EH, 0:P], hs[:, :], ident[0:P, 0:P]).then_inc(f_hT, 1)
                if live(2):
                    n = seg(2)[0]
                    e = pe.value_load(fkind_i[0:1, bass.ds(n, 1)], min_val=0, max_val=EXP - 1)
                    pe.wait_ge(f_hs, n)
                    pe.wait_ge(f_zT, n + 1)
                    for k in range(KC):
                        a = mm(PM[0:P, 0:EH], zsT[:, k, :], fw1[:, k, bass.ds(e * EH, EH)], k == 0, k == KC - 1)
                    a.then_inc(f_h, 1)
                if live(1):
                    n = seg(1)[0]
                    pe.wait_ge(f_z, n + 1)
                    pe.wait_ge(f_zT, n)
                    for k in range(KC):
                        a = nc.tensor.transpose(PT[:, k * P:(k + 1) * P], zs[:, k * 128:(k + 1) * 128], ident[0:P, 0:P])
                    a.then_inc(f_T, 1)
            pe.wait_ge(r_table, 2)
            nc.tensor.transpose(PH0[0:EH, 0:EXP], fb1_r[:, :], ident[0:EXP, 0:EXP]).then_inc(f_bT, 1)
            segments(pe, 4, expert)
    return nc


INPUTS = ["x", "src", "edge_attr_64", "L0_gnn_u", "L0_gnn_W1", "L0_gnn_b1", "L0_gnn_W2", "L0_gnn_b2", "L0_mix_Wq", "L0_mix_Wk",
          "L0_mix_Wv", "L0_mix_Wo", "L0_mix_bo", "L0_mix_ln1_g", "L0_mix_ln1_b", "L0_mix_W1", "L0_mix_b1", "L0_mix_W2",
          "L0_mix_b2", "L0_mix_ln2_g", "L0_mix_ln2_b", "L0_ffn_router_w", "L0_ffn_router_b", "L0_ffn_W1", "L0_ffn_b1",
          "L0_ffn_W2", "L0_ffn_b2"]


def kernel(**inputs):
    import numpy as np
    import concourse.bacc as bacc
    from concourse.bass_utils import run_bass_kernel_spmd

    nc = bacc.Bacc("TRN2", target_bir_lowering=False, num_devices=1)
    arrays, args = {}, []
    for name in INPUTS:
        a = np.ascontiguousarray(inputs[name])
        arrays[f"in_{name}"] = a
        args.append(nc.dram_tensor(f"in_{name}", a.shape, mybir.dt.from_np(a.dtype), kind="ExternalInput").ap())
    args.append(nc.dram_tensor("nodes_out", (N, D), F32, kind="ExternalOutput").ap())
    build(nc, *args)
    r = run_bass_kernel_spmd(nc, [arrays], core_ids=[0])
    return r.results[0]["nodes_out"]
```
